# Optimizing a Trainium2 kernel written in Bass

```python
import numpy as np
import jax
import jax.numpy as jnp

def _softmax(x, axis=-1):
    return jax.nn.softmax(x, axis=axis)

def _gelu(x):
    return jax.nn.gelu(x, approximate=True)

def _silu(x):
    return jax.nn.silu(x)

def _sigmoid(x):
    return jax.nn.sigmoid(x)

def _layernorm(x, axis=-1, eps=1e-05):
    m = jnp.mean(x, axis=axis, keepdims=True)
    v = jnp.var(x, axis=axis, keepdims=True)
    return (x - m) / jnp.sqrt(v + eps)

def _scatter_add(tgt, idx, src, axis=0):
    return tgt.at[idx].add(src)

def _segment_sum(src, seg, n):
    return jax.ops.segment_sum(src, seg, n)
kernel_name = 'mk_lm_tower_d1_tok_ids1024_r4_5a1593'

def setup_inputs(seed: int=0):
    np.random.seed(seed)
    _w = jnp.asarray

    def _rec_inputs():
        import jax
        import jax.numpy as jnp
        _rk = jax.random.key(seed)
        x = jax.random.randint(jax.random.fold_in(_rk, 1), (32, 128), 0, 50226, jnp.int32)
        return x
    x = _rec_inputs()

    def _L0_tok_setup():
        import jax, jax.numpy as jnp
        import numpy as np
        B, T, D, H, L, V = (8, 256, 256, 16, 4, 50257)
        HD = D // H
        DF = 4 * D
        EPS = 1e-05

        def _layernorm(x, w, b):
            m = jnp.mean(x, axis=-1, keepdims=True)
            v = jnp.mean((x - m) ** 2, axis=-1, keepdims=True)
            return (x - m) * jax.lax.rsqrt(v + EPS) * w + b
        key = jax.random.key(seed)
        ks = jax.random.split(key, 17)
        s = 0.02
        n = lambda k, shape: (jax.random.normal(k, shape) * s).astype(jnp.float32)
        return {'idx': jax.random.randint(ks[0], (B, T), 0, V), 'tok_emb': n(ks[1], (V, D)), 'pos_emb': n(ks[2], (T, D)), 'wq': n(ks[3], (L, D, D)), 'wk': n(ks[4], (L, D, D)), 'wv': n(ks[5], (L, D, D)), 'w_proj': n(ks[6], (L, D, D)), 'b_proj': jnp.zeros((L, D), jnp.float32), 'ln1_w': jnp.ones((L, D), jnp.float32), 'ln1_b': jnp.zeros((L, D), jnp.float32), 'ln2_w': jnp.ones((L, D), jnp.float32), 'ln2_b': jnp.zeros((L, D), jnp.float32), 'w1': n(ks[7], (L, D, DF)), 'b1': jnp.zeros((L, DF), jnp.float32), 'w2': n(ks[8], (L, DF, D)), 'b2': jnp.zeros((L, D), jnp.float32)}
    _L0_tok_all = _L0_tok_setup()
    _L0_tok_in = {k: v for k, v in _L0_tok_all.items() if k in ('tok_emb', 'pos_emb', 'wq', 'wk', 'wv', 'w_proj', 'b_proj', 'ln1_w', 'ln1_b', 'ln2_w', 'ln2_b', 'w1', 'b1', 'w2', 'b2')}
    del _L0_tok_all

    def _L0_attn_setup():
        import jax, jax.numpy as jnp
        import numpy as np
        D_MODEL = 256
        N_HEADS = 16

        def get_freqs(seq, n_dim):
            inv = 1.0 / 10000.0 ** (jnp.arange(0, n_dim, 2, dtype=jnp.float32) / n_dim)
            pos = jnp.arange(seq, dtype=jnp.float32)
            return pos[:, None] * inv[None, :]

        def rope(x, freq):
            xf = x.astype(jnp.float32)
            x1 = xf[..., 0::2]
            x2 = xf[..., 1::2]
            cos = jnp.cos(freq)[None, :, None, :]
            sin = jnp.sin(freq)[None, :, None, :]
            r1 = x1 * cos - x2 * sin
            r2 = x1 * sin + x2 * cos
            out = jnp.stack([r1, r2], axis=-1).reshape(x.shape)
            return out.astype(x.dtype)
        key = jax.random.key(seed)
        k1, k2, k3, k4, k5 = jax.random.split(key, 5)
        batch, seq = (2, 512)
        x = jax.random.normal(k1, (batch, seq, D_MODEL), dtype=jnp.float16)
        scale = jnp.float16(0.02)
        qw = jax.random.normal(k2, (D_MODEL, D_MODEL), dtype=jnp.float16) * scale
        kw = jax.random.normal(k3, (D_MODEL, D_MODEL), dtype=jnp.float16) * scale
        vw = jax.random.normal(k4, (D_MODEL, D_MODEL), dtype=jnp.float16) * scale
        ow = jax.random.normal(k5, (D_MODEL, D_MODEL), dtype=jnp.float16) * scale
        return {'x': x, 'qw': qw, 'kw': kw, 'vw': vw, 'ow': ow}
    _L0_attn_all = _L0_attn_setup()
    _L0_attn_in = {k: v for k, v in _L0_attn_all.items() if k in ('qw', 'kw', 'vw', 'ow')}
    del _L0_attn_all

    def _L0_ffn_setup():
        import jax, jax.numpy as jnp
        import numpy as np
        S, B, D, E, C, FF = (512, 4, 256, 8, 512, 1024)
        N = S * B
        key = jax.random.key(seed)
        ks = jax.random.split(key, 7)
        return {'hidden_states': jax.random.normal(ks[0], (S, B, D), dtype=jnp.float32), 'combine_weights': jax.random.uniform(ks[1], (N, E), dtype=jnp.float32), 'top_idx': jax.random.randint(ks[2], (C, E), 0, N, dtype=jnp.int64), 'W1': jax.random.normal(ks[3], (E, D, FF), dtype=jnp.float32) * (1.0 / np.sqrt(D)), 'b1': jnp.zeros((E, FF), dtype=jnp.float32), 'W2': jax.random.normal(ks[4], (E, FF, D), dtype=jnp.float32) * (1.0 / np.sqrt(FF)), 'b2': jnp.zeros((E, D), dtype=jnp.float32)}
    _L0_ffn_all = _L0_ffn_setup()
    _L0_ffn_in = {k: v for k, v in _L0_ffn_all.items() if k in ('combine_weights', 'top_idx', 'W1', 'b1', 'W2', 'b2')}
    del _L0_ffn_all
    return {'x': x, 'L0_tok_tok_emb': _L0_tok_in['tok_emb'], 'L0_tok_pos_emb': _L0_tok_in['pos_emb'], 'L0_tok_wq': _L0_tok_in['wq'], 'L0_tok_wk': _L0_tok_in['wk'], 'L0_tok_wv': _L0_tok_in['wv'], 'L0_tok_w_proj': _L0_tok_in['w_proj'], 'L0_tok_b_proj': _L0_tok_in['b_proj'], 'L0_tok_ln1_w': _L0_tok_in['ln1_w'], 'L0_tok_ln1_b': _L0_tok_in['ln1_b'], 'L0_tok_ln2_w': _L0_tok_in['ln2_w'], 'L0_tok_ln2_b': _L0_tok_in['ln2_b'], 'L0_tok_w1': _L0_tok_in['w1'], 'L0_tok_b1': _L0_tok_in['b1'], 'L0_tok_w2': _L0_tok_in['w2'], 'L0_tok_b2': _L0_tok_in['b2'], 'L0_attn_qw': _L0_attn_in['qw'], 'L0_attn_kw': _L0_attn_in['kw'], 'L0_attn_vw': _L0_attn_in['vw'], 'L0_attn_ow': _L0_attn_in['ow'], 'L0_ffn_combine_weights': _L0_ffn_in['combine_weights'], 'L0_ffn_top_idx': _L0_ffn_in['top_idx'], 'L0_ffn_W1': _L0_ffn_in['W1'], 'L0_ffn_b1': _L0_ffn_in['b1'], 'L0_ffn_W2': _L0_ffn_in['W2'], 'L0_ffn_b2': _L0_ffn_in['b2']}

def reference(x, L0_tok_tok_emb, L0_tok_pos_emb, L0_tok_wq, L0_tok_wk, L0_tok_wv, L0_tok_w_proj, L0_tok_b_proj, L0_tok_ln1_w, L0_tok_ln1_b, L0_tok_ln2_w, L0_tok_ln2_b, L0_tok_w1, L0_tok_b1, L0_tok_w2, L0_tok_b2, L0_attn_qw, L0_attn_kw, L0_attn_vw, L0_attn_ow, L0_ffn_combine_weights, L0_ffn_top_idx, L0_ffn_W1, L0_ffn_b1, L0_ffn_W2, L0_ffn_b2):
    import jax
    import jax.numpy as jnp

    def _L0_tok_ref(idx, tok_emb, pos_emb, wq, wk, wv, w_proj, b_proj, ln1_w, ln1_b, ln2_w, ln2_b, w1, b1, w2, b2):
        import jax, jax.numpy as jnp
        import numpy as np
        B, T, D, H, L, V = (8, 256, 256, 16, 4, 50257)
        HD = D // H
        DF = 4 * D
        EPS = 1e-05

        def _layernorm(x, w, b):
            m = jnp.mean(x, axis=-1, keepdims=True)
            v = jnp.mean((x - m) ** 2, axis=-1, keepdims=True)
            return (x - m) * jax.lax.rsqrt(v + EPS) * w + b
        b, t = idx.shape
        x = tok_emb[idx] + pos_emb[:t]
        causal_mask = jnp.tril(jnp.ones((t, t), dtype=bool))
        scale = jnp.asarray(D, x.dtype) ** (-0.5)
        for l in range(L):
            h = _layernorm(x, ln1_w[l], ln1_b[l])
            q = (h @ wq[l]).reshape(b, t, H, HD)
            k = (h @ wk[l]).reshape(b, t, H, HD)
            v = (h @ wv[l]).reshape(b, t, H, HD)
            scores = jnp.einsum('bthd,bshd->bhts', q, k) * scale
            scores = jnp.where(causal_mask, scores, -jnp.inf)
            attn = jax.nn.softmax(scores, axis=-1)
            ctx = jnp.einsum('bhts,bshd->bthd', attn, v).reshape(b, t, D)
            x = x + (ctx @ w_proj[l] + b_proj[l])
            h2 = _layernorm(x, ln2_w[l], ln2_b[l])
            ff = jax.nn.relu(h2 @ w1[l] + b1[l]) @ w2[l] + b2[l]
            x = x + ff
        return x

    def _L0_attn_ref(x, qw, kw, vw, ow):
        import jax, jax.numpy as jnp
        import numpy as np
        D_MODEL = 256
        N_HEADS = 16

        def get_freqs(seq, n_dim):
            inv = 1.0 / 10000.0 ** (jnp.arange(0, n_dim, 2, dtype=jnp.float32) / n_dim)
            pos = jnp.arange(seq, dtype=jnp.float32)
            return pos[:, None] * inv[None, :]

        def rope(x, freq):
            xf = x.astype(jnp.float32)
            x1 = xf[..., 0::2]
            x2 = xf[..., 1::2]
            cos = jnp.cos(freq)[None, :, None, :]
            sin = jnp.sin(freq)[None, :, None, :]
            r1 = x1 * cos - x2 * sin
            r2 = x1 * sin + x2 * cos
            out = jnp.stack([r1, r2], axis=-1).reshape(x.shape)
            return out.astype(x.dtype)
        batch, seq, dim = x.shape
        n_heads = N_HEADS
        n_dim = dim // n_heads
        Q = (x @ qw).reshape(batch, seq, n_heads, n_dim)
        K = (x @ kw).reshape(batch, seq, n_heads, n_dim)
        V = (x @ vw).reshape(batch, seq, n_heads, n_dim)
        freq = get_freqs(seq, n_dim)
        Q = rope(Q, freq)
        K = rope(K, freq)
        Q = jnp.transpose(Q, (0, 2, 1, 3))
        K = jnp.transpose(K, (0, 2, 1, 3))
        V = jnp.transpose(V, (0, 2, 1, 3))
        score = Q @ jnp.swapaxes(K, -1, -2) / jnp.sqrt(jnp.float16(dim))
        score = score.astype(jnp.float32)
        mask = jnp.tril(jnp.ones((1, 1, seq, seq), dtype=jnp.float32))
        score = score - 10000000000.0 * (1.0 - mask)
        weights = jax.nn.softmax(score, axis=-1)
        attn = weights @ V.astype(jnp.float32)
        merged = jnp.transpose(attn, (0, 2, 1, 3)).reshape(batch, seq, dim)
        out = merged @ ow.astype(jnp.float32)
        return out

    def _L0_ffn_ref(hidden_states, combine_weights, top_idx, W1, b1, W2, b2):
        import jax, jax.numpy as jnp
        import numpy as np
        S, B, D, E, C, FF = (512, 4, 256, 8, 512, 1024)
        N = S * B
        s, b, d = hidden_states.shape
        x = hidden_states.reshape(-1, d)
        tok = top_idx.T
        gathered = x[tok]
        h = jax.nn.gelu(jnp.einsum('ecd,edf->ecf', gathered, W1) + b1[:, None, :])
        out_e = jnp.einsum('ecf,efd->ecd', h, W2) + b2[:, None, :]
        e_ids = jnp.arange(tok.shape[0])[:, None]
        w = combine_weights[tok, e_ids]
        weighted = (out_e * w[..., None]).reshape(-1, d)
        out = jnp.zeros_like(x).at[tok.reshape(-1)].add(weighted)
        return out.reshape(s, b, d)
    h = _L0_tok_ref(x, L0_tok_tok_emb, L0_tok_pos_emb, L0_tok_wq, L0_tok_wk, L0_tok_wv, L0_tok_w_proj, L0_tok_b_proj, L0_tok_ln1_w, L0_tok_ln1_b, L0_tok_ln2_w, L0_tok_ln2_b, L0_tok_w1, L0_tok_b1, L0_tok_w2, L0_tok_b2)
    h = h + _L0_attn_ref(_layernorm(h, axis=-1), L0_attn_qw, L0_attn_kw, L0_attn_vw, L0_attn_ow)
    h = h + _L0_ffn_ref(_layernorm(h, axis=-1), L0_ffn_combine_weights, L0_ffn_top_idx, L0_ffn_W1, L0_ffn_b1, L0_ffn_W2, L0_ffn_b2)
    return h

_drawn_inputs = setup_inputs


def setup_inputs(seed=0):
    import zlib

    import numpy as np

    out = dict(_drawn_inputs(seed))
    spreads = {'L0_tok_b_proj': (0.0, 0.1),
     'L0_tok_ln1_w': (1.0, 0.2),
     'L0_tok_ln1_b': (0.0, 0.1),
     'L0_tok_ln2_w': (1.0, 0.2),
     'L0_tok_ln2_b': (0.0, 0.1),
     'L0_tok_b1': (0.0, 0.1),
     'L0_tok_b2': (0.0, 0.1),
     'L0_ffn_b1': (0.0, 0.1),
     'L0_ffn_b2': (0.0, 0.1)}
    factors = {'L0_tok_wq': 8.0, 'L0_tok_wk': 8.0, 'L0_attn_qw': 29.187, 'L0_attn_kw': 27.552}
    for name, (base, spread) in spreads.items():
        noise = np.random.default_rng([zlib.crc32(name.encode()), seed]).standard_normal(out[name].shape)
        drawn = base * np.exp(spread * noise) if base else spread * noise
        out[name] = jnp.asarray(drawn.astype(out[name].dtype))
    for name, factor in factors.items():
        out[name] = (out[name] * factor).astype(out[name].dtype)
    return out
```

```python
from contextlib import ExitStack

import concourse.bass as bass
from concourse import mybir

F32 = mybir.dt.float32
F16 = mybir.dt.float16
BF16 = mybir.dt.bfloat16
I32 = mybir.dt.int32
U32 = mybir.dt.uint32
ALU = mybir.AluOpType
ACT = mybir.ActivationFunctionType
AX_X = mybir.AxisListType.X

P = 128
NB, T = 32, 128
D = 256
KD = D // P
H, HD = 16, 16
PAIRS = H // 2
L = 4
FF = 4 * D
KF = FF // P
GB = 4
NG = NB // GB
N5 = GB * T
TOWER = L * NG
INST = TOWER + NG
UNITS = GB * H // 4
SLOTS = UNITS
HV = 2 * HD + 1
E, CAP = 8, 512
MB = 16
NCH = E * CAP // P
HOT = 256
EPS = 1e-5
WS = 16.0
LOADS = 12 * 16
SPLITS = 6
SCORE = 1.0 / (WS * WS * 16.0)

A_TOWER = [("t", 0, 3), ("t", 1, 4), ("q", 0, 5), ("q", 1, 6), ("k", 0, 7), ("k", 1, 8), ("v", 0, 9), ("v", 1, 10)]
A_ROTARY = [("t", 0, 2), ("t", 1, 3), ("q", 0, 4), ("qs", 0, 5), ("q", 1, 6), ("qs", 1, 7),
            ("k", 0, 8), ("ks", 0, 9), ("k", 1, 10), ("ks", 1, 11), ("v", 0, 12), ("v", 1, 13)]
C_TOWER = [("ct", 0, 1), ("ct", 1, 2), ("pj", 0, 3), ("pj", 1, 4), ("t", 0, 6), ("t", 1, 7)] + \
          [("f1", j, 8 + j // 2) for j in range(KF)] + [("f2", 0, 12), ("f2", 1, 14)]
C_ROTARY = C_TOWER[:4]
LN_C_SLOT = 4
ROW1_SLOTS = (0, 1, 1, 2)
ROW2_SLOTS = (7, 8, 9, 11)


def tower_model_kernel(nc, ids, tok_emb, pos_emb, wq, wk, wv, w_proj, b_proj, ln1_w, ln1_b, ln2_w, ln2_b,
                       w1, b1, w2, b2, qw, kw, vw, ow, combine, top_idx, e_w1, e_b1, e_w2, e_b2,
                       consts, out):
    ctx = ExitStack()

    def sb(name, shape, dt):
        return ctx.enter_context(nc.sbuf_tensor(name, shape, dt))

    def psum(name, shape):
        return ctx.enter_context(nc.psum_tensor(name, shape, F32))

    def sem(name):
        return ctx.enter_context(nc.semaphore(name))

    x = sb("x", [P, NB, D], F32)
    cst = sb("cst", [P, 7, P], F32)
    ident16 = sb("ident16", [P, P], BF16)
    mask_ts = sb("mask_ts", [P, P], BF16)
    mask_st = sb("mask_st", [P, P], BF16)
    ident, cos16, sin16 = cst[:, 0, :], cst[:, 3, :], cst[:, 4, :]
    half = sb("half", [P, GB], F32)
    idx = sb("idx", [P, NB], I32)
    pos = sb("pos", [P, D], F32)

    raw_a = sb("raw_a", [P, 3, KD, D], F32)
    raw_p = sb("raw_p", [P, KD, D], F32)
    raw_f = sb("raw_f", [P, KD * FF], F32)
    raw_1 = raw_f[:, :].rearrange("p (k n) -> p k n", k=KD)
    raw_2 = raw_f[:, :].rearrange("p (k n) -> p k n", k=KF)
    raw_v = sb("raw_v", [P, 4, KD], F32)
    raw_b1 = sb("raw_b1", [P, KF], F32)
    raw_rows = sb("raw_rows", [P, 2, D], F32)
    wa = sb("wa", [P, 3, 2, KD, D], F16)
    wp = sb("wp", [P, 2, KD, D], F16)
    w1s = sb("w1s", [P, 2, KD, FF], F16)
    w2s = sb("w2s", [P, 2, KF, D], F16)
    bqk = sb("bqk", [P, 4], F32)
    bv = sb("bv", [P, KD], F32)
    b1c = sb("b1c", [P, KF], F32)
    row1 = sb("row1", [P, D], F32)
    row2 = sb("row2", [P, D], F32)
    fw = raw_a[:, :, :, :].bitcast(F16).rearrange("p m k n -> p (m k n)").rearrange("p (m k n) -> p m k n", m=6, k=KD)
    lnw16 = sb("lnw16", [P, 2, KD], F32)

    a_st = sb("a_st", [P, GB, 6], F32)
    a_mv = sb("a_mv", [P, GB, 2], F32)
    a_ve = sb("a_ve", [P, GB], F32)
    a_rs = sb("a_rs", [P, GB], F32)
    c_st = sb("c_st", [P, GB, 6], F32)
    c_mv = sb("c_mv", [P, GB, 2], F32)
    c_ve = sb("c_ve", [P, GB], F32)
    c_rs = sb("c_rs", [P, GB], F32)
    a_x = sb("a_x", [P, GB, D], F32)
    c_x = sb("c_x", [P, GB, D], F32)
    a_xt = sb("a_xt", [P, KD, 2, N5], F16)
    c_xt = sb("c_xt", [P, KD, 2, N5], F16)
    qk_hl = sb("qk_hl", [P, 2, 2, 2, N5], F16)
    rot_a, rot_b, rot = (raw_f[:, i * N5:(i + 1) * N5] for i in range(3))
    qs = sb("qs", [P, 2, PAIRS, N5], F16)
    ks = sb("ks", [P, 2, PAIRS, 2, N5], F16)
    vs = sb("vs", [P, 2, GB, H, HV], F16)
    negm = sb("negm", [P, 4, 4], BF16)
    pr = sb("pr", [P, 4, 4, T], F32)
    pr_lo = sb("pr_lo", [P, 4, 4, T], F16)
    rec = sb("rec", [P, 8], F32)
    o_hl = sb("o_hl", [P, 8, 2, HD], F32)
    cx = sb("cx", [P, GB, D], F32)
    cxt = sb("cxt", [P, KD, 2, N5], F16)
    act32 = sb("act32", [P, 2, N5], F32)
    hid = sb("hid", [P, 2, KF, N5], F16)

    e_w1s = [w1s[:, :, :, :], qs[:, 0, :, :].rearrange("p a n -> p (a n)").rearrange("p (h k n) -> p h k n", h=2, k=KD)]
    e_w2s = [w2s[:, :, :, :], qs[:, 1, :, :].rearrange("p a n -> p (a n)").rearrange("p (h k n) -> p h k n", h=2, k=KF)]
    e_raw2 = pr[:, :, :, :].rearrange("p u h t -> p (u h t)").rearrange("p (k n) -> p k n", k=KF)
    wout = ks[:, :, :, :, :].rearrange("p a b e n -> p (a b e n)").rearrange("p (c h n) -> p c h n", c=NCH, h=2)
    hot = [qs[:, :, :, :].rearrange("p a b n -> p (a b n)").rearrange("p (c n) -> p c n", c=NCH),
           hid[:, :, :, :].rearrange("p a b n -> p (a b n)").rearrange("p (c n) -> p c n", c=NCH)]
    e_x = [a_x, c_x]
    e_row = [row1, row2]
    e_b1c = sb("e_b1c", [P, E, KF], F32)
    e_idx = sb("e_idx", [P, E, CAP // P], I32)
    e_idxf = sb("e_idxf", [P, NCH], F32)
    e_cw = sb("e_cw", [P, NCH, E], F32)
    num16 = a_xt[:, :, :, :].rearrange("p k a n -> p (k a n)").rearrange("p (i n) -> p i n", n=HOT)
    e_tmp = cx

    ps_s = [psum(f"ps_s{i}", [P, 4, T]) for i in range(2)]
    ps_st = [psum(f"ps_st{i}", [P, 4, T]) for i in range(2)]
    ps_o = psum("ps_o", [P, 512])
    ps_a = psum("ps_a", [P, 512])
    ps_c = [psum(f"ps_c{i}", [P, 512]) for i in range(2)]
    o_ps = ps_o[:, 0:8 * HV].rearrange("p (h v) -> p h v", v=HV)

    stack_d = nc.dram_tensor("stack_d", (2, 2, P, 2, 2, N5), F16).ap()
    tokens_d = nc.dram_tensor("tokens_d", (MB * T, D), F32).ap()

    s_cst = sem("s_cst")
    s_ids = sem("s_ids")
    s_emb = [sem(f"s_emb{g}") for g in range(NG)]
    s_init = sem("s_init")
    s_zero = sem("s_zero")
    s_pos = sem("s_pos")
    s_ld = sem("s_ld")
    s_ld2 = sem("s_ld2")
    s_fw = sem("s_fw")
    s_fws = sem("s_fws")
    s_wa = sem("s_wa")
    s_wp = sem("s_wp")
    s_w1 = sem("s_w1")
    s_w2 = sem("s_w2")
    s_b1 = sem("s_b1")
    s_num = sem("s_num")
    s_wh = sem("s_wh")
    s_ln16 = sem("s_ln16")
    s_bias_pe = sem("s_bias_pe")
    s_bias_a = sem("s_bias_a")
    s_bias_c = sem("s_bias_c")
    a_stat, a_mvs, a_ves, a_rstd, a_xn = sem("a_stat"), sem("a_mvs"), sem("a_ves"), sem("a_rstd"), sem("a_xn")
    a_ready, a_hi, a_free = sem("a_ready"), sem("a_hi"), sem("a_free")
    r_sum, r_hi, r_lo = sem("r_sum"), sem("r_hi"), sem("r_lo")
    st_out = sem("st_out")
    st_q, st_k = sem("st_q"), sem("st_k")
    s_ready, mx, st_ready, p_exp, p_lo, pv = sem("s_ready"), sem("mx"), sem("st_ready"), sem("p_exp"), sem("p_lo"), sem("pv")
    o_rec, o_free, o_ctx = sem("o_rec"), sem("o_free"), sem("o_ctx")
    c_stat, c_mvs, c_ves, c_rstd, c_xn = sem("c_stat"), sem("c_mvs"), sem("c_ves"), sem("c_rstd"), sem("c_xn")
    c_ready, c_hi, c_act, c_lo, c_free = sem("c_ready"), sem("c_hi"), sem("c_act"), sem("c_lo"), sem("c_free")
    s_row1, s_row2 = sem("s_row1"), sem("s_row2")
    m_out, m_idx, m_idxf = sem("m_out"), sem("m_idx"), sem("m_idxf")
    m_x = [sem(f"m_x{i}") for i in range(2)]
    m_cw, m_ld1, m_ld2, m_b1 = sem("m_cw"), sem("m_ld1"), sem("m_ld2"), sem("m_b1")
    m_row = [sem(f"m_row{i}") for i in range(2)]
    m_h1, m_l1, m_h2, m_l2 = sem("m_h1"), sem("m_l1"), sem("m_h2"), sem("m_l2")
    m_gh, m_o, m_wh, m_w = sem("m_gh"), sem("m_o"), sem("m_wh"), sem("m_w")
    m_hot, m_fin, s_out = sem("m_hot"), sem("m_fin"), sem("s_out")

    def ua(n, rotary):
        return n * 12 - 4 * TOWER if rotary else n * 8

    def ha(n, rotary):
        return n * 4 + 4 * TOWER if rotary else n * 8

    def uc(n, rotary):
        return n * 4 + 12 * TOWER if rotary else n * 16

    def hc(n, rotary):
        return n * 2 + 10 * TOWER if rotary else n * 12

    def wait(eng, s, value):
        if not isinstance(value, int) or value > 0:
            eng.wait_ge(s, value)

    def walk(eng, step, before_loop=None, at_layer=None, before_rotary=None):
        step(0, 0, 0, 0, 0, 0, "t", False, None, "a")
        step(1, 1, 1, 0, 0, 0, "t", True, None, "c")
        if before_loop:
            before_loop()
        with eng.Fori(0, L - 1) as l:
            if at_layer:
                at_layer(l)
            with eng.Fori(0, (NG - 2) // 2) as k:
                step(l * NG + k * 2 + 2, 0, k * 2 + 2, k * 2, l, l, "t", True, "t", None)
                step(l * NG + k * 2 + 3, 1, k * 2 + 3, k * 2 + 1, l, l, "t", True, "t", None)
            step(l * NG + NG, 0, 0, NG - 2, l + 1, l, "t", True, "t", "a")
            step(l * NG + NG + 1, 1, 1, NG - 1, l + 1, l, "t", True, "t", "c")
        if before_rotary:
            before_rotary()
        with eng.Fori(0, (NG - 2) // 2) as k:
            step(k * 2 + (TOWER - NG + 2), 0, k * 2 + 2, k * 2, L - 1, L - 1, "t", True, "t", None)
            step(k * 2 + (TOWER - NG + 3), 1, k * 2 + 3, k * 2 + 1, L - 1, L - 1, "t", True, "t", None)
        step(TOWER, 0, 0, NG - 2, L, L - 1, "r", True, "t", "r")
        step(TOWER + 1, 1, 1, NG - 1, L, L - 1, "r", True, "t", None)
        with eng.Fori(0, (NG - 2) // 2) as k:
            step(k * 2 + (TOWER + 2), 0, k * 2 + 2, k * 2, L, L, "r", True, "r", None)
            step(k * 2 + (TOWER + 3), 1, k * 2 + 3, k * 2 + 1, L, L, "r", True, "r", None)
        step(INST, 0, 0, NG - 2, L, L, None, True, "r", None)
        step(INST + 1, 1, 0, NG - 1, L, L, None, False, "r", None)

    def uses(table, slot):
        return [(k, kind, j) for k, (kind, j, at) in enumerate(table) if at == slot]

    def a_uses(A, slot):
        return uses({"t": A_TOWER, "r": A_ROTARY, None: []}[A], slot)

    def c_uses(C, slot):
        return uses({"t": C_TOWER, "r": C_ROTARY, None: []}[C], slot)

    def group(g):
        return x[:, bass.ds(g * GB, GB), :]

    def hi_view(ap):
        return ap.bitcast(BF16).rearrange("p (n two) -> p n two", two=2)[:, :, 1]

    PASSES = ((0, 0), (1, 0), (0, 1))

    E_USES = [("t", 0), ("t", 1)] + [("f1", j) for j in range(KF)] + [("f2", 0), ("f2", 1)]
    U_E, H_E = uc(INST, True), hc(INST, True)

    def ue(e):
        return e * len(E_USES) + U_E

    def he(e):
        return e * (2 + KF) + H_E

    def experts(eng, expert):
        with eng.Fori(0, E // 2) as k:
            expert(k * 2, 0, k)
            expert(k * 2 + 1, 1, k)

    block = ctx.enter_context(nc.Block())

    @block.sync
    def _(sp):
        def load_layer(l):
            one = bass.ds(l, 1)
            for i, v in enumerate((ln1_w, ln1_b, ln2_w, ln2_b)):
                sp.dma_start(raw_v[:, i, :], v[one, :].rearrange("l (k p) -> p (l k)", p=P),
                             allow_slow_non_contiguous=True).then_inc(s_ld, 16)
            for m, w in enumerate((wq, wk, wv)):
                sp.dma_start(raw_a[:, m, :, :], w[one, :, :].rearrange("l (k p) n -> p (l k) n", p=P)).then_inc(s_ld, 16)
            sp.dma_start(raw_p[:], w_proj[one, :, :].rearrange("l (k p) n -> p (l k) n", p=P)).then_inc(s_ld, 16)
            sp.dma_start(raw_1, w1[one, :, :].rearrange("l (k p) n -> p (l k) n", p=P)).then_inc(s_ld, 16)
            sp.dma_start(raw_b1[:], b1[one, :].rearrange("l (k p) -> p (l k)", p=P),
                         allow_slow_non_contiguous=True).then_inc(s_ld, 16)
            sp.dma_start(raw_rows[:, 0, :], b_proj[one, :].broadcast_to([P, D])).then_inc(s_ld, 16)
            sp.dma_start(raw_rows[:, 1, :], b2[one, :].broadcast_to([P, D])).then_inc(s_ld, 16)

        sp.dma_start(idx[:], ids.rearrange("b t -> t b"), allow_slow_non_contiguous=True).then_inc(s_ids, 16)
        sp.dma_start(cst[:], consts.rearrange("c p n -> p c n")).then_inc(s_cst, 16)
        sp.dma_start(pos[:], pos_emb[0:T, :]).then_inc(s_cst, 16)
        load_layer(0)

        def step(n, par, ga, gc, la, lc, A, B, C, prep):
            for which in range(2):
                if A is None:
                    continue
                if A == "t":
                    sp.wait_ge(a_free, ua(n, False) + 4 + 2 * which)
                    sp.nop(nofuse=True)
                else:
                    sp.wait_ge(r_lo, (n - TOWER) * 4 + 2 + 2 * which)
                    sp.nop(nofuse=True)
                wait(sp, st_q, n * 128)
                sp.nop(nofuse=True)
                wait(sp, st_k, n * 256)
                sp.nop(nofuse=True)
                sp.dma_start(stack_d[par, which], qk_hl[:, which]).then_inc(st_out, 16)
                sp.wait_ge(st_out, n * 32 + 16 * (which + 1))
                sp.nop(nofuse=True)
                wait(sp, st_ready, (n - 1) * UNITS)
                sp.nop(nofuse=True)
                for c in range(4):
                    for j in range(2):
                        if which == 0:
                            rows = stack_d[par, 0, :, j, c // 2, :].rearrange("(i p) n -> p i n", p=32)
                            sp.dma_start(qs[32 * c:32 * c + 32, par, 4 * j:4 * j + 4, :], rows).then_inc(st_q, 16)
                        else:
                            for e in range(2):
                                r = 32 * c + HD * e
                                rows = stack_d[par, 1, :, j, c % 2, :].rearrange("(i e p) n -> e p i n", e=2, p=HD)[e]
                                sp.dma_start(ks[r:r + HD, par, 4 * j:4 * j + 4, e, :], rows).then_inc(st_k, 16)
            if prep == "c":
                sp.wait_ge(s_w1, la + 1)
                sp.nop(nofuse=True)
                sp.wait_ge(s_bias_pe, la * 2 + 2)
                sp.nop(nofuse=True)
                sp.dma_start(raw_2, w2[bass.ds(la, 1), :, :].rearrange("l (k p) n -> p (l k) n", p=P)).then_inc(s_ld2, 16)

        def layer_done(l):
            sp.wait_ge(s_w2, l + 1)
            sp.nop(nofuse=True)
            sp.wait_ge(s_bias_c, l * 3 + 3)
            sp.nop(nofuse=True)

        def next_layer(l):
            layer_done(l)
            load_layer(l + 1)

        def rotary_weights():
            layer_done(L - 1)
            for m, w in enumerate((qw, kw, vw, ow)):
                sp.dma_start(fw[:, m, :, :], w.rearrange("(k p) n -> p k n", p=P)).then_inc(s_fw, 16)
            sp.dma_start(e_idx[:], top_idx.rearrange("(c p) e -> p e c", p=P), allow_slow_non_contiguous=True).then_inc(m_idx, 16)
            sp.dma_start(e_b1c[:], e_b1.rearrange("e (k p) -> p e k", p=P), allow_slow_non_contiguous=True).then_inc(m_b1, 16)

        walk(sp, step, None, next_layer, rotary_weights)

        for m in range(MB // GB):
            sp.wait_ge(c_xn, (TOWER + m + 1) * GB)
            sp.nop(nofuse=True)
            sp.dma_start(tokens_d[m * N5:(m + 1) * N5, :].rearrange("(b t) d -> t b d", t=T), e_x[m % 2][:]).then_inc(m_out, 16)
        for g in range(MB // GB, NG):
            sp.dma_start(out[g * GB:(g + 1) * GB].rearrange("b t d -> t b d"), group(g)).then_inc(s_out, 16)

        def expert(e, par, k):
            one = bass.ds(e, 1)
            sp.wait_ge(m_l1, e)
            sp.nop(nofuse=True)
            sp.dma_start(raw_1, e_w1[one, :, :].rearrange("l (k p) n -> p (l k) n", p=P)).then_inc(m_ld1, 16)
            sp.wait_ge(m_l2, e)
            sp.nop(nofuse=True)
            sp.dma_start(e_raw2, e_w2[one, :, :].rearrange("l (k p) n -> p (l k) n", p=P)).then_inc(m_ld2, 16)
            sp.wait_ge(m_w, k * 8)
            sp.nop(nofuse=True)
            sp.dma_start(e_row[par][:], e_b2[one, :].broadcast_to([P, D])).then_inc(m_row[par], 16)

        sp.wait_ge(c_free, U_E)
        sp.nop(nofuse=True)
        for e in range(2):
            if e:
                sp.wait_ge(m_l1, e)
                sp.nop(nofuse=True)
            sp.dma_start(raw_1, e_w1[e].rearrange("(k p) n -> p k n", p=P)).then_inc(m_ld1, 16)
            if e:
                sp.wait_ge(m_l2, e)
                sp.nop(nofuse=True)
            sp.dma_start(e_raw2, e_w2[e].rearrange("(k p) n -> p k n", p=P)).then_inc(m_ld2, 16)
            sp.dma_start(e_row[e][:], e_b2[e:e + 1, :].broadcast_to([P, D])).then_inc(m_row[e], 16)
        with sp.Fori(1, E // 2) as k:
            expert(k * 2, 0, k)
            expert(k * 2 + 1, 1, k)
        for g in range(MB // GB):
            sp.wait_ge(m_fin, (g + 1) * GB)
            sp.nop(nofuse=True)
            sp.dma_start(out[g * GB:(g + 1) * GB].rearrange("b t d -> t b d"), group(g)).then_inc(s_out, 16)
        sp.wait_ge(s_out, NG * 16)
        sp.nop(nofuse=True)

    @block.gpsimd
    def _(pool):
        pool.wait_ge(s_ids, 16)
        for b in range(NB):
            pool.indirect_dma_start(x[:, b, :], None, tok_emb, bass.IndirectOffsetOnAxis(ap=idx[:, b:b + 1].bitcast(U32), axis=0),
                                    ).then_inc(s_emb[b // GB], 16)
        nc.gpsimd.memset(half[:], -0.5).then_inc(s_zero, 1)
        nc.gpsimd.memset(vs[:], 1.0).then_inc(s_zero, 1)
        nc.gpsimd.memset(ks[:], 0.0).then_inc(s_zero, 1)
        pool.wait_ge(s_zero, 3)

        def inv_std(mv, ve, rs, s_mv, s_ve, s_rs, n):
            pool.wait_ge(s_mv, n * GB + GB)
            pool.nop(nofuse=True)
            nc.gpsimd.tensor_scalar(ve[:], mv[:, :, 1], EPS, 1.0, ALU.add, ALU.mult).then_inc(s_ve, 1)
            pool.wait_ge(s_ve, n + 1)
            nc.gpsimd.tensor_tensor(rs[:], ve[:], half[:], ALU.pow).then_inc(s_rs, 1)

        def add_contexts(b, q):
            pool.wait_ge(o_free, b * 8 + q + 1)
            dst = cx[:, q // 2, P * (q % 2):P * (q % 2) + P].rearrange("p (h d) -> p h d", d=HD)
            nc.gpsimd.tensor_tensor(dst, o_hl[:, :, 0, :], o_hl[:, :, 1, :], ALU.add).then_inc(o_ctx, 1)

        def add_row(row, g, i, done):
            seq = x[:, bass.ds(g * GB + i, 1), :].rearrange("p a d -> p (a d)")
            nc.gpsimd.tensor_tensor(seq, seq, row[:, :], ALU.add).then_inc(done, 1)

        def step(n, par, ga, gc, la, lc, A, B, C, prep):
            b, c = n - 1, n - 2
            for s in range(SLOTS):
                for k, kind, j in a_uses(A, s):
                    if kind in ("qs", "ks"):
                        r = (n - TOWER) * 4 + 2 * (kind == "ks") + j
                        pool.wait_ge(a_free, ua(n, True) + k + 1)
                        wait(pool, r_lo, r)
                        nc.gpsimd.tensor_tensor(rot, rot_a, rot_b, ALU.add).then_inc(r_sum, 1)
                if B:
                    pool.wait_ge(p_exp, b * UNITS + s + 1)
                    wait(pool, pv, b * UNITS + s - 3)
                    flat = pr[:, s % 4].rearrange("p h t -> p (h t)")
                    nc.gpsimd.tensor_tensor(pr_lo[:, s % 4].rearrange("p h t -> p (h t)"), flat, hi_view(flat),
                                            ALU.subtract).then_inc(p_lo, 1)
                if s == 0 and C:
                    add_contexts(c, 7)
                if s == 0 and A:
                    inv_std(a_mv, a_ve, a_rs, a_mvs, a_ves, a_rstd, n)
                if B and s >= 2 and s % 2 == 0:
                    if C and s == 2:
                        pool.wait_ge(c_ready, uc(c, C == "r") + 2)
                    add_contexts(b, s // 2 - 1)
                if C == "t" and s in ROW1_SLOTS:
                    if s == ROW1_SLOTS[0]:
                        pool.wait_ge(s_bias_c, lc * 3 + 3)
                        pool.nop(nofuse=True)
                    for i in range(GB):
                        if ROW1_SLOTS[i] == s:
                            add_row(row1, gc, i, s_row1)
                if C == "t" and s == LN_C_SLOT:
                    inv_std(c_mv, c_ve, c_rs, c_mvs, c_ves, c_rstd, c)
                if C == "t" and s in ROW2_SLOTS:
                    i = ROW2_SLOTS.index(s)
                    pool.wait_ge(c_xn, c * GB + i + 1)
                    pool.nop(nofuse=True)
                    add_row(row2, gc, i, s_row2)

        walk(pool, step)

        for m in range(MB // GB):
            inv_std(c_mv, c_ve, c_rs, c_mvs, c_ves, c_rstd, TOWER + m)
        pool.wait_ge(m_idx, 16)
        for ch in range(NCH):
            pool.indirect_dma_start(e_cw[:, ch, :], None, combine,
                                    bass.IndirectOffsetOnAxis(ap=e_idx[:, ch // 4, ch % 4:ch % 4 + 1].bitcast(U32), axis=0)
                                    ).then_inc(m_cw, 16)
        pool.wait_ge(m_out, 16 * (MB // GB))
        for e in range(E):
            if e >= 2:
                pool.wait_ge(c_ready, ue(e - 2) + 2)
            for ch in range(CAP // P):
                pool.indirect_dma_start(e_x[e % 2][:, ch, :], None, tokens_d,
                                        bass.IndirectOffsetOnAxis(ap=e_idx[:, e, ch:ch + 1].bitcast(U32), axis=0)
                                        ).then_inc(m_x[e % 2], 16)

    @block.scalar
    def _(act):
        def step(n, par, ga, gc, la, lc, A, B, C, prep):
            b, c = n - 1, n - 2
            for s in range(SLOTS):
                for k, kind, j in a_uses(A, s):
                    if kind in ("t", "v") or A == "t":
                        act.wait_ge(a_ready, ua(n, A == "r") + k + 1)
                    if kind == "t":
                        nc.scalar.activation(a_xt[:, j, 0, :], ps_a[:, :], ACT.Copy).then_inc(a_hi, 1)
                    elif kind == "v":
                        if j == 0:
                            wait(act, pv, (n - 1) * UNITS)
                        src = ps_a[:, :].rearrange("p (b h d) -> p b h d", b=2, h=H)
                        nc.scalar.activation(vs[:, par, 2 * j:2 * j + 2, :, 0:HD], src, ACT.Copy,
                                             scale=1.0 if A == "t" else WS).then_inc(a_hi, 1)
                    elif A == "t":
                        w = int(kind == "k")
                        wait(act, st_out, n * 32)
                        if kind == "q" and j == 0:
                            act.wait_ge(s_bias_a, la * 2 + 2)
                        nc.scalar.activation(qk_hl[:, w, j, 0, :], ps_a[:, :], ACT.Identity,
                                             bias=bqk[:, 2 * w + j:2 * w + j + 1]).then_inc(a_hi, 1)
                if B:
                    act.wait_ge(st_ready, b * UNITS + s + 1)
                    wait(act, pv, b * UNITS + s - 3)
                    nc.scalar.activation(pr[:, s % 4], ps_st[s % 2][:], ACT.Exp, scale=SCORE).then_inc(p_exp, 1)
                for k, kind, j in a_uses(A, s):
                    if kind in ("qs", "ks"):
                        w = int(kind == "ks")
                        r = (n - TOWER) * 4 + 2 * w + j
                        act.wait_ge(r_sum, r + 1)
                        act.wait_ge(st_out, n * 32)
                        nc.scalar.activation(qk_hl[:, w, j, 0, :], rot, ACT.Copy).then_inc(r_hi, 1)
                for k, kind, j in c_uses(C, s):
                    if kind in ("pj", "f2"):
                        continue
                    act.wait_ge(c_ready, uc(c, C == "r") + k + 1)
                    bank = ps_c[k % 2]
                    if kind == "ct":
                        nc.scalar.activation(cxt[:, j, 0, :], bank[:, :], ACT.Copy).then_inc(c_hi, 1)
                    elif kind == "t":
                        nc.scalar.activation(c_xt[:, j, 0, :], bank[:, :], ACT.Copy).then_inc(c_hi, 1)
                    else:
                        if j == 0:
                            act.wait_ge(s_bias_c, lc * 3 + 3)
                        nc.scalar.activation(hid[:, 0, j, :], bank[:, :], ACT.Relu, bias=b1c[:, j:j + 1]).then_inc(c_hi, 1)

        walk(act, step)

        act.wait_ge(m_b1, 16)

        def expert(e, par, k_):
            for k, (kind, j) in enumerate(E_USES):
                if kind == "f2":
                    continue
                act.wait_ge(c_ready, ue(e) + k + 1)
                if kind == "t":
                    nc.scalar.activation(c_xt[:, j, 0, :], ps_c[k % 2][:, :], ACT.Copy).then_inc(c_hi, 1)
                else:
                    act.wait_ge(c_free, ue(e) + k - 1)
                    nc.scalar.activation(act32[:, j % 2, :], ps_c[k % 2][:, :], ACT.Gelu_apprx_tanh,
                                         scale=1.0 / WS, bias=e_b1c[:, bass.ds(e, 1), j:j + 1].rearrange("p a b -> p (a b)")).then_inc(c_hi, 1)

        experts(act, expert)

    @block.tensor
    def _(pe):
        mm = nc.tensor.matmul

        def step(n, par, ga, gc, la, lc, A, B, C, prep):
            b, c, pb = n - 1, n - 2, 1 - par
            UA, UC = ua(n, A == "r"), uc(c, C == "r")

            def tok(bb):
                return slice(T * bb, T * bb + T)

            def scores(i, pi, u):
                bb, quad = u // 4, u % 4
                dst = ps_s[u % 2]
                if u == 0:
                    pe.wait_ge(st_q, i * 128 + 128)
                    pe.wait_ge(st_k, i * 256 + 256)
                wait(pe, mx, i * UNITS + u - 1)
                mm(dst[:], ident16[:], mask_ts[:, :].unsqueeze(1).broadcast_to([P, 4, T]), start=True, stop=False)
                for z in range(2):
                    p = 2 * quad + z
                    last = mm(dst[:, 2 * z:2 * z + 2, :], qs[:, pi, p, tok(bb)], ks[:, pi, p, :, tok(bb)], start=False, stop=z == 1)
                last.then_inc(s_ready, 1)

            def scores_t(u):
                bb, quad = u // 4, u % 4
                dst = ps_st[u % 2]
                pe.wait_ge(mx, b * UNITS + u + 1)
                wait(pe, p_exp, b * UNITS + u - 1)
                mm(dst[:], ident16[:], mask_st[:, :].unsqueeze(1).broadcast_to([P, 4, T]), start=True, stop=False)
                for h in range(4):
                    p = 2 * quad + h // 2
                    mm(dst[:, h, :], negm[:, u % 4, h:h + 1].broadcast_to([P, T]), ident16[:], start=False, stop=False)
                    last = mm(dst[:, h, :], ks[:, pb, p, h % 2, tok(bb)], qs[:, pb, p, tok(bb)], start=False, stop=h == 3)
                last.then_inc(st_ready, 1)

            def times_v(i, pi, u):
                bb, quad = u // 4, u % 4
                pe.wait_ge(p_lo, i * UNITS + u + 1)
                if u % 2 == 0:
                    wait(pe, o_free, i * 8 + u // 2)
                for h in range(4):
                    dst = o_ps[:, 4 * (u % 2) + h, :]
                    v = vs[:, pi, bb, 4 * quad + h, :]
                    mm(dst, hi_view(pr[:, u % 4, h, :]), v, start=True, stop=False)
                    last = mm(dst, pr_lo[:, u % 4, h, :], v, start=False, stop=True)
                last.then_inc(pv, 1)

            def a_use(k, kind, j):
                wait(pe, a_free, UA + k)
                if kind == "t":
                    if j == 0:
                        pe.wait_ge(a_xn, n * GB + GB)
                        if prep == "a":
                            pe.wait_ge(s_bias_a, la * 2 + 2)
                    for bb in range(GB):
                        last = nc.tensor.transpose(ps_a[:, tok(bb)], a_x[:, bb, P * j:P * j + P], ident)
                elif kind == "v":
                    for i in range(2):
                        t = tok(2 * j + i)
                        terms = [(kt, hw, hx) for kt in range(KD) for hw, hx in (PASSES if A == "t" else ((0, 0), (0, 1)))]
                        for z, (kt, hw, hx) in enumerate(terms):
                            w = wa[:, 2, hw, kt, :] if A == "t" else fw[:, 2, kt, :]
                            last = mm(ps_a[:, D * i:D * i + D], a_xt[:, kt, hx, t], w, start=z == 0, stop=z == len(terms) - 1)
                else:
                    if kind == "q" and j == 0:
                        pe.wait_ge(s_wa, la + 1) if A == "t" else pe.wait_ge(s_fws, 4)
                    terms = [(kt, hw, hx) for kt in range(KD) for hw, hx in (PASSES if A == "t" else ((0, 0), (0, 1)))]
                    m = {"q": 0, "k": 1, "qs": 4, "ks": 5}[kind]
                    for z, (kt, hw, hx) in enumerate(terms):
                        w = (wa[:, m, hw, kt, :] if A == "t" else fw[:, m, kt, :])[:, P * j:P * j + P]
                        last = mm(ps_a[:, :], w, a_xt[:, kt, hx, :], start=z == 0, stop=z == len(terms) - 1)
                last.then_inc(a_ready, 1)

            def c_use(k, kind, j):
                bank = ps_c[k % 2]
                if kind != "f2":
                    wait(pe, c_free, UC + max(k - 1, 0))
                if kind == "ct":
                    if j == 0:
                        pe.wait_ge(o_ctx, c * 8 + 8)
                    for bb in range(GB):
                        last = nc.tensor.transpose(bank[:, tok(bb)], cx[:, bb, P * j:P * j + P], ident)
                elif kind == "pj":
                    if j == 0:
                        pe.wait_ge(c_free, UC + 2)
                        if C == "t":
                            pe.wait_ge(s_wp, lc + 1)
                    for i in range(2):
                        t = tok(2 * j + i)
                        terms = [(kt, hw, hx) for kt in range(KD) for hw, hx in (PASSES if C == "t" else ((0, 0), (0, 1)))]
                        for z, (kt, hw, hx) in enumerate(terms):
                            w = wp[:, hw, kt, :] if C == "t" else fw[:, 3, kt, :]
                            last = mm(bank[:, D * i:D * i + D], cxt[:, kt, hx, t], w, start=z == 0, stop=z == len(terms) - 1)
                elif kind == "t":
                    if j == 0:
                        pe.wait_ge(c_xn, c * GB + GB)
                    for bb in range(GB):
                        last = nc.tensor.transpose(bank[:, tok(bb)], c_x[:, bb, P * j:P * j + P], ident)
                elif kind == "f1":
                    if j == 0:
                        pe.wait_ge(c_free, UC + 6)
                        pe.wait_ge(s_w1, lc + 1)
                    last = feed_1(bank, w1s, j)
                last.then_inc(c_ready, 1)

            if prep == "a":
                bias_products_a(n, la)
            for s in range(SLOTS):
                for use in a_uses(A, s):
                    a_use(*use)
                if B:
                    scores_t(s)
                if s < SLOTS - 1 and B:
                    scores(b, pb, s + 1)
                elif s == SLOTS - 1 and A:
                    scores(n, par, 0)
                if s == 0 and C:
                    times_v(c, par, UNITS - 1)
                elif s and B:
                    times_v(b, pb, s - 1)
                for use in c_uses(C, s):
                    if use[1] != "f2":
                        c_use(*use)
                if C == "t" and s >= 12:
                    j, i = (s - 12) // 2, s % 2
                    k = 14 + j
                    if s == 12:
                        pe.wait_ge(s_w2, lc + 1)
                    if i == 0:
                        pe.wait_ge(c_free, UC + k - 1)
                    last = feed_2(ps_c[k % 2], w2s, 2 * j + i, i, c if s == 12 else None)
                    if i == 1:
                        last.then_inc(c_ready, 1)
            if prep == "c":
                bias_products_c(n, la)

        def feed_1(bank, w, j):
            terms = [(kt, hw, hx) for kt in range(KD) for hw, hx in PASSES]
            for z, (kt, hw, hx) in enumerate(terms):
                last = mm(bank[:, :], w[:, hw, kt, P * j:P * j + P], c_xt[:, kt, hx, :], start=z == 0, stop=z == len(terms) - 1)
            return last

        def feed_2(bank, w, bb, i, c=None):
            terms = [(kt, hw, hx) for kt in range(KF) for hw, hx in PASSES]
            for z, (kt, hw, hx) in enumerate(terms):
                if c is not None and z % len(PASSES) == 0:
                    pe.wait_ge(c_lo, c * KF + kt + 1)
                last = mm(bank[:, D * i:D * i + D], hid[:, hx, kt, T * bb:T * bb + T], w[:, hw, kt, :],
                          start=z == 0, stop=z == len(terms) - 1)
            return last

        def bias_products_a(n, l):
            pe.wait_ge(s_ld, l * LOADS + LOADS)
            wait(pe, a_free, ua(n, False))
            for m in range(3):
                for j in range(KD):
                    for kt in range(KD):
                        col = 2 * m + j
                        last = mm(ps_a[:, col:col + 1], raw_a[:, m, kt, P * j:P * j + P], raw_v[:, 1, kt:kt + 1],
                                  start=kt == 0, stop=kt == KD - 1)
            last.then_inc(s_bias_pe, 1)

        def bias_products_c(n, l):
            pe.wait_ge(a_free, ua(n, False) + len(A_TOWER))
            for kt in range(KD):
                mm(ps_a[:, 0:D], bv[:, kt:kt + 1].broadcast_to([P, P]), raw_p[:, kt, :], start=kt == 0, stop=kt == KD - 1)
            for j in range(KF):
                for kt in range(KD):
                    last = mm(ps_a[:, D + j:D + j + 1], raw_1[:, kt, P * j:P * j + P], raw_v[:, 3, kt:kt + 1],
                              start=kt == 0, stop=kt == KD - 1)
            last.then_inc(s_bias_pe, 1)

        pe.wait_ge(s_cst, 32)
        pe.wait_ge(s_init, 3)
        pe.wait_ge(s_zero, 3)
        walk(pe, step)

        def expert(e, par, k_):
            for k, (kind, j) in enumerate(E_USES):
                bank = ps_c[k % 2]
                pe.wait_ge(c_free, ue(e) + k - 1)
                if kind == "t":
                    if j == 0:
                        pe.wait_ge(m_x[par], k_ * 64 + 64)
                    for ch in range(CAP // P):
                        last = nc.tensor.transpose(bank[:, T * ch:T * ch + T], e_x[par][:, ch, P * j:P * j + P], ident)
                elif kind == "f1":
                    if j == 0:
                        pe.wait_ge(c_free, ue(e) + 2)
                        pe.wait_ge(m_l1, e + 1)
                    last = feed_1(bank, e_w1s[par], j)
                else:
                    if j == 0:
                        pe.wait_ge(c_free, ue(e) + 2 + KF)
                        pe.wait_ge(m_l2, e + 1)
                    for i in range(2):
                        last = feed_2(bank, e_w2s[par], 2 * j + i, i)
                last.then_inc(c_ready, 1)

        experts(pe, expert)

        pe.wait_ge(m_w, E * 4)
        pe.wait_ge(c_free, ue(E))
        for b in range(MB):
            pe.wait_ge(m_hot, (b * T // HOT + 1) * NCH)
            if b >= 2:
                pe.wait_ge(m_fin, b - 1)
            n0 = b * T % HOT
            for ch in range(NCH):
                for hl in range(2):
                    last = mm(ps_c[b % 2][:, 0:D], hot[b * T // HOT % 2][:, ch, n0:n0 + T], wout[:, ch, hl, :],
                              start=ch + hl == 0, stop=ch + hl == NCH)
            last.then_inc(c_ready, 1)

    @block.vector
    def _(dve):
        V = nc.vector
        ln_a = (a_st, a_mv, a_rs, a_x, a_stat, a_mvs, a_rstd, a_xn)
        ln_c = (c_st, c_mv, c_rs, c_x, c_stat, c_mvs, c_rstd, c_xn)

        def stats(ln, n, g, seqs=range(GB)):
            st, mv, rs, xn, s_st, s_mv, s_rs, s_xn = ln
            dve.nop(nofuse=True)
            for i in seqs:
                V.bn_stats(st[:, i, :], x[:, bass.ds(g * GB + i, 1), :].rearrange("p a d -> p (a d)")).then_inc(s_st, 1)
            for i in seqs:
                dve.wait_ge(s_st, n * GB + i + 1)
                dve.nop(nofuse=True)
                V.bn_aggr(mv[:, i, :], st[:, i, :]).then_inc(s_mv, 1)

        def normalise(ln, n, g, dst=None):
            st, mv, rs, xn, s_st, s_mv, s_rs, s_xn = ln
            dve.wait_ge(s_rs, n + 1)
            for i in range(GB):
                V.tensor_scalar((dst or xn)[:, i, :], x[:, bass.ds(g * GB + i, 1), :].rearrange("p a d -> p (a d)"),
                                mv[:, i, 0:1], rs[:, i:i + 1], ALU.subtract, ALU.mult).then_inc(s_xn, 1)

        def split_lo(dst, raw, scale, hi):
            return V.scalar_tensor_tensor(out=dst, in0=raw, scalar=scale, in1=hi, op0=ALU.mult, op1=ALU.subtract)

        def prep_a(n, l):
            dve.wait_ge(s_ld, l * LOADS + LOADS)
            wait(dve, a_ready, ua(n, False))
            V.tensor_scalar(lnw16[:], raw_v[:, 0:4:2, :], WS, None, ALU.mult).then_inc(s_ln16, 1)
            dve.wait_ge(s_ln16, l + 1)
            for kt in range(KD):
                V.tensor_scalar(wa[:, :, 0, kt, :], raw_a[:, :, kt, :], lnw16[:, 0, kt:kt + 1], None, ALU.mult).then_inc(s_wh, 1)
            dve.wait_ge(s_bias_pe, l * 2 + 1)
            V.tensor_scalar(bqk[:], ps_a[:, 0:4], WS, None, ALU.mult).then_inc(s_bias_a, 1)
            V.tensor_copy(bv[:], ps_a[:, 4:6]).then_inc(s_bias_a, 1)
            for kt in range(KD):
                dve.wait_ge(s_wh, l * SPLITS + kt + 1)
                last = split_lo(wa[:, :, 1, kt, :], raw_a[:, :, kt, :], lnw16[:, 0, kt:kt + 1], wa[:, :, 0, kt, :])
            last.then_inc(s_wa, 1)

        def prep_p(c, l):
            wait(dve, c_ready, uc(c, False) + 4)
            V.tensor_scalar(wp[:, 0], raw_p[:], WS, None, ALU.mult).then_inc(s_wh, 1)
            dve.wait_ge(s_wh, l * SPLITS + 3)
            split_lo(wp[:, 1], raw_p[:], WS, wp[:, 0]).then_inc(s_wp, 1)

        def prep_1(c, l):
            wait(dve, c_ready, uc(c, False) + 14)
            for kt in range(KD):
                V.tensor_scalar(w1s[:, 0, kt, :], raw_1[:, kt, :], lnw16[:, 1, kt:kt + 1], None, ALU.mult).then_inc(s_wh, 1)
            for kt in range(KD):
                dve.wait_ge(s_wh, l * SPLITS + 4 + kt)
                last = split_lo(w1s[:, 1, kt, :], raw_1[:, kt, :], lnw16[:, 1, kt:kt + 1], w1s[:, 0, kt, :])
            last.then_inc(s_w1, 1)

        def prep_2(n, c, l):
            wait(dve, c_ready, uc(c, False) + 16)
            dve.wait_ge(s_bias_pe, l * 2 + 2)
            wait(dve, s_row1, c * GB + GB)
            wait(dve, s_row2, c * GB + GB)
            wait(dve, c_hi, hc(c, False) + 12)
            V.tensor_tensor(row1[:], ps_a[:, 0:D], raw_rows[:, 0, :], ALU.add).then_inc(s_bias_c, 1)
            V.tensor_copy(row2[:], raw_rows[:, 1, :]).then_inc(s_bias_c, 1)
            V.tensor_tensor(b1c[:], ps_a[:, D:D + KF], raw_b1[:], ALU.add).then_inc(s_b1, 1)
            dve.wait_ge(s_b1, l + 1)
            V.tensor_scalar(b1c[:], b1c[:], WS, None, ALU.mult).then_inc(s_bias_c, 1)
            dve.wait_ge(s_ld2, l * 16 + 16)
            V.tensor_scalar(w2s[:, 0], raw_2, WS, None, ALU.mult).then_inc(s_wh, 1)
            dve.wait_ge(s_wh, l * SPLITS + 6)
            split_lo(w2s[:, 1], raw_2, WS, w2s[:, 0]).then_inc(s_w2, 1)

        def prep_r():
            dve.wait_ge(s_fw, 64)
            for m in range(2):
                src = fw[:, m].rearrange("p k (n two) -> p k n two", two=2)
                dst = fw[:, 4 + m].rearrange("p k (n two) -> p k n two", two=2)
                V.tensor_scalar(dst[:, :, :, 0], src[:, :, :, 1], -1.0, None, ALU.mult).then_inc(s_fws, 1)
                V.tensor_copy(dst[:, :, :, 1], src[:, :, :, 0]).then_inc(s_fws, 1)

        def step(n, par, ga, gc, la, lc, A, B, C, prep):
            b, c = n - 1, n - 2
            UA, UC = ua(n, A == "r"), uc(c, C == "r")

            def maxima(i, u):
                dve.wait_ge(s_ready, i * UNITS + u + 1)
                V.tensor_reduce(negm[:, u % 4, :], ps_s[u % 2][:], AX_X, ALU.max, negate=True).then_inc(mx, 1)

            def contexts(i, q):
                dve.wait_ge(pv, i * UNITS + 2 * q + 2)
                V.reciprocal(rec[:], o_ps[:, :, 2 * HD]).then_inc(o_rec, 1)
                dve.wait_ge(o_rec, i * 8 + q + 1)
                wait(dve, o_ctx, i * 8 + q)
                V.tensor_tensor(o_hl[:].rearrange("p h a d -> p h (a d)"), o_ps[:, :, 0:2 * HD],
                                rec[:, :].unsqueeze(2).broadcast_to([P, 8, 2 * HD]), ALU.mult).then_inc(o_free, 1)

            def rotary_lo(kind, j):
                w = int(kind == "ks")
                r = (n - TOWER) * 4 + 2 * w + j
                dve.wait_ge(r_hi, r + 1)
                V.tensor_tensor(qk_hl[:, w, j, 1, :], rot, qk_hl[:, w, j, 0, :], ALU.subtract).then_inc(r_lo, 1)

            for s in range(SLOTS):
                for k, kind, j in a_uses(A, s - 1):
                    if kind in ("qs", "ks"):
                        rotary_lo(kind, j)
                for k, kind, j in a_uses(A, s):
                    if kind in ("t", "v") or A == "t":
                        dve.wait_ge(a_hi, ha(n, A == "r") + (k + 1 if A == "t" or kind == "t" else k - 7))
                    if kind == "t":
                        V.tensor_tensor(a_xt[:, j, 1, :], ps_a[:, :], a_xt[:, j, 0, :], ALU.subtract).then_inc(a_free, 1)
                    elif kind == "v":
                        src = ps_a[:, :].rearrange("p (h d) -> p h d", d=HD)
                        v = vs[:, par, 2 * j:2 * j + 2, :, :].rearrange("p b h v -> p (b h) v")
                        V.scalar_tensor_tensor(out=v[:, :, HD:2 * HD], in0=src, scalar=1.0 if A == "t" else WS,
                                               in1=v[:, :, 0:HD], op0=ALU.mult, op1=ALU.subtract).then_inc(a_free, 1)
                    elif A == "t":
                        w = int(kind == "k")
                        V.scalar_tensor_tensor(out=qk_hl[:, w, j, 1, :], in0=ps_a[:, :], scalar=bqk[:, 2 * w + j:2 * w + j + 1],
                                               in1=qk_hl[:, w, j, 0, :], op0=ALU.add, op1=ALU.subtract).then_inc(a_free, 1)
                    else:
                        r = (n - TOWER) * 4 + 2 * (kind[0] == "k") + j
                        dve.wait_ge(a_ready, UA + k + 1)
                        wait(dve, r_sum, r)
                        table = sin16 if kind[1:] else cos16
                        V.tensor_tensor((rot_b if kind[1:] else rot_a).rearrange("p (b t) -> p b t", t=T),
                                        ps_a[:, :].rearrange("p (b t) -> p b t", t=T),
                                        table.unsqueeze(1).broadcast_to([P, GB, T]), ALU.mult).then_inc(a_free, 1)
                if s < SLOTS - 1 and B:
                    maxima(b, s + 1)
                elif s == SLOTS - 1 and A:
                    maxima(n, 0)
                if s == 0 and C:
                    contexts(c, 7)
                if s == 0 and A:
                    if isinstance(n, int) and n < 2:
                        position(n)
                    stats(ln_a, n, ga)
                if s >= 2 and s % 2 == 0 and B:
                    contexts(b, s // 2 - 1)
                if s == 1 and A:
                    wait(dve, a_ready, UA)
                    normalise(ln_a, n, ga)
                if s == 1 and prep == "a":
                    prep_a(n, la)
                if s == 1 and prep == "r":
                    prep_r()
                for k, kind, j in c_uses(C, s):
                    if kind == "f2":
                        continue
                    bank = ps_c[k % 2]
                    if kind == "pj":
                        dve.wait_ge(c_ready, UC + k + 1)
                        if C == "t":
                            dve.wait_ge(s_row1, c * GB + 2 * j + 2)
                        residual(bank, gc, j, WS * WS if C == "t" else WS)
                        continue
                    order = k + 1 if k < 2 else k - 1
                    dve.wait_ge(c_hi, hc(c, C == "r") + order)
                    if kind == "ct":
                        V.tensor_tensor(cxt[:, j, 1, :], bank[:, :], cxt[:, j, 0, :], ALU.subtract).then_inc(c_free, 1)
                    elif kind == "t":
                        V.tensor_tensor(c_xt[:, j, 1, :], bank[:, :], c_xt[:, j, 0, :], ALU.subtract).then_inc(c_free, 1)
                    else:
                        wait(dve, c_lo, c * KF + max(j - 1, 0))
                        V.tensor_scalar(act32[:, j % 2, :], bank[:, :], b1c[:, j:j + 1], 0.0, ALU.add, ALU.max).then_inc(c_free, 1)
                for k, kind, j in c_uses(C, s):
                    if kind == "f1":
                        dve.wait_ge(c_free, UC + k + 1)
                        V.tensor_tensor(hid[:, 1, j, :], act32[:, j % 2, :], hid[:, 0, j, :], ALU.subtract).then_inc(c_lo, 1)
                if C == "t" and s in (LN_C_SLOT - 1, LN_C_SLOT):
                    j = s - (LN_C_SLOT - 1)
                    dve.wait_ge(c_free, UC + 3 + j)
                    stats(ln_c, c, gc, range(2 * j, 2 * j + 2))
                if C == "t" and s == LN_C_SLOT + 1:
                    normalise(ln_c, c, gc)
                if C == "t" and s in (13, 15):
                    j = (s - 13) // 2
                    dve.wait_ge(c_ready, UC + 14 + j + 1)
                    dve.wait_ge(s_row2, c * GB + 2 * j + 2)
                    residual(ps_c[j], gc, j, WS * WS)
                if prep == "c" and s == 8:
                    prep_p(c, la)
                if prep == "c" and s == 13:
                    prep_1(c, la)
            if prep == "c":
                prep_2(n, c, la)

        def residual(bank, g, j, scale):
            dst = x[:, bass.ds(g * GB + 2 * j, 2), :]
            V.scalar_tensor_tensor(out=dst, in0=bank[:, :].rearrange("p (b d) -> p b d", b=2), scalar=1.0 / scale, in1=dst,
                                   op0=ALU.mult, op1=ALU.add).then_inc(c_free, 1)

        def position(g):
            dve.wait_ge(s_emb[g], GB * 16)
            V.tensor_tensor(group(g), group(g), pos[:, :].unsqueeze(1).broadcast_to([P, GB, D]), ALU.add).then_inc(s_pos, 1)
            dve.wait_ge(s_pos, g + 1)

        dve.wait_ge(s_cst, 32)
        V.tensor_copy(ident16[:], cst[:, 0, :]).then_inc(s_init, 1)
        V.tensor_copy(mask_ts[:], cst[:, 1, :]).then_inc(s_init, 1)
        V.tensor_copy(mask_st[:], cst[:, 2, :]).then_inc(s_init, 1)

        def positions():
            for g in range(2, NG):
                position(g)

        walk(dve, step, positions)

        dve.wait_ge(c_free, U_E)
        for m in range(MB // GB):
            stats(ln_c, TOWER + m, m)
            if m >= 2:
                dve.wait_ge(m_out, 16 * m)
            normalise(ln_c, TOWER + m, m, e_x[m % 2])
        dve.wait_ge(m_idx, 16)
        V.tensor_copy(e_idxf[:], e_idx[:].rearrange("p e c -> p (e c)")).then_inc(m_idxf, 1)
        for i in range(MB * T // HOT):
            V.tensor_scalar(num16[:, i, :], cst[:, 5:7, :].rearrange("p a n -> p (a n)"), float(i * HOT), None, ALU.add).then_inc(s_num, 1)
        dve.wait_ge(m_cw, NCH * 16)

        def expert(e, par, k_):
            dve.wait_ge(m_ld1, e * 16 + 16)
            V.tensor_scalar(e_w1s[par][:, 0], raw_1, WS, None, ALU.mult).then_inc(m_h1, 1)
            dve.wait_ge(m_h1, e + 1)
            split_lo(e_w1s[par][:, 1], raw_1, WS, e_w1s[par][:, 0]).then_inc(m_l1, 1)
            dve.wait_ge(m_ld2, e * 16 + 16)
            V.tensor_scalar(e_w2s[par][:, 0], e_raw2, WS, None, ALU.mult).then_inc(m_h2, 1)
            dve.wait_ge(m_h2, e + 1)
            split_lo(e_w2s[par][:, 1], e_raw2, WS, e_w2s[par][:, 0]).then_inc(m_l2, 1)
            for k, (kind, j) in enumerate(E_USES):
                bank = ps_c[k % 2]
                if kind == "t":
                    dve.wait_ge(c_hi, he(e) + k + 1)
                    V.tensor_tensor(c_xt[:, j, 1, :], bank[:, :], c_xt[:, j, 0, :], ALU.subtract).then_inc(c_free, 1)
                elif kind == "f1":
                    dve.wait_ge(c_hi, he(e) + k + 1)
                    V.tensor_copy(hid[:, 0, j, :], act32[:, j % 2, :]).then_inc(m_gh, 1)
                    dve.wait_ge(m_gh, e * KF + j + 1)
                    V.tensor_tensor(hid[:, 1, j, :], act32[:, j % 2, :], hid[:, 0, j, :], ALU.subtract).then_inc(c_free, 1)
                else:
                    dve.wait_ge(c_ready, ue(e) + k + 1)
                    if j == 0:
                        dve.wait_ge(m_row[par], k_ * 16 + 16)
                    for i in range(2):
                        done = V.scalar_tensor_tensor(out=e_tmp[:, 2 * j + i, :], in0=bank[:, D * i:D * i + D], scalar=1.0 / WS,
                                                      in1=e_row[par][:], op0=ALU.mult, op1=ALU.add)
                        done.then_inc(m_o if i == 0 else c_free, 1)
                    for i in range(2):
                        if i == 0:
                            dve.wait_ge(m_o, e * 2 + j + 1)
                        else:
                            dve.wait_ge(c_free, ue(e) + k + 1)
                        ch = e * 4 + (2 * j + i)
                        w = e_cw[:, bass.ds(ch, 1), bass.ds(e, 1)].rearrange("p a b -> p (a b)")
                        dst = wout[:, bass.ds(ch, 1), :, :].rearrange("p c h n -> p (c h) n")
                        V.tensor_scalar(dst[:, 0, :], e_tmp[:, 2 * j + i, :], w, None, ALU.mult).then_inc(m_wh, 1)
                        dve.wait_ge(m_wh, e * 4 + 2 * j + i + 1)
                        split_lo(dst[:, 1, :], e_tmp[:, 2 * j + i, :], w, dst[:, 0, :]).then_inc(m_w, 1)

        experts(dve, expert)

        dve.wait_ge(m_idxf, 1)
        dve.wait_ge(s_num, MB * T // HOT)
        dve.wait_ge(c_ready, ue(E))
        dve.wait_ge(m_w, E * 4)

        def one_hot(i):
            if i >= 2:
                dve.wait_ge(c_ready, ue(E) + (i - 1) * (HOT // T))
            for ch in range(NCH):
                V.tensor_scalar(hot[i % 2][:, ch, :], num16[:, i, :], e_idxf[:, ch:ch + 1], None, ALU.is_equal).then_inc(m_hot, 1)

        one_hot(0)
        for i in range(MB * T // HOT):
            if i + 1 < MB * T // HOT:
                one_hot(i + 1)
            for b in range(i * (HOT // T), (i + 1) * (HOT // T)):
                dve.wait_ge(c_ready, ue(E) + b + 1)
                V.tensor_tensor(x[:, b, :], ps_c[b % 2][:, 0:D], x[:, b, :], ALU.add).then_inc(m_fin, 1)

    ctx.close()


_INS = ['x', 'L0_tok_tok_emb', 'L0_tok_pos_emb', 'L0_tok_wq', 'L0_tok_wk', 'L0_tok_wv', 'L0_tok_w_proj', 'L0_tok_b_proj',
        'L0_tok_ln1_w', 'L0_tok_ln1_b', 'L0_tok_ln2_w', 'L0_tok_ln2_b', 'L0_tok_w1', 'L0_tok_b1', 'L0_tok_w2', 'L0_tok_b2',
        'L0_attn_qw', 'L0_attn_kw', 'L0_attn_vw', 'L0_attn_ow', 'L0_ffn_combine_weights', 'L0_ffn_top_idx',
        'L0_ffn_W1', 'L0_ffn_b1', 'L0_ffn_W2', 'L0_ffn_b2']


def _constants():
    import numpy as np

    c = np.zeros((7, P, P), np.float32)
    i = np.arange(P)
    c[0] = np.eye(P)
    c[1] = np.where(i[None, :] > i[:, None], np.float32(-2.0 ** 80), 0)
    c[2] = np.where(i[:, None] > i[None, :], np.float32(-2.0 ** 80), 0)
    inv = (np.float32(1.0) / np.float32(10000.0) ** (np.arange(0, HD, 2, dtype=np.float32) / np.float32(HD))).astype(np.float32)
    freq = (i.astype(np.float32)[:, None] * inv[None, :]).astype(np.float32)
    by_row = freq[:, (i % HD) // 2].T
    c[3] = np.cos(by_row) * np.float32(WS)
    c[4] = np.sin(by_row) * np.float32(WS)
    c[5], c[6] = i[None, :], i[None, :] + P
    return c


def kernel(**inputs):
    import numpy as _np
    import concourse.bacc as _bacc
    from concourse import mybir as _mybir
    from concourse.bass_utils import run_bass_kernel_spmd as _run

    nc = _bacc.Bacc("TRN2", target_bir_lowering=False, num_devices=1)
    arrays, args = {}, []
    for name in _INS + ["consts"]:
        a = _constants() if name == "consts" else _np.ascontiguousarray(inputs[name])
        arrays[f"in_{name}_dram"] = a
        args.append(nc.dram_tensor(f"in_{name}_dram", a.shape, _mybir.dt.from_np(a.dtype), kind="ExternalInput").ap())
    args.append(nc.dram_tensor("out_0_dram", (NB, T, D), _mybir.dt.from_np(_np.dtype("float32")), kind="ExternalOutput").ap())
    tower_model_kernel(nc, *args)
    r = _run(nc, [arrays], core_ids=[0])
    return r.results[0]["out_0_dram"]
```

```python
from contextlib import ExitStack

import concourse.bass as bass
from concourse import mybir

F32 = mybir.dt.float32
F16 = mybir.dt.float16
BF16 = mybir.dt.bfloat16
I32 = mybir.dt.int32
U32 = mybir.dt.uint32
ALU = mybir.AluOpType
ACT = mybir.ActivationFunctionType
AX_X = mybir.AxisListType.X

P = 128
NB, T = 32, 128
D = 256
KD = D // P
H, HD = 16, 16
PAIRS = H // 2
L = 4
FF = 4 * D
KF = FF // P
GB = 4
NG = NB // GB
N5 = GB * T
TOWER = L * NG
INST = TOWER + NG
UNITS = GB * H // 4
SLOTS = UNITS
HV = 2 * HD + 1
E, CAP = 8, 512
MB = 16
NCH = E * CAP // P
HOT = 256
EPS = 1e-5
WS = 16.0
LOADS_A, LOADS_C = 7 * 16, 5 * 16
SPLITS = 5
SCORE = 1.0 / (WS * WS * 16.0)

A_TOWER = [("t", 0, 3), ("t", 1, 4), ("q", 0, 5), ("q", 1, 6), ("k", 0, 7), ("k", 1, 8), ("v", 0, 9), ("v", 1, 10)]
A_ROTARY = [("t", 0, 2), ("t", 1, 3), ("q", 0, 4), ("qs", 0, 4), ("q", 1, 5), ("qs", 1, 6),
            ("k", 0, 7), ("ks", 0, 8), ("k", 1, 8), ("ks", 1, 9), ("v", 0, 11), ("v", 1, 12)]
C_TOWER = [("ct", 0, 1), ("ct", 1, 2), ("pj", 0, 3), ("pj", 1, 4), ("t", 0, 6), ("t", 1, 7)] + \
          [("f1", j, 8 + j // 2) for j in range(KF)] + [("f2", 0, 12), ("f2", 1, 14)]
C_ROTARY = C_TOWER[:4]
LN_C_SLOT = 4
X_SLOT = 6
PREP_C_SLOT = 11
ROW1_SLOTS = (0, 1, 1, 2)
ROW2_SLOTS = (7, 8, 9, 11)


def tower_model_kernel(nc, ids, tok_emb, pos_emb, wq, wk, wv, w_proj, b_proj, ln1_w, ln1_b, ln2_w, ln2_b,
                       w1, b1, w2, b2, qw, kw, vw, ow, combine, top_idx, e_w1, e_b1, e_w2, e_b2,
                       consts, out):
    ctx = ExitStack()

    def sb(name, shape, dt):
        return ctx.enter_context(nc.sbuf_tensor(name, shape, dt))

    def psum(name, shape):
        return ctx.enter_context(nc.psum_tensor(name, shape, F32))

    def sem(name):
        return ctx.enter_context(nc.semaphore(name))

    x = sb("x", [P, NB, D], F32)
    cst = sb("cst", [P, 7, P], F32)
    ident16 = sb("ident16", [P, P], BF16)
    mask_ts = sb("mask_ts", [P, P], BF16)
    mask_st = sb("mask_st", [P, P], BF16)
    ident, cos16, sin16 = cst[:, 0, :], cst[:, 3, :], cst[:, 4, :]
    half = sb("half", [P, GB], F32)
    idx = sb("idx", [P, NB], I32)
    pos = sb("pos", [P, D], F32)

    raw_a = sb("raw_a", [P, 3, KD, D], F32)
    raw_p = sb("raw_p", [P, KD, D], F32)
    raw_f = sb("raw_f", [P, KD * FF], F32)
    raw_1 = raw_f[:, :].rearrange("p (k n) -> p k n", k=KD)
    raw_2 = raw_f[:, :].rearrange("p (k n) -> p k n", k=KF)
    raw_v = sb("raw_v", [P, 4, KD], F32)
    raw_b1 = sb("raw_b1", [P, KF], F32)
    raw_rows = sb("raw_rows", [P, 2, D], F32)
    wa = sb("wa", [P, 3, 2, KD, D], F16)
    wp = sb("wp", [P, 2, KD, D], F16)
    w1s = sb("w1s", [P, 2, KD, FF], F16)
    w2s = sb("w2s", [P, 2, KF, D], F16)
    bqk = sb("bqk", [P, 4], F32)
    bv = sb("bv", [P, KD], F32)
    b1c = sb("b1c", [P, KF], F32)
    row1 = sb("row1", [P, D], F32)
    row2 = sb("row2", [P, D], F32)
    fw = raw_a[:, :, :, :].bitcast(F16).rearrange("p m k n -> p (m k n)").rearrange("p (m k n) -> p m k n", m=6, k=KD)
    lnw16 = sb("lnw16", [P, 2, KD], F32)

    a_st = sb("a_st", [P, GB, 6], F32)
    a_mv = sb("a_mv", [P, GB, 2], F32)
    a_ve = sb("a_ve", [P, GB], F32)
    a_rs = sb("a_rs", [P, GB], F32)
    c_st = sb("c_st", [P, GB, 6], F32)
    c_mv = sb("c_mv", [P, GB, 2], F32)
    c_ve = sb("c_ve", [P, GB], F32)
    c_rs = sb("c_rs", [P, GB], F32)
    a_x = sb("a_x", [P, GB, D], F32)
    c_x = sb("c_x", [P, GB, D], F32)
    a_xt = sb("a_xt", [P, KD, 2, N5], F16)
    c_xt = sb("c_xt", [P, KD, 2, N5], F16)
    qk_hl = sb("qk_hl", [P, 2, 2, 2, N5], F16)
    rot_a, rot_b, rot = (raw_f[:, i * N5:(i + 1) * N5] for i in range(3))
    qs = sb("qs", [P, 2, PAIRS, N5], F16)
    ks = sb("ks", [P, 2, PAIRS, 2, N5], F16)
    vs = sb("vs", [P, 2, GB, H, HV], F16)
    negm = sb("negm", [P, 4, 4], BF16)
    pr = sb("pr", [P, 4, 4, T], F32)
    pr_lo = sb("pr_lo", [P, 4, 4, T], F16)
    rec = sb("rec", [P, 8], F32)
    o_hl = sb("o_hl", [P, 8, 2, HD], F32)
    cx = sb("cx", [P, GB, D], F32)
    cxt = sb("cxt", [P, KD, 2, N5], F16)
    act32 = sb("act32", [P, 2, N5], F32)
    hid = sb("hid", [P, 2, KF, N5], F16)

    e_w1s = [w1s[:, :, :, :], qs[:, 0, :, :].rearrange("p a n -> p (a n)").rearrange("p (h k n) -> p h k n", h=2, k=KD)]
    e_w2s = [w2s[:, :, :, :], qs[:, 1, :, :].rearrange("p a n -> p (a n)").rearrange("p (h k n) -> p h k n", h=2, k=KF)]
    e_raw2 = pr[:, :, :, :].rearrange("p u h t -> p (u h t)").rearrange("p (k n) -> p k n", k=KF)
    wout = ks[:, :, :, :, :].rearrange("p a b e n -> p (a b e n)").rearrange("p (c h n) -> p c h n", c=NCH, h=2)
    e_raw2_0 = hid[:, 0, :, :].bitcast(F32).rearrange("p k n -> p (k n)").rearrange("p (k n) -> p k n", k=KF)
    e_x = [c_x, a_x]
    e_row = [row1, row2]
    e_b1c = sb("e_b1c", [P, E, KF], F32)
    e_idx = sb("e_idx", [P, E, CAP // P], I32)
    e_idxf = sb("e_idxf", [P, NCH], F32)
    e_cw = sb("e_cw", [P, NCH, E], F32)
    num16 = a_xt[:, :, :, :].rearrange("p k a n -> p (k a n)").rearrange("p (i n) -> p i n", n=HOT)
    e_tmp = cx

    ps_s = [psum(f"ps_s{i}", [P, 4, T]) for i in range(2)]
    ps_st = [psum(f"ps_st{i}", [P, 4, T]) for i in range(2)]
    ps_o = psum("ps_o", [P, 512])
    ps_a = psum("ps_a", [P, 512])
    ps_c = [psum(f"ps_c{i}", [P, 512]) for i in range(2)]
    rows_ps = [ps_s[i][:, :, :].rearrange("p h t -> p (h t)") for i in range(2)]
    out_ps = [ps_st[i][:, :, :].rearrange("p h t -> p (h t)") for i in range(2)]
    o_ps = ps_o[:, 0:8 * HV].rearrange("p (h v) -> p h v", v=HV)

    stack_d = nc.dram_tensor("stack_d", (2, 2, P, 2, 2, N5), F16).ap()
    tokens_d = nc.dram_tensor("tokens_d", (MB * T, D), F32).ap()

    s_cst = sem("s_cst")
    s_ids = sem("s_ids")
    s_emb = [sem(f"s_emb{g}") for g in range(NG)]
    s_init = sem("s_init")
    s_zero = sem("s_zero")
    s_half = sem("s_half")
    s_pos = sem("s_pos")
    s_lda = sem("s_lda")
    s_ldc = sem("s_ldc")
    s_ld2 = sem("s_ld2")
    s_fw = sem("s_fw")
    s_fws = sem("s_fws")
    s_wa = sem("s_wa")
    s_wp = sem("s_wp")
    s_w1 = sem("s_w1")
    s_w2 = sem("s_w2")
    s_b1 = sem("s_b1")
    s_num = sem("s_num")
    s_wh = sem("s_wh")
    s_w2h = sem("s_w2h")
    s_ln16 = sem("s_ln16")
    s_bias_pe = sem("s_bias_pe")
    s_bias_a = sem("s_bias_a")
    s_bias_c = sem("s_bias_c")
    a_stat, a_mvs, a_ves, a_rstd, a_xn = sem("a_stat"), sem("a_mvs"), sem("a_ves"), sem("a_rstd"), sem("a_xn")
    a_ready, a_hi, a_free = sem("a_ready"), sem("a_hi"), sem("a_free")
    r_sum, r_hi, r_lo = sem("r_sum"), sem("r_hi"), sem("r_lo")
    st_out = sem("st_out")
    st_q, st_k = sem("st_q"), sem("st_k")
    s_ready, mx, st_ready, p_exp, p_lo, pv = sem("s_ready"), sem("mx"), sem("st_ready"), sem("p_exp"), sem("p_lo"), sem("pv")
    o_rec, o_free, o_ctx = sem("o_rec"), sem("o_free"), sem("o_ctx")
    c_stat, c_mvs, c_ves, c_rstd, c_xn = sem("c_stat"), sem("c_mvs"), sem("c_ves"), sem("c_rstd"), sem("c_xn")
    c_ready, c_hi, c_act, c_lo, c_free = sem("c_ready"), sem("c_hi"), sem("c_act"), sem("c_lo"), sem("c_free")
    s_row1, s_row2 = sem("s_row1"), sem("s_row2")
    m_out, m_idx, m_idxf = sem("m_out"), sem("m_idx"), sem("m_idxf")
    m_x = [sem(f"m_x{i}") for i in range(2)]
    m_cw, m_ld1, m_ld2, m_b1 = sem("m_cw"), sem("m_ld1"), sem("m_ld2"), sem("m_b1")
    m_row = [sem(f"m_row{i}") for i in range(2)]
    m_h1, m_l1, m_h2, m_l2 = sem("m_h1"), sem("m_l1"), sem("m_h2"), sem("m_l2")
    m_g, m_lo, m_o, m_wh, m_w = sem("m_g"), sem("m_lo"), sem("m_o"), sem("m_wh"), sem("m_w")
    m_hot, m_fin, s_out = sem("m_hot"), sem("m_fin"), sem("s_out")

    def ua(n, rotary):
        return n * 12 - 4 * TOWER if rotary else n * 8

    def ha(n, rotary):
        return n * 4 + 4 * TOWER if rotary else n * 8

    def uc(n, rotary):
        return n * 4 + 12 * TOWER if rotary else n * 16

    def hc(n, rotary):
        return n * 2 + 10 * TOWER if rotary else n * 12

    def wait(eng, s, value):
        if not isinstance(value, int) or value > 0:
            eng.wait_ge(s, value)

    def walk(eng, step, at_layer=None, before_rotary=None):
        step(0, 0, 0, 0, 0, 0, "t", False, None, "a")
        step(1, 1, 1, 0, 0, 0, "t", True, None, "c")
        with eng.Fori(0, L - 1) as l:
            if at_layer:
                at_layer(l)
            with eng.Fori(0, (NG - 2) // 2) as k:
                step(l * NG + k * 2 + 2, 0, k * 2 + 2, k * 2, l, l, "t", True, "t", None)
                step(l * NG + k * 2 + 3, 1, k * 2 + 3, k * 2 + 1, l, l, "t", True, "t", None)
            step(l * NG + NG, 0, 0, NG - 2, l + 1, l, "t", True, "t", "a")
            step(l * NG + NG + 1, 1, 1, NG - 1, l + 1, l, "t", True, "t", "c")
        if before_rotary:
            before_rotary()
        with eng.Fori(0, (NG - 2) // 2) as k:
            step(k * 2 + (TOWER - NG + 2), 0, k * 2 + 2, k * 2, L - 1, L - 1, "t", True, "t", None)
            step(k * 2 + (TOWER - NG + 3), 1, k * 2 + 3, k * 2 + 1, L - 1, L - 1, "t", True, "t", None)
        step(TOWER, 0, 0, NG - 2, L, L - 1, "r", True, "t", "r")
        step(TOWER + 1, 1, 1, NG - 1, L, L - 1, "r", True, "t", None)
        with eng.Fori(0, MB // GB // 2) as k:
            step(k * 2 + (TOWER + 2), 0, k * 2 + 2, k * 2, L, L, "r", True, "e", None)
            step(k * 2 + (TOWER + 3), 1, k * 2 + 3, k * 2 + 1, L, L, "r", True, "e", None)
        step(INST - 2, 0, NG - 2, NG - 4, L, L, "r", True, "r", "w")
        step(INST - 1, 1, NG - 1, NG - 3, L, L, "r", True, "r", "w")
        step(INST, 0, 0, NG - 2, L, L, None, True, "r", "x")
        step(INST + 1, 1, 0, NG - 1, L, L, None, False, "r", None)

    def uses(table, slot):
        return [(k, kind, j) for k, (kind, j, at) in enumerate(table) if at == slot]

    def a_uses(A, slot):
        return uses({"t": A_TOWER, "r": A_ROTARY, None: []}[A], slot)

    def c_uses(C, slot):
        return uses({"t": C_TOWER, "r": C_ROTARY, "e": C_ROTARY, None: []}[C], slot)

    def group(g):
        return x[:, bass.ds(g * GB, GB), :]

    def hi_view(ap):
        return ap.bitcast(BF16).rearrange("p (n two) -> p n two", two=2)[:, :, 1]

    PASSES = ((0, 0), (1, 0), (0, 1))

    U_E, H_E = uc(INST, True), hc(INST, True)
    U_END = U_E + E * (KF + 4)

    def ue(e):
        return e * (KF + 4) + (U_E + 2)

    def he(e):
        return e * (KF + 2) + (H_E + 2)

    def fe(e):
        return e * 4 + (U_E + 2)

    def experts(eng, expert):
        with eng.Fori(0, E // 2 - 1) as k:
            expert(k * 2, 0, k, False)
            expert(k * 2 + 1, 1, k, False)
        expert(E - 2, 0, E // 2 - 1, False)
        expert(E - 1, 1, E // 2 - 1, True)

    def hot(i, ch):
        if i % 2:
            return qs[:, :, :, :].rearrange("p a b n -> p (a b n)").rearrange("p (c n) -> p c n", c=NCH)[:, ch, :]
        w = (w1s, w2s)[ch // (NCH // 2)]
        return w[:, :, :, :].rearrange("p a k n -> p (a k n)").rearrange("p (c n) -> p c n", c=NCH // 2)[:, ch % (NCH // 2), :]

    block = ctx.enter_context(nc.Block())

    @block.sync
    def _(sp):
        def load_layer(l):
            one = bass.ds(l, 1)
            for i, v in enumerate((ln1_w, ln1_b, ln2_w, ln2_b)):
                sp.dma_start(raw_v[:, i, :], v[one, :].rearrange("l (k p) -> p (l k)", p=P),
                             allow_slow_non_contiguous=True).then_inc(s_lda, 16)
            for m, w in enumerate((wq, wk, wv)):
                sp.dma_start(raw_a[:, m, :, :], w[one, :, :].rearrange("l (k p) n -> p (l k) n", p=P)).then_inc(s_lda, 16)
            sp.dma_start(raw_p[:], w_proj[one, :, :].rearrange("l (k p) n -> p (l k) n", p=P)).then_inc(s_ldc, 16)
            sp.dma_start(raw_1, w1[one, :, :].rearrange("l (k p) n -> p (l k) n", p=P)).then_inc(s_ldc, 16)
            sp.dma_start(raw_b1[:], b1[one, :].rearrange("l (k p) -> p (l k)", p=P),
                         allow_slow_non_contiguous=True).then_inc(s_ldc, 16)
            sp.dma_start(raw_rows[:, 0, :], b_proj[one, :].broadcast_to([P, D])).then_inc(s_ldc, 16)
            sp.dma_start(raw_rows[:, 1, :], b2[one, :].broadcast_to([P, D])).then_inc(s_ldc, 16)

        sp.dma_start(idx[:], ids.rearrange("b t -> t b"), allow_slow_non_contiguous=True).then_inc(s_ids, 16)
        sp.dma_start(cst[:], consts.rearrange("c p n -> p c n")).then_inc(s_cst, 16)
        sp.dma_start(pos[:], pos_emb[0:T, :]).then_inc(s_cst, 16)
        load_layer(0)

        def step(n, par, ga, gc, la, lc, A, B, C, prep):
            for which in range(2):
                if A is None:
                    continue
                if A == "t":
                    sp.wait_ge(a_free, ua(n, False) + 4 + 2 * which)
                    sp.nop(nofuse=True)
                else:
                    sp.wait_ge(r_lo, (n - TOWER) * 4 + 2 + 2 * which)
                    sp.nop(nofuse=True)
                wait(sp, st_q, n * 128)
                sp.nop(nofuse=True)
                wait(sp, st_k, n * 256)
                sp.nop(nofuse=True)
                sp.dma_start(stack_d[par, which], qk_hl[:, which]).then_inc(st_out, 16)
                sp.wait_ge(st_out, n * 32 + 16 * (which + 1))
                sp.nop(nofuse=True)
                wait(sp, st_ready, (n - 1) * UNITS)
                sp.nop(nofuse=True)
                for c in range(4):
                    for j in range(2):
                        if which == 0:
                            rows = stack_d[par, 0, :, j, c // 2, :].rearrange("(i p) n -> p i n", p=32)
                            sp.dma_start(qs[32 * c:32 * c + 32, par, 4 * j:4 * j + 4, :], rows).then_inc(st_q, 16)
                        else:
                            for e in range(2):
                                r = 32 * c + HD * e
                                rows = stack_d[par, 1, :, j, c % 2, :].rearrange("(i e p) n -> e p i n", e=2, p=HD)[e]
                                sp.dma_start(ks[r:r + HD, par, 4 * j:4 * j + 4, e, :], rows).then_inc(st_k, 16)
                if which == 0 and C == "e":
                    sp.wait_ge(c_xn, (n - 2) * GB + GB)
                    sp.nop(nofuse=True)
                    sp.dma_start(tokens_d.rearrange("(b t) d -> t b d", t=T)[:, bass.ds(gc * GB, GB), :], c_x[:]).then_inc(m_out, 16)
            if prep == "c":
                sp.wait_ge(s_w1, la + 1)
                sp.nop(nofuse=True)
                sp.wait_ge(s_bias_pe, la * 2 + 2)
                sp.nop(nofuse=True)
                sp.dma_start(raw_2, w2[bass.ds(la, 1), :, :].rearrange("l (k p) n -> p (l k) n", p=P)).then_inc(s_ld2, 16)
            if prep == "x":
                sp.wait_ge(r_lo, NG * 4)
                sp.nop(nofuse=True)
                sp.dma_start(raw_1, e_w1[0].rearrange("(k p) n -> p k n", p=P)).then_inc(m_ld1, 16)
                sp.dma_start(e_raw2_0, e_w2[0].rearrange("(k p) n -> p k n", p=P)).then_inc(m_ld2, 16)
                for e in range(2):
                    sp.dma_start(e_row[e][:], e_b2[e:e + 1, :].broadcast_to([P, D])).then_inc(m_row[e], 16)

        def layer_done(l):
            sp.wait_ge(s_w2, l + 1)
            sp.nop(nofuse=True)
            sp.wait_ge(s_bias_c, l * 3 + 3)
            sp.nop(nofuse=True)

        def next_layer(l):
            layer_done(l)
            load_layer(l + 1)

        def rotary_weights():
            layer_done(L - 1)
            for m, w in enumerate((qw, kw, vw, ow)):
                sp.dma_start(fw[:, m, :, :], w.rearrange("(k p) n -> p k n", p=P)).then_inc(s_fw, 16)
            sp.dma_start(e_idx[:], top_idx.rearrange("(c p) e -> p e c", p=P), allow_slow_non_contiguous=True).then_inc(m_idx, 16)
            sp.dma_start(e_b1c[:], e_b1.rearrange("e (k p) -> p e k", p=P), allow_slow_non_contiguous=True).then_inc(m_b1, 16)

        walk(sp, step, next_layer, rotary_weights)

        sp.wait_ge(m_l1, 1)
        sp.nop(nofuse=True)
        sp.dma_start(raw_1, e_w1[1].rearrange("(k p) n -> p k n", p=P)).then_inc(m_ld1, 16)
        sp.wait_ge(pv, INST * UNITS)
        sp.nop(nofuse=True)
        sp.wait_ge(m_l2, 1)
        sp.nop(nofuse=True)
        sp.dma_start(e_raw2, e_w2[1].rearrange("(k p) n -> p k n", p=P)).then_inc(m_ld2, 16)
        sp.wait_ge(c_free, U_E)
        sp.nop(nofuse=True)
        for g in range(MB // GB, NG):
            sp.dma_start(out[g * GB:(g + 1) * GB].rearrange("b t d -> t b d"), group(g)).then_inc(s_out, 16)

        def expert(e, par, k):
            one = bass.ds(e, 1)
            sp.wait_ge(m_l1, e)
            sp.nop(nofuse=True)
            sp.dma_start(raw_1, e_w1[one, :, :].rearrange("l (k p) n -> p (l k) n", p=P)).then_inc(m_ld1, 16)
            sp.wait_ge(m_l2, e)
            sp.nop(nofuse=True)
            sp.dma_start(e_raw2, e_w2[one, :, :].rearrange("l (k p) n -> p (l k) n", p=P)).then_inc(m_ld2, 16)
            sp.wait_ge(m_w, e * 4 - 4)
            sp.nop(nofuse=True)
            sp.dma_start(e_row[par][:], e_b2[one, :].broadcast_to([P, D])).then_inc(m_row[par], 16)

        with sp.Fori(1, E // 2) as k:
            expert(k * 2, 0, k)
            expert(k * 2 + 1, 1, k)
        for g in range(MB // GB):
            sp.wait_ge(m_fin, (g + 1) * GB)
            sp.nop(nofuse=True)
            sp.dma_start(out[g * GB:(g + 1) * GB].rearrange("b t d -> t b d"), group(g)).then_inc(s_out, 16)
        sp.wait_ge(s_out, NG * 16)
        sp.nop(nofuse=True)

    @block.gpsimd
    def _(pool):
        pool.wait_ge(s_ids, 16)
        def embed(b):
            pool.indirect_dma_start(x[:, b, :], None, tok_emb, bass.IndirectOffsetOnAxis(ap=idx[:, b:b + 1].bitcast(U32), axis=0),
                                    ).then_inc(s_emb[b // GB], 16)

        for b in range(2 * GB):
            embed(b)
        nc.gpsimd.memset(half[:], -0.5).then_inc(s_half, 1)
        pool.wait_ge(s_half, 1)

        def inv_std(mv, ve, rs, s_mv, s_ve, s_rs, n):
            pool.wait_ge(s_mv, n * GB + GB)
            pool.nop(nofuse=True)
            nc.gpsimd.tensor_scalar(ve[:], mv[:, :, 1], EPS, 1.0, ALU.add, ALU.mult).then_inc(s_ve, 1)
            pool.wait_ge(s_ve, n + 1)
            nc.gpsimd.tensor_tensor(rs[:], ve[:], half[:], ALU.pow).then_inc(s_rs, 1)

        def add_contexts(b, q):
            pool.wait_ge(o_free, b * 8 + q + 1)
            dst = cx[:, q // 2, P * (q % 2):P * (q % 2) + P].rearrange("p (h d) -> p h d", d=HD)
            nc.gpsimd.tensor_tensor(dst, o_hl[:, :, 0, :], o_hl[:, :, 1, :], ALU.add).then_inc(o_ctx, 1)

        def add_row(row, g, i, done):
            seq = x[:, bass.ds(g * GB + i, 1), :].rearrange("p a d -> p (a d)")
            nc.gpsimd.tensor_tensor(seq, seq, row[:, :], ALU.add).then_inc(done, 1)

        def expert_rows(e, ch):
            pool.indirect_dma_start(e_x[e % 2][:, ch, :], None, tokens_d,
                                    bass.IndirectOffsetOnAxis(ap=e_idx[:, e, ch:ch + 1].bitcast(U32), axis=0)
                                    ).then_inc(m_x[e % 2], 16)

        def step(n, par, ga, gc, la, lc, A, B, C, prep):
            b, c = n - 1, n - 2
            for s in range(SLOTS):
                for k, kind, j in a_uses(A, s):
                    if kind in ("qs", "ks"):
                        r = (n - TOWER) * 4 + 2 * (kind == "ks") + j
                        pool.wait_ge(a_free, ua(n, True) + k + 1)
                        wait(pool, r_lo, r)
                        nc.gpsimd.tensor_tensor(rot, rot_a, rot_b, ALU.add).then_inc(r_sum, 1)
                if B:
                    pool.wait_ge(p_exp, b * UNITS + s + 1)
                    wait(pool, pv, b * UNITS + s - 3)
                    flat = pr[:, s % 4].rearrange("p h t -> p (h t)")
                    nc.gpsimd.tensor_tensor(pr_lo[:, s % 4].rearrange("p h t -> p (h t)"), flat, hi_view(flat),
                                            ALU.subtract).then_inc(p_lo, 1)
                if s == 0 and C:
                    add_contexts(c, 7)
                if s == 0 and A:
                    inv_std(a_mv, a_ve, a_rs, a_mvs, a_ves, a_rstd, n)
                if isinstance(n, int) and n == 0 and 2 * (s + 1) <= NB - 2 * GB:
                    embed(2 * GB + 2 * s)
                    embed(2 * GB + 2 * s + 1)
                if B and s >= 2 and s % 2 == 0:
                    if C and s == 2:
                        pool.wait_ge(c_ready, uc(c, C != "t") + 2)
                    add_contexts(b, s // 2 - 1)
                if C == "t" and s in ROW1_SLOTS:
                    if s == ROW1_SLOTS[0]:
                        pool.wait_ge(s_bias_c, lc * 3 + 3)
                        pool.nop(nofuse=True)
                    for i in range(GB):
                        if ROW1_SLOTS[i] == s:
                            add_row(row1, gc, i, s_row1)
                if C in ("t", "e") and s == LN_C_SLOT:
                    inv_std(c_mv, c_ve, c_rs, c_mvs, c_ves, c_rstd, c)
                if C == "t" and s in ROW2_SLOTS:
                    i = ROW2_SLOTS.index(s)
                    pool.wait_ge(c_xn, c * GB + i + 1)
                    pool.nop(nofuse=True)
                    add_row(row2, gc, i, s_row2)

                if prep == "w":
                    if s == 0:
                        pool.wait_ge(m_idx, 16)
                    ch = (n - (INST - 2)) * SLOTS + s
                    pool.indirect_dma_start(e_cw[:, ch, :], None, combine,
                                            bass.IndirectOffsetOnAxis(ap=e_idx[:, ch // 4, ch % 4:ch % 4 + 1].bitcast(U32), axis=0)
                                            ).then_inc(m_cw, 16)
                if prep == "x" and s < 2 * (CAP // P):
                    if s == 0:
                        pool.wait_ge(m_out, 16 * (MB // GB))
                        pool.wait_ge(a_ready, ua(INST, True))
                    expert_rows(s // (CAP // P), s % (CAP // P))

        walk(pool, step)

        for e in range(2, E):
            pool.wait_ge(c_ready, max(ue(e - 2) - 2, U_E + 2))
            for ch in range(CAP // P):
                expert_rows(e, ch)

    @block.scalar
    def _(act):
        def split_hi(e, par, raw2=None):
            act.wait_ge(m_ld1, e * 16 + 16)
            nc.scalar.activation(e_w1s[par][:, 0], raw_1, ACT.Copy, scale=WS).then_inc(m_h1, 1)
            act.wait_ge(m_ld2, e * 16 + 16)
            nc.scalar.activation(e_w2s[par][:, 0], e_raw2 if raw2 is None else raw2, ACT.Copy, scale=WS).then_inc(m_h2, 1)

        def step(n, par, ga, gc, la, lc, A, B, C, prep):
            b, c = n - 1, n - 2
            for s in range(SLOTS):
                for k, kind, j in a_uses(A, s):
                    if kind in ("t", "v") or A == "t":
                        act.wait_ge(a_ready, ua(n, A == "r") + k + 1)
                    if kind == "t":
                        nc.scalar.activation(a_xt[:, j, 0, :], ps_a[:, :], ACT.Copy).then_inc(a_hi, 1)
                    elif kind == "v":
                        if j == 0:
                            wait(act, pv, (n - 1) * UNITS)
                        src = ps_a[:, :].rearrange("p (b h d) -> p b h d", b=2, h=H)
                        nc.scalar.activation(vs[:, par, 2 * j:2 * j + 2, :, 0:HD], src, ACT.Copy,
                                             scale=1.0 if A == "t" else WS).then_inc(a_hi, 1)
                    elif A == "t":
                        w = int(kind == "k")
                        wait(act, st_out, n * 32)
                        if kind == "q" and j == 0:
                            act.wait_ge(s_bias_a, la * 2 + 2)
                        nc.scalar.activation(qk_hl[:, w, j, 0, :], ps_a[:, :], ACT.Identity,
                                             bias=bqk[:, 2 * w + j:2 * w + j + 1]).then_inc(a_hi, 1)
                if B:
                    act.wait_ge(st_ready, b * UNITS + s + 1)
                    wait(act, pv, b * UNITS + s - 3)
                    nc.scalar.activation(pr[:, s % 4], ps_st[s % 2][:], ACT.Exp, scale=SCORE).then_inc(p_exp, 1)
                for k, kind, j in a_uses(A, s):
                    if kind in ("qs", "ks"):
                        w = int(kind == "ks")
                        r = (n - TOWER) * 4 + 2 * w + j
                        act.wait_ge(r_sum, r + 1)
                        act.wait_ge(st_out, n * 32)
                        nc.scalar.activation(qk_hl[:, w, j, 0, :], rot, ACT.Copy).then_inc(r_hi, 1)
                for k, kind, j in c_uses(C, s):
                    if kind in ("pj", "f2"):
                        continue
                    act.wait_ge(c_ready, uc(c, C != "t") + k + 1)
                    bank = ps_c[k % 2]
                    if kind == "ct":
                        nc.scalar.activation(cxt[:, j, 0, :], bank[:, :], ACT.Copy).then_inc(c_hi, 1)
                    elif kind == "t":
                        nc.scalar.activation(c_xt[:, j, 0, :], bank[:, :], ACT.Copy).then_inc(c_hi, 1)
                    else:
                        if j == 0:
                            act.wait_ge(s_bias_c, lc * 3 + 3)
                        nc.scalar.activation(hid[:, 0, j, :], bank[:, :], ACT.Relu, bias=b1c[:, j:j + 1]).then_inc(c_hi, 1)

                if prep == "x" and s == X_SLOT:
                    split_hi(0, 0, e_raw2_0)
            if prep == "c":
                wait(act, c_ready, uc(c, False) + 16)
                act.wait_ge(s_ld2, la * 16 + 16)
                nc.scalar.activation(w2s[:, 0], raw_2, ACT.Copy, scale=WS).then_inc(s_w2h, 1)

        walk(act, step)

        act.wait_ge(m_b1, 16)

        def token_hi(count, j):
            act.wait_ge(c_ready, count)
            nc.scalar.activation(c_xt[:, j, 0, :], rows_ps[j], ACT.Copy).then_inc(c_hi, 1)

        for j in range(KD):
            token_hi(U_E + j + 1, j)
        act.wait_ge(m_l2, 1)

        def expert(e, par, k_, last):
            for j in range(KF):
                act.wait_ge(c_ready, ue(e) + j + 1)
                act.wait_ge(m_lo, e * KF + max(j - 1, 0))
                nc.scalar.activation(act32[:, j % 2, :], ps_c[j % 2][:, :], ACT.Gelu_apprx_tanh,
                                     scale=1.0 / WS, bias=e_b1c[:, bass.ds(e, 1), j:j + 1].rearrange("p a b -> p (a b)")).then_inc(m_g, 1)
                act.wait_ge(m_g, e * KF + j + 1)
                nc.scalar.activation(hid[:, 0, j, :], act32[:, j % 2, :], ACT.Copy).then_inc(c_hi, 1)
            if not last:
                for j in range(KD):
                    token_hi(ue(e) + KF + j + 1, j)
                split_hi(e + 1, 1 - par)

        experts(act, expert)

    @block.tensor
    def _(pe):
        mm = nc.tensor.matmul

        def step(n, par, ga, gc, la, lc, A, B, C, prep):
            b, c, pb = n - 1, n - 2, 1 - par
            UA, UC = ua(n, A == "r"), uc(c, C != "t")

            def tok(bb):
                return slice(T * bb, T * bb + T)

            def scores(i, pi, u):
                bb, quad = u // 4, u % 4
                dst = ps_s[u % 2]
                if u == 0:
                    pe.wait_ge(st_q, i * 128 + 128)
                    pe.wait_ge(st_k, i * 256 + 256)
                wait(pe, mx, i * UNITS + u - 1)
                mm(dst[:], ident16[:], mask_ts[:, :].unsqueeze(1).broadcast_to([P, 4, T]), start=True, stop=False)
                for z in range(2):
                    p = 2 * quad + z
                    last = mm(dst[:, 2 * z:2 * z + 2, :], qs[:, pi, p, tok(bb)], ks[:, pi, p, :, tok(bb)], start=False, stop=z == 1)
                last.then_inc(s_ready, 1)

            def scores_t(u):
                bb, quad = u // 4, u % 4
                dst = ps_st[u % 2]
                pe.wait_ge(mx, b * UNITS + u + 1)
                wait(pe, p_exp, b * UNITS + u - 1)
                mm(dst[:], ident16[:], mask_st[:, :].unsqueeze(1).broadcast_to([P, 4, T]), start=True, stop=False)
                for h in range(4):
                    p = 2 * quad + h // 2
                    mm(dst[:, h, :], negm[:, u % 4, h:h + 1].broadcast_to([P, T]), ident16[:], start=False, stop=False)
                    last = mm(dst[:, h, :], ks[:, pb, p, h % 2, tok(bb)], qs[:, pb, p, tok(bb)], start=False, stop=h == 3)
                last.then_inc(st_ready, 1)

            def times_v(i, pi, u):
                bb, quad = u // 4, u % 4
                pe.wait_ge(p_lo, i * UNITS + u + 1)
                if u % 2 == 0:
                    wait(pe, o_free, i * 8 + u // 2)
                for h in range(4):
                    dst = o_ps[:, 4 * (u % 2) + h, :]
                    v = vs[:, pi, bb, 4 * quad + h, :]
                    mm(dst, hi_view(pr[:, u % 4, h, :]), v, start=True, stop=False)
                    last = mm(dst, pr_lo[:, u % 4, h, :], v, start=False, stop=True)
                last.then_inc(pv, 1)

            def a_use(k, kind, j):
                wait(pe, a_free, UA + k)
                if kind == "t":
                    if j == 0:
                        pe.wait_ge(a_xn, n * GB + GB)
                        if prep == "a":
                            pe.wait_ge(s_bias_a, la * 2 + 2)
                    for bb in range(GB):
                        last = nc.tensor.transpose(ps_a[:, tok(bb)], a_x[:, bb, P * j:P * j + P], ident)
                elif kind == "v":
                    for i in range(2):
                        t = tok(2 * j + i)
                        terms = [(kt, hw, hx) for kt in range(KD) for hw, hx in (PASSES if A == "t" else ((0, 0), (0, 1)))]
                        for z, (kt, hw, hx) in enumerate(terms):
                            w = wa[:, 2, hw, kt, :] if A == "t" else fw[:, 2, kt, :]
                            last = mm(ps_a[:, D * i:D * i + D], a_xt[:, kt, hx, t], w, start=z == 0, stop=z == len(terms) - 1)
                else:
                    if kind == "q" and j == 0:
                        pe.wait_ge(s_wa, la + 1) if A == "t" else pe.wait_ge(s_fws, 4)
                    terms = [(kt, hw, hx) for kt in range(KD) for hw, hx in (PASSES if A == "t" else ((0, 0), (0, 1)))]
                    m = {"q": 0, "k": 1, "qs": 4, "ks": 5}[kind]
                    for z, (kt, hw, hx) in enumerate(terms):
                        w = (wa[:, m, hw, kt, :] if A == "t" else fw[:, m, kt, :])[:, P * j:P * j + P]
                        last = mm(ps_a[:, :], w, a_xt[:, kt, hx, :], start=z == 0, stop=z == len(terms) - 1)
                last.then_inc(a_ready, 1)

            def c_use(k, kind, j):
                bank = ps_c[k % 2]
                if kind != "f2":
                    wait(pe, c_free, UC + max(k - 1, 0))
                if kind == "ct":
                    if j == 0:
                        pe.wait_ge(o_ctx, c * 8 + 8)
                    for bb in range(GB):
                        last = nc.tensor.transpose(bank[:, tok(bb)], cx[:, bb, P * j:P * j + P], ident)
                elif kind == "pj":
                    if j == 0:
                        pe.wait_ge(c_free, UC + 2)
                        if C == "t":
                            pe.wait_ge(s_wp, lc + 1)
                    for i in range(2):
                        t = tok(2 * j + i)
                        terms = [(kt, hw, hx) for kt in range(KD) for hw, hx in (PASSES if C == "t" else ((0, 0), (0, 1)))]
                        for z, (kt, hw, hx) in enumerate(terms):
                            w = wp[:, hw, kt, :] if C == "t" else fw[:, 3, kt, :]
                            last = mm(bank[:, D * i:D * i + D], cxt[:, kt, hx, t], w, start=z == 0, stop=z == len(terms) - 1)
                elif kind == "t":
                    if j == 0:
                        pe.wait_ge(c_xn, c * GB + GB)
                    for bb in range(GB):
                        last = nc.tensor.transpose(bank[:, tok(bb)], c_x[:, bb, P * j:P * j + P], ident)
                elif kind == "f1":
                    if j == 0:
                        pe.wait_ge(c_free, UC + 6)
                        pe.wait_ge(s_w1, lc + 1)
                    last = feed_1(bank, w1s, j)
                last.then_inc(c_ready, 1)

            if prep == "a":
                bias_products_a(n, la)
            for s in range(SLOTS):
                if prep == "c" and s == PREP_C_SLOT:
                    bias_products_c(n, la)
                for use in a_uses(A, s):
                    a_use(*use)
                if B:
                    scores_t(s)
                if s < SLOTS - 1 and B:
                    scores(b, pb, s + 1)
                elif s == SLOTS - 1 and A:
                    scores(n, par, 0)
                if s == 0 and C:
                    times_v(c, par, UNITS - 1)
                elif s and B:
                    times_v(b, pb, s - 1)
                for use in c_uses(C, s):
                    if use[1] != "f2":
                        c_use(*use)
                if C == "t" and s >= 12:
                    j, i = (s - 12) // 2, s % 2
                    k = 14 + j
                    if s == 12:
                        pe.wait_ge(s_w2, lc + 1)
                    if i == 0:
                        pe.wait_ge(c_free, UC + k - 1)
                    last = feed_2(ps_c[k % 2], w2s, 2 * j + i, i, (c_lo, c * KF) if s == 12 else None)
                    if i == 1:
                        last.then_inc(c_ready, 1)

        def feed_1(bank, w, j):
            terms = [(kt, hw, hx) for kt in range(KD) for hw, hx in PASSES]
            for z, (kt, hw, hx) in enumerate(terms):
                last = mm(bank[:, :], w[:, hw, kt, P * j:P * j + P], c_xt[:, kt, hx, :], start=z == 0, stop=z == len(terms) - 1)
            return last

        def feed_2(bank, w, bb, i, split=None):
            terms = [(kt, hw, hx) for kt in range(KF) for hw, hx in PASSES]
            for z, (kt, hw, hx) in enumerate(terms):
                if split and z % len(PASSES) == 0:
                    pe.wait_ge(split[0], split[1] + (kt + 1))
                last = mm(bank[:, D * i:D * i + D], hid[:, hx, kt, T * bb:T * bb + T], w[:, hw, kt, :],
                          start=z == 0, stop=z == len(terms) - 1)
            return last

        def bias_products_a(n, l):
            pe.wait_ge(s_lda, l * LOADS_A + LOADS_A)
            wait(pe, a_free, ua(n, False))
            for m in range(3):
                for j in range(KD):
                    for kt in range(KD):
                        col = 2 * m + j
                        last = mm(ps_a[:, col:col + 1], raw_a[:, m, kt, P * j:P * j + P], raw_v[:, 1, kt:kt + 1],
                                  start=kt == 0, stop=kt == KD - 1)
            last.then_inc(s_bias_pe, 1)

        def bias_products_c(n, l):
            pe.wait_ge(s_ldc, l * LOADS_C + LOADS_C)
            pe.wait_ge(a_free, ua(n, False) + len(A_TOWER))
            for kt in range(KD):
                mm(ps_a[:, 0:D], bv[:, kt:kt + 1].broadcast_to([P, P]), raw_p[:, kt, :], start=kt == 0, stop=kt == KD - 1)
            for j in range(KF):
                for kt in range(KD):
                    last = mm(ps_a[:, D + j:D + j + 1], raw_1[:, kt, P * j:P * j + P], raw_v[:, 3, kt:kt + 1],
                              start=kt == 0, stop=kt == KD - 1)
            last.then_inc(s_bias_pe, 1)

        pe.wait_ge(s_cst, 32)
        pe.wait_ge(s_init, 3)
        pe.wait_ge(s_zero, 2)
        walk(pe, step)

        def transpose_rows(j, par):
            for ch in range(CAP // P):
                last = nc.tensor.transpose(rows_ps[j][:, T * ch:T * ch + T], e_x[par][:, ch, P * j:P * j + P], ident)
            last.then_inc(c_ready, 1)

        pe.wait_ge(m_x[0], CAP // P * 16)
        pe.wait_ge(mx, INST * UNITS)
        for j in range(KD):
            transpose_rows(j, 0)
        pe.wait_ge(c_free, U_E + 2)
        pe.wait_ge(p_exp, INST * UNITS)

        def expert(e, par, k_, last):
            for j in range(KF):
                if j == 0:
                    pe.wait_ge(c_free, fe(e) - 2)
                    pe.wait_ge(m_l1, e + 1)
                pe.wait_ge(m_g, e * KF + max(j - 1, 0))
                feed_1(ps_c[j % 2], e_w1s[par], j).then_inc(c_ready, 1)
            if not last:
                pe.wait_ge(m_x[1 - par], (k_ + par) * 64 + 64)
                for j in range(KD):
                    transpose_rows(j, 1 - par)
            for j in range(2):
                pe.wait_ge(c_free, fe(e) - 1 + j)
                if j == 0:
                    pe.wait_ge(m_l2, e + 1)
                for i in range(2):
                    done = feed_2(out_ps[j], e_w2s[par], 2 * j + i, i, (m_lo, e * KF) if i == j == 0 else None)
                done.then_inc(c_ready, 1)

        experts(pe, expert)

        for b in range(MB):
            i, n0 = b * T // HOT, b * T % HOT
            if b >= 2:
                pe.wait_ge(m_fin, b - 1)
            elif b == 0:
                pe.wait_ge(m_g, E * KF)
            for ch in range(NCH):
                if n0 == 0:
                    pe.wait_ge(m_hot, i * NCH + ch + 1)
                if b == 0 and ch % (CAP // P) == 0:
                    pe.wait_ge(m_w, ch + CAP // P)
                for hl in range(2):
                    last = mm(ps_c[b % 2][:, 0:D], hot(i, ch)[:, n0:n0 + T], wout[:, ch, hl, :],
                              start=ch + hl == 0, stop=ch + hl == NCH)
            last.then_inc(c_ready, 1)

    @block.vector
    def _(dve):
        V = nc.vector
        ln_a = (a_st, a_mv, a_rs, a_x, a_stat, a_mvs, a_rstd, a_xn)
        ln_c = (c_st, c_mv, c_rs, c_x, c_stat, c_mvs, c_rstd, c_xn)

        def stats(ln, n, g, seqs=range(GB)):
            st, mv, rs, xn, s_st, s_mv, s_rs, s_xn = ln
            dve.nop(nofuse=True)
            for i in seqs:
                V.bn_stats(st[:, i, :], x[:, bass.ds(g * GB + i, 1), :].rearrange("p a d -> p (a d)")).then_inc(s_st, 1)
            for i in seqs:
                dve.wait_ge(s_st, n * GB + i + 1)
                dve.nop(nofuse=True)
                V.bn_aggr(mv[:, i, :], st[:, i, :]).then_inc(s_mv, 1)

        def normalise(ln, n, g, dst=None):
            st, mv, rs, xn, s_st, s_mv, s_rs, s_xn = ln
            dve.wait_ge(s_rs, n + 1)
            for i in range(GB):
                V.tensor_scalar((dst or xn)[:, i, :], x[:, bass.ds(g * GB + i, 1), :].rearrange("p a d -> p (a d)"),
                                mv[:, i, 0:1], rs[:, i:i + 1], ALU.subtract, ALU.mult).then_inc(s_xn, 1)

        def split_lo(dst, raw, scale, hi):
            return V.scalar_tensor_tensor(out=dst, in0=raw, scalar=scale, in1=hi, op0=ALU.mult, op1=ALU.subtract)

        def prep_a(n, l):
            dve.wait_ge(s_lda, l * LOADS_A + LOADS_A)
            wait(dve, a_ready, ua(n, False))
            V.tensor_scalar(lnw16[:], raw_v[:, 0:4:2, :], WS, None, ALU.mult).then_inc(s_ln16, 1)
            dve.wait_ge(s_ln16, l + 1)
            for kt in range(KD):
                V.tensor_scalar(wa[:, :, 0, kt, :], raw_a[:, :, kt, :], lnw16[:, 0, kt:kt + 1], None, ALU.mult).then_inc(s_wh, 1)
            dve.wait_ge(s_bias_pe, l * 2 + 1)
            V.tensor_scalar(bqk[:], ps_a[:, 0:4], WS, None, ALU.mult).then_inc(s_bias_a, 1)
            V.tensor_copy(bv[:], ps_a[:, 4:6]).then_inc(s_bias_a, 1)
            for kt in range(KD):
                dve.wait_ge(s_wh, l * SPLITS + kt + 1)
                last = split_lo(wa[:, :, 1, kt, :], raw_a[:, :, kt, :], lnw16[:, 0, kt:kt + 1], wa[:, :, 0, kt, :])
            last.then_inc(s_wa, 1)

        def prep_p(c, l):
            dve.wait_ge(s_ldc, l * LOADS_C + LOADS_C)
            wait(dve, c_ready, uc(c, False) + 4)
            V.tensor_scalar(wp[:, 0], raw_p[:], WS, None, ALU.mult).then_inc(s_wh, 1)
            dve.wait_ge(s_wh, l * SPLITS + 3)
            split_lo(wp[:, 1], raw_p[:], WS, wp[:, 0]).then_inc(s_wp, 1)

        def prep_1(c, l):
            wait(dve, c_ready, uc(c, False) + 14)
            for kt in range(KD):
                V.tensor_scalar(w1s[:, 0, kt, :], raw_1[:, kt, :], lnw16[:, 1, kt:kt + 1], None, ALU.mult).then_inc(s_wh, 1)
            for kt in range(KD):
                dve.wait_ge(s_wh, l * SPLITS + 4 + kt)
                last = split_lo(w1s[:, 1, kt, :], raw_1[:, kt, :], lnw16[:, 1, kt:kt + 1], w1s[:, 0, kt, :])
            last.then_inc(s_w1, 1)

        def prep_b(c, l):
            dve.wait_ge(s_bias_pe, l * 2 + 2)
            wait(dve, s_row1, c * GB + GB)
            wait(dve, s_row2, c * GB + GB)
            wait(dve, c_hi, hc(c, False) + 12)
            wait(dve, c_free, uc(c, False) + 14)
            V.tensor_tensor(row1[:], ps_a[:, 0:D], raw_rows[:, 0, :], ALU.add).then_inc(s_bias_c, 1)
            V.tensor_copy(row2[:], raw_rows[:, 1, :]).then_inc(s_bias_c, 1)
            V.tensor_tensor(b1c[:], ps_a[:, D:D + KF], raw_b1[:], ALU.add).then_inc(s_b1, 1)
            dve.wait_ge(s_b1, l + 1)
            V.tensor_scalar(b1c[:], b1c[:], WS, None, ALU.mult).then_inc(s_bias_c, 1)

        def prep_2(c, l):
            dve.wait_ge(s_w2h, l + 1)
            split_lo(w2s[:, 1], raw_2, WS, w2s[:, 0]).then_inc(s_w2, 1)

        def split_lows(e, par, raw2=None):
            dve.wait_ge(m_h1, e + 1)
            split_lo(e_w1s[par][:, 1], raw_1, WS, e_w1s[par][:, 0]).then_inc(m_l1, 1)
            dve.wait_ge(m_h2, e + 1)
            split_lo(e_w2s[par][:, 1], e_raw2 if raw2 is None else raw2, WS, e_w2s[par][:, 0]).then_inc(m_l2, 1)

        def prep_r():
            dve.wait_ge(s_fw, 64)
            for m in range(2):
                src = fw[:, m].rearrange("p k (n two) -> p k n two", two=2)
                dst = fw[:, 4 + m].rearrange("p k (n two) -> p k n two", two=2)
                V.tensor_scalar(dst[:, :, :, 0], src[:, :, :, 1], -1.0, None, ALU.mult).then_inc(s_fws, 1)
                V.tensor_copy(dst[:, :, :, 1], src[:, :, :, 0]).then_inc(s_fws, 1)

        def step(n, par, ga, gc, la, lc, A, B, C, prep):
            b, c = n - 1, n - 2
            UA, UC = ua(n, A == "r"), uc(c, C != "t")

            def maxima(i, u):
                dve.wait_ge(s_ready, i * UNITS + u + 1)
                V.tensor_reduce(negm[:, u % 4, :], ps_s[u % 2][:], AX_X, ALU.max, negate=True).then_inc(mx, 1)

            def contexts(i, q):
                dve.wait_ge(pv, i * UNITS + 2 * q + 2)
                V.reciprocal(rec[:], o_ps[:, :, 2 * HD]).then_inc(o_rec, 1)
                dve.wait_ge(o_rec, i * 8 + q + 1)
                wait(dve, o_ctx, i * 8 + q)
                V.tensor_tensor(o_hl[:].rearrange("p h a d -> p h (a d)"), o_ps[:, :, 0:2 * HD],
                                rec[:, :].unsqueeze(2).broadcast_to([P, 8, 2 * HD]), ALU.mult).then_inc(o_free, 1)

            def rotary_lo(kind, j):
                w = int(kind == "ks")
                r = (n - TOWER) * 4 + 2 * w + j
                dve.wait_ge(r_hi, r + 1)
                V.tensor_tensor(qk_hl[:, w, j, 1, :], rot, qk_hl[:, w, j, 0, :], ALU.subtract).then_inc(r_lo, 1)

            for s in range(SLOTS):
                for k, kind, j in a_uses(A, s - 1):
                    if kind in ("qs", "ks"):
                        rotary_lo(kind, j)
                for k, kind, j in a_uses(A, s):
                    if kind in ("t", "v") or A == "t":
                        dve.wait_ge(a_hi, ha(n, A == "r") + (k + 1 if A == "t" or kind == "t" else k - 7))
                    if kind == "t":
                        V.tensor_tensor(a_xt[:, j, 1, :], ps_a[:, :], a_xt[:, j, 0, :], ALU.subtract).then_inc(a_free, 1)
                    elif kind == "v":
                        src = ps_a[:, :].rearrange("p (h d) -> p h d", d=HD)
                        v = vs[:, par, 2 * j:2 * j + 2, :, :].rearrange("p b h v -> p (b h) v")
                        V.scalar_tensor_tensor(out=v[:, :, HD:2 * HD], in0=src, scalar=1.0 if A == "t" else WS,
                                               in1=v[:, :, 0:HD], op0=ALU.mult, op1=ALU.subtract).then_inc(a_free, 1)
                    elif A == "t":
                        w = int(kind == "k")
                        V.scalar_tensor_tensor(out=qk_hl[:, w, j, 1, :], in0=ps_a[:, :], scalar=bqk[:, 2 * w + j:2 * w + j + 1],
                                               in1=qk_hl[:, w, j, 0, :], op0=ALU.add, op1=ALU.subtract).then_inc(a_free, 1)
                    else:
                        r = (n - TOWER) * 4 + 2 * (kind[0] == "k") + j
                        dve.wait_ge(a_ready, UA + k + 1)
                        wait(dve, r_sum, r)
                        table = sin16 if kind[1:] else cos16
                        V.tensor_tensor((rot_b if kind[1:] else rot_a).rearrange("p (b t) -> p b t", t=T),
                                        ps_a[:, :].rearrange("p (b t) -> p b t", t=T),
                                        table.unsqueeze(1).broadcast_to([P, GB, T]), ALU.mult).then_inc(a_free, 1)
                if s < SLOTS - 1 and B:
                    maxima(b, s + 1)
                elif s == SLOTS - 1 and A:
                    maxima(n, 0)
                if s == 0 and C:
                    contexts(c, 7)
                if s == 0 and A:
                    if isinstance(n, int) and n < 2:
                        position(n)
                    stats(ln_a, n, ga)
                if s >= 2 and s % 2 == 0 and B:
                    contexts(b, s // 2 - 1)
                if s == 1 and A:
                    wait(dve, a_ready, UA)
                    normalise(ln_a, n, ga)
                if s == 1 and prep == "a":
                    prep_a(n, la)
                if s == 1 and prep == "r":
                    prep_r()
                if isinstance(n, int) and n == 1 and 3 <= s < 1 + NG:
                    position(s - 1)
                for k, kind, j in c_uses(C, s):
                    if kind == "f2":
                        continue
                    bank = ps_c[k % 2]
                    if kind == "pj":
                        dve.wait_ge(c_ready, UC + k + 1)
                        if C == "t":
                            dve.wait_ge(s_row1, c * GB + 2 * j + 2)
                        residual(bank, gc, j, WS * WS if C == "t" else WS)
                        continue
                    order = k + 1 if k < 2 else k - 1
                    dve.wait_ge(c_hi, hc(c, C != "t") + order)
                    if kind == "ct":
                        V.tensor_tensor(cxt[:, j, 1, :], bank[:, :], cxt[:, j, 0, :], ALU.subtract).then_inc(c_free, 1)
                    elif kind == "t":
                        V.tensor_tensor(c_xt[:, j, 1, :], bank[:, :], c_xt[:, j, 0, :], ALU.subtract).then_inc(c_free, 1)
                    else:
                        wait(dve, c_lo, c * KF + max(j - 1, 0))
                        V.tensor_scalar(act32[:, j % 2, :], bank[:, :], b1c[:, j:j + 1], 0.0, ALU.add, ALU.max).then_inc(c_free, 1)
                for k, kind, j in c_uses(C, s):
                    if kind == "f1":
                        dve.wait_ge(c_free, UC + k + 1)
                        V.tensor_tensor(hid[:, 1, j, :], act32[:, j % 2, :], hid[:, 0, j, :], ALU.subtract).then_inc(c_lo, 1)
                if C in ("t", "e") and s in (LN_C_SLOT - 1, LN_C_SLOT):
                    j = s - (LN_C_SLOT - 1)
                    dve.wait_ge(c_free, UC + 3 + j)
                    stats(ln_c, c, gc, range(2 * j, 2 * j + 2))
                if C in ("t", "e") and s == LN_C_SLOT + 1:
                    if C == "e":
                        dve.wait_ge(m_out, (c - TOWER) * 16)
                    normalise(ln_c, c, gc)
                if prep == "x" and s == X_SLOT + 1:
                    split_lows(0, 0, e_raw2_0)
                if C == "t" and s in (13, 15):
                    j = (s - 13) // 2
                    dve.wait_ge(c_ready, UC + 14 + j + 1)
                    dve.wait_ge(s_row2, c * GB + 2 * j + 2)
                    residual(ps_c[j], gc, j, WS * WS)
                if prep == "c" and s == 8:
                    prep_p(c, la)
                if prep == "c" and s == PREP_C_SLOT + 1:
                    prep_1(c, la)
                if prep == "c" and s == PREP_C_SLOT + 2:
                    prep_b(c, la)
            if prep == "c":
                prep_2(c, la)

        def residual(bank, g, j, scale):
            dst = x[:, bass.ds(g * GB + 2 * j, 2), :]
            V.scalar_tensor_tensor(out=dst, in0=bank[:, :].rearrange("p (b d) -> p b d", b=2), scalar=1.0 / scale, in1=dst,
                                   op0=ALU.mult, op1=ALU.add).then_inc(c_free, 1)

        def position(g):
            dve.wait_ge(s_emb[g], GB * 16)
            V.tensor_tensor(group(g), group(g), pos[:, :].unsqueeze(1).broadcast_to([P, GB, D]), ALU.add).then_inc(s_pos, 1)
            dve.wait_ge(s_pos, g + 1)

        V.memset(ks[:], 0.0).then_inc(s_zero, 1)
        V.memset(vs[:], 1.0).then_inc(s_zero, 1)
        dve.wait_ge(s_zero, 2)
        dve.wait_ge(s_cst, 32)
        V.tensor_copy(ident16[:], cst[:, 0, :]).then_inc(s_init, 1)
        V.tensor_copy(mask_ts[:], cst[:, 1, :]).then_inc(s_init, 1)
        V.tensor_copy(mask_st[:], cst[:, 2, :]).then_inc(s_init, 1)

        walk(dve, step)

        def token_lo(count, j):
            dve.wait_ge(c_hi, count)
            V.tensor_tensor(c_xt[:, j, 1, :], rows_ps[j], c_xt[:, j, 0, :], ALU.subtract).then_inc(c_free, 1)

        for j in range(KD):
            token_lo(H_E + j + 1, j)
        dve.wait_ge(m_idx, 16)
        V.tensor_copy(e_idxf[:], e_idx[:].rearrange("p e c -> p (e c)")).then_inc(m_idxf, 1)
        for i in range(MB * T // HOT):
            V.tensor_scalar(num16[:, i, :], cst[:, 5:7, :].rearrange("p a n -> p (a n)"), float(i * HOT), None, ALU.add).then_inc(s_num, 1)
        dve.wait_ge(m_cw, NCH * 16)
        dve.wait_ge(m_l2, 1)

        def one_hot(i):
            for ch in range(NCH):
                V.tensor_scalar(hot(i, ch), num16[:, i, :], e_idxf[:, ch:ch + 1], None, ALU.is_equal).then_inc(m_hot, 1)

        def expert(e, par, k_, last):
            for j in range(KF):
                dve.wait_ge(c_hi, he(e) + j + 1)
                V.tensor_tensor(hid[:, 1, j, :], act32[:, j % 2, :], hid[:, 0, j, :], ALU.subtract).then_inc(m_lo, 1)
            if not last:
                for j in range(KD):
                    token_lo(he(e) + KF + j + 1, j)
                split_lows(e + 1, 1 - par)
            else:
                dve.wait_ge(m_idxf, 1)
                dve.wait_ge(s_num, MB * T // HOT)
                one_hot(0)
            dve.wait_ge(m_w, e * 4)
            for j in range(2):
                use = ue(e) + KF + j + (1 if last else 3)
                free = fe(e) + j + (1 if last else 3)
                dve.wait_ge(c_ready, use)
                if j == 0:
                    dve.wait_ge(m_row[par], k_ * 16 + 16)
                for i in range(2):
                    done = V.scalar_tensor_tensor(out=e_tmp[:, 2 * j + i, :], in0=out_ps[j][:, D * i:D * i + D], scalar=1.0 / WS,
                                                  in1=e_row[par][:], op0=ALU.mult, op1=ALU.add)
                    done.then_inc(m_o if i == 0 else c_free, 1)
                for i in range(2):
                    if i == 0:
                        dve.wait_ge(m_o, e * 2 + j + 1)
                    else:
                        dve.wait_ge(c_free, free)
                    ch = e * 4 + (2 * j + i)
                    w = e_cw[:, bass.ds(ch, 1), bass.ds(e, 1)].rearrange("p a b -> p (a b)")
                    dst = wout[:, bass.ds(ch, 1), :, :].rearrange("p c h n -> p (c h) n")
                    V.tensor_scalar(dst[:, 0, :], e_tmp[:, 2 * j + i, :], w, None, ALU.mult).then_inc(m_wh, 1)
                    dve.wait_ge(m_wh, e * 4 + 2 * j + i + 1)
                    split_lo(dst[:, 1, :], e_tmp[:, 2 * j + i, :], w, dst[:, 0, :]).then_inc(m_w, 1)

        experts(dve, expert)

        for i in range(MB * T // HOT):
            if i + 1 < MB * T // HOT:
                if i == 0:
                    dve.wait_ge(c_ready, U_END)
                else:
                    dve.wait_ge(c_ready, U_END + i * (HOT // T))
                one_hot(i + 1)
            for b in range(i * (HOT // T), (i + 1) * (HOT // T)):
                dve.wait_ge(c_ready, U_END + b + 1)
                V.tensor_tensor(x[:, b, :], ps_c[b % 2][:, 0:D], x[:, b, :], ALU.add).then_inc(m_fin, 1)

    ctx.close()


_INS = ['x', 'L0_tok_tok_emb', 'L0_tok_pos_emb', 'L0_tok_wq', 'L0_tok_wk', 'L0_tok_wv', 'L0_tok_w_proj', 'L0_tok_b_proj',
        'L0_tok_ln1_w', 'L0_tok_ln1_b', 'L0_tok_ln2_w', 'L0_tok_ln2_b', 'L0_tok_w1', 'L0_tok_b1', 'L0_tok_w2', 'L0_tok_b2',
        'L0_attn_qw', 'L0_attn_kw', 'L0_attn_vw', 'L0_attn_ow', 'L0_ffn_combine_weights', 'L0_ffn_top_idx',
        'L0_ffn_W1', 'L0_ffn_b1', 'L0_ffn_W2', 'L0_ffn_b2']


def _constants():
    import numpy as np

    c = np.zeros((7, P, P), np.float32)
    i = np.arange(P)
    c[0] = np.eye(P)
    c[1] = np.where(i[None, :] > i[:, None], np.float32(-2.0 ** 80), 0)
    c[2] = np.where(i[:, None] > i[None, :], np.float32(-2.0 ** 80), 0)
    inv = (np.float32(1.0) / np.float32(10000.0) ** (np.arange(0, HD, 2, dtype=np.float32) / np.float32(HD))).astype(np.float32)
    freq = (i.astype(np.float32)[:, None] * inv[None, :]).astype(np.float32)
    by_row = freq[:, (i % HD) // 2].T
    c[3] = np.cos(by_row) * np.float32(WS)
    c[4] = np.sin(by_row) * np.float32(WS)
    c[5], c[6] = i[None, :], i[None, :] + P
    return c


def kernel(**inputs):
    import numpy as _np
    import concourse.bacc as _bacc
    from concourse import mybir as _mybir
    from concourse.bass_utils import run_bass_kernel_spmd as _run

    nc = _bacc.Bacc("TRN2", target_bir_lowering=False, num_devices=1)
    arrays, args = {}, []
    for name in _INS + ["consts"]:
        a = _constants() if name == "consts" else _np.ascontiguousarray(inputs[name])
        arrays[f"in_{name}_dram"] = a
        args.append(nc.dram_tensor(f"in_{name}_dram", a.shape, _mybir.dt.from_np(a.dtype), kind="ExternalInput").ap())
    args.append(nc.dram_tensor("out_0_dram", (NB, T, D), _mybir.dt.from_np(_np.dtype("float32")), kind="ExternalOutput").ap())
    tower_model_kernel(nc, *args)
    r = _run(nc, [arrays], core_ids=[0])
    return r.results[0]["out_0_dram"]
```

```python
from contextlib import ExitStack

import concourse.bass as bass
from concourse import mybir

F32 = mybir.dt.float32
F16 = mybir.dt.float16
BF16 = mybir.dt.bfloat16
I32 = mybir.dt.int32
U32 = mybir.dt.uint32
ALU = mybir.AluOpType
ACT = mybir.ActivationFunctionType
AX_X = mybir.AxisListType.X

P = 128
NB, T = 32, 128
D = 256
KD = D // P
H, HD = 16, 16
PAIRS = H // 2
L = 4
FF = 4 * D
KF = FF // P
GB = 4
NG = NB // GB
N5 = GB * T
TOWER = L * NG
INST = TOWER + NG
UNITS = GB * H // 4
SLOTS = UNITS
HV = 2 * HD + 1
E, CAP = 8, 512
MB = 16
NCH = E * CAP // P
HOT = 256
EPS = 1e-5
WS = 16.0
LOADS_A, LOADS_C = 7 * 16, 5 * 16
STACK_Q, STACK_K = 4 * 16, 8 * 16
SPLITS = 5
SCORE = 1.0 / (WS * WS * 16.0)

A_TOWER = [("t", 0, 3), ("t", 1, 4), ("q", 0, 5), ("q", 1, 6), ("k", 0, 7), ("k", 1, 8), ("v", 0, 0), ("v", 1, 1)]
A_ROTARY = [("t", 0, 2), ("t", 1, 3), ("q", 0, 4), ("qs", 0, 4), ("q", 1, 5), ("qs", 1, 6),
            ("k", 0, 7), ("ks", 0, 8), ("k", 1, 9), ("ks", 1, 10), ("v", 0, 0), ("v", 1, 1)]
C_TOWER = [("ct", 0, 2), ("ct", 1, 3), ("pj", 0, 4), ("pj", 1, 5), ("t", 0, 7), ("t", 1, 7)] + \
          [("f1", j, 8 + j // 2) for j in range(KF)] + [("f2", 0, 12), ("f2", 1, 14)]
C_ROTARY = C_TOWER[:4]
LN_C_SLOT = 5
LAG = 2
LAST_CONTEXTS = LAG - 1
AHEAD = 2
X_SLOT = 6
PREP_A_SLOT = 2
PREP_C_SLOT = 11
ROW1_SLOTS = (1, 2, 3, 4)
ROW2_SLOTS = (8, 9, 11, 12)


def tower_model_kernel(nc, ids, tok_emb, pos_emb, wq, wk, wv, w_proj, b_proj, ln1_w, ln1_b, ln2_w, ln2_b,
                       w1, b1, w2, b2, qw, kw, vw, ow, combine, top_idx, e_w1, e_b1, e_w2, e_b2,
                       consts, out):
    ctx = ExitStack()

    def sb(name, shape, dt):
        return ctx.enter_context(nc.sbuf_tensor(name, shape, dt))

    def psum(name, shape):
        return ctx.enter_context(nc.psum_tensor(name, shape, F32))

    def sem(name):
        return ctx.enter_context(nc.semaphore(name))

    x = sb("x", [P, NB, D], F32)
    cst = sb("cst", [P, 6, P], F32)
    ident16 = sb("ident16", [P, P], BF16)
    mask_ts = sb("mask_ts", [P, P], BF16)
    ident, cos16, sin16 = cst[:, 0, :], cst[:, 2, :], cst[:, 3, :]
    half = sb("half", [P, GB], F32)
    idx = sb("idx", [P, NB], I32)
    pos = sb("pos", [P, D], F32)

    raw_a = sb("raw_a", [P, 3, KD, D], F32)
    raw_p = sb("raw_p", [P, KD, D], F32)
    raw_f = sb("raw_f", [P, KD * FF], F32)
    raw_1 = raw_f[:, :].rearrange("p (k n) -> p k n", k=KD)
    raw_2 = raw_f[:, :].rearrange("p (k n) -> p k n", k=KF)
    raw_v = sb("raw_v", [P, 4, KD], F32)
    raw_b1 = sb("raw_b1", [P, KF], F32)
    raw_rows = sb("raw_rows", [P, 2, D], F32)
    wa = sb("wa", [P, 3, 2, KD, D], F16)
    wp = sb("wp", [P, 2, KD, D], F16)
    w1s = sb("w1s", [P, 2, KD, FF], F16)
    w2s = sb("w2s", [P, 2, KF, D], F16)
    bqk = sb("bqk", [P, 4], F32)
    bv = sb("bv", [P, KD], F32)
    b1c = sb("b1c", [P, KF], F32)
    row1 = sb("row1", [P, D], F32)
    row2 = sb("row2", [P, D], F32)
    fw = raw_a[:, :, :, :].bitcast(F16).rearrange("p m k n -> p (m k n)").rearrange("p (m k n) -> p m k n", m=6, k=KD)
    lnw16 = sb("lnw16", [P, 2, KD], F32)

    a_st = sb("a_st", [P, GB, 6], F32)
    a_mv = sb("a_mv", [P, GB, 2], F32)
    a_ve = sb("a_ve", [P, GB], F32)
    a_rs = sb("a_rs", [P, GB], F32)
    c_st = sb("c_st", [P, GB, 6], F32)
    c_mv = sb("c_mv", [P, GB, 2], F32)
    c_ve = sb("c_ve", [P, GB], F32)
    c_rs = sb("c_rs", [P, GB], F32)
    a_x = sb("a_x", [P, GB, D], F32)
    c_x = sb("c_x", [P, GB, D], F32)
    a_xt = sb("a_xt", [P, KD, 2, N5], F16)
    c_xt = sb("c_xt", [P, KD, 2, N5], F16)
    qk_hl = sb("qk_hl", [P, 2, 2, 2, N5], F16)
    rot_a, rot_b, rot = (raw_f[:, i * N5:(i + 1) * N5] for i in range(3))
    qs = sb("qs", [P, 2, PAIRS, N5], F16)
    ks = sb("ks", [P, 2, PAIRS, 2, N5], F16)
    vs = sb("vs", [P, 2, GB, H, HV], F16)
    negm = sb("negm", [P, 4, 4], F32)
    shift = sb("shift", [P, 2, 4, T], BF16)
    pr = sb("pr", [P, 4, 4, T], F32)
    pr_lo = sb("pr_lo", [P, 4, 4, T], F16)
    rec = sb("rec", [P, 8], F32)
    o_hl = sb("o_hl", [P, 8, 2, HD], F32)
    cx = sb("cx", [P, GB, D], F32)
    cxt = sb("cxt", [P, KD, 2, N5], F16)
    act32 = sb("act32", [P, 2, N5], F32)
    hid = sb("hid", [P, 2, KF, N5], F16)

    e_w1s = [w1s[:, :, :, :], qs[:, 0, :, :].rearrange("p a n -> p (a n)").rearrange("p (h k n) -> p h k n", h=2, k=KD)]
    e_w2s = [w2s[:, :, :, :], qs[:, 1, :, :].rearrange("p a n -> p (a n)").rearrange("p (h k n) -> p h k n", h=2, k=KF)]
    e_raw2 = pr[:, :, :, :].rearrange("p u h t -> p (u h t)").rearrange("p (k n) -> p k n", k=KF)
    wout = ks[:, :, :, :, :].rearrange("p a b e n -> p (a b e n)").rearrange("p (c h n) -> p c h n", c=NCH, h=2)
    e_raw2_0 = hid[:, 0, :, :].bitcast(F32).rearrange("p k n -> p (k n)").rearrange("p (k n) -> p k n", k=KF)
    e_x = [c_x, a_x]
    e_row = [row1, row2]
    e_b1c = sb("e_b1c", [P, E, KF], F32)
    e_idx = sb("e_idx", [P, E, CAP // P], I32)
    e_idxf = sb("e_idxf", [P, NCH], F32)
    e_cw = sb("e_cw", [P, NCH, E], F32)
    num16 = a_xt[:, :, :, :].rearrange("p k a n -> p (k a n)").rearrange("p (i n) -> p i n", n=HOT)
    e_tmp = cx

    ps_s = [psum(f"ps_s{i}", [P, 4, T]) for i in range(2)]
    ps_st = [psum(f"ps_st{i}", [P, 4, T]) for i in range(2)]
    ps_o = psum("ps_o", [P, 512])
    ps_a = psum("ps_a", [P, 512])
    ps_c = [psum(f"ps_c{i}", [P, 512]) for i in range(2)]
    rows_ps = [ps_s[i][:, :, :].rearrange("p h t -> p (h t)") for i in range(2)]
    out_ps = [ps_st[i][:, :, :].rearrange("p h t -> p (h t)") for i in range(2)]
    o_ps = ps_o[:, 0:8 * HV].rearrange("p (h v) -> p h v", v=HV)

    stack_d = nc.dram_tensor("stack_d", (2, 2, 2, P, 2, N5), F16).ap()
    tokens_d = nc.dram_tensor("tokens_d", (MB * T, D), F32).ap()

    s_cst = sem("s_cst")
    s_ids = sem("s_ids")
    s_emb = [sem(f"s_emb{g}") for g in range(NG)]
    s_init = sem("s_init")
    s_zero = sem("s_zero")
    s_half = sem("s_half")
    s_pos = sem("s_pos")
    s_lda = sem("s_lda")
    s_ldc = sem("s_ldc")
    s_ld2 = sem("s_ld2")
    s_fw = sem("s_fw")
    s_fws = sem("s_fws")
    s_wa = sem("s_wa")
    s_wp = sem("s_wp")
    s_w1 = sem("s_w1")
    s_w2 = sem("s_w2")
    s_b1 = sem("s_b1")
    s_num = sem("s_num")
    s_wh = sem("s_wh")
    s_w2h = sem("s_w2h")
    s_ln16 = sem("s_ln16")
    s_bias_pe = sem("s_bias_pe")
    s_bias_a = sem("s_bias_a")
    s_bias_c = sem("s_bias_c")
    a_stat, a_mvs, a_ves, a_rstd, a_xn = sem("a_stat"), sem("a_mvs"), sem("a_ves"), sem("a_rstd"), sem("a_xn")
    a_ready, a_hi, a_free = sem("a_ready"), sem("a_hi"), sem("a_free")
    r_sum, r_hi, r_lo = sem("r_sum"), sem("r_hi"), sem("r_lo")
    st_out = sem("st_out")
    st_q, st_k = sem("st_q"), sem("st_k")
    shifted = sem("shifted")
    s_ready, mx, st_ready, p_exp, p_lo, pv = sem("s_ready"), sem("mx"), sem("st_ready"), sem("p_exp"), sem("p_lo"), sem("pv")
    o_rec, o_free, o_ctx = sem("o_rec"), sem("o_free"), sem("o_ctx")
    c_stat, c_mvs, c_ves, c_rstd, c_xn = sem("c_stat"), sem("c_mvs"), sem("c_ves"), sem("c_rstd"), sem("c_xn")
    c_ready, c_hi, c_act, c_lo, c_free = sem("c_ready"), sem("c_hi"), sem("c_act"), sem("c_lo"), sem("c_free")
    s_row1, s_row2 = sem("s_row1"), sem("s_row2")
    m_out, m_idx, m_idxf = sem("m_out"), sem("m_idx"), sem("m_idxf")
    m_x = [sem(f"m_x{i}") for i in range(2)]
    m_cw, m_ld1, m_ld2, m_b1 = sem("m_cw"), sem("m_ld1"), sem("m_ld2"), sem("m_b1")
    m_row = [sem(f"m_row{i}") for i in range(2)]
    m_h1, m_l1, m_h2, m_l2 = sem("m_h1"), sem("m_l1"), sem("m_h2"), sem("m_l2")
    m_g, m_lo, m_o, m_wh, m_w = sem("m_g"), sem("m_lo"), sem("m_o"), sem("m_wh"), sem("m_w")
    m_hot, m_fin, s_out = sem("m_hot"), sem("m_fin"), sem("s_out")

    def ua(n, rotary):
        return n * 12 - 4 * TOWER if rotary else n * 8

    def ha(n, rotary):
        return n * 4 + 4 * TOWER if rotary else n * 8

    def uc(n, rotary):
        return n * 4 + 12 * TOWER if rotary else n * 16

    def hc(n, rotary):
        return n * 2 + 10 * TOWER if rotary else n * 12

    def wait(eng, s, value):
        if not isinstance(value, int) or value > 0:
            eng.wait_ge(s, value)

    def walk(eng, step, at_layer=None, before_rotary=None):
        step(0, 0, 0, 0, 0, 0, "t", None, None, "a")
        step(1, 1, 1, 0, 0, 0, "t", "t", None, "c")
        with eng.Fori(0, L - 1) as l:
            if at_layer:
                at_layer(l)
            with eng.Fori(0, (NG - 2) // 2) as k:
                step(l * NG + k * 2 + 2, 0, k * 2 + 2, k * 2, l, l, "t", "t", "t", None)
                step(l * NG + k * 2 + 3, 1, k * 2 + 3, k * 2 + 1, l, l, "t", "t", "t", None)
            step(l * NG + NG, 0, 0, NG - 2, l + 1, l, "t", "t", "t", "a")
            step(l * NG + NG + 1, 1, 1, NG - 1, l + 1, l, "t", "t", "t", "c")
        if before_rotary:
            before_rotary()
        with eng.Fori(0, (NG - 2) // 2) as k:
            step(k * 2 + (TOWER - NG + 2), 0, k * 2 + 2, k * 2, L - 1, L - 1, "t", "t", "t", None)
            step(k * 2 + (TOWER - NG + 3), 1, k * 2 + 3, k * 2 + 1, L - 1, L - 1, "t", "t", "t", None)
        step(TOWER, 0, 0, NG - 2, L, L - 1, "r", "t", "t", "r")
        step(TOWER + 1, 1, 1, NG - 1, L, L - 1, "r", "r", "t", None)
        with eng.Fori(0, MB // GB // 2) as k:
            step(k * 2 + (TOWER + 2), 0, k * 2 + 2, k * 2, L, L, "r", "r", "e", None)
            step(k * 2 + (TOWER + 3), 1, k * 2 + 3, k * 2 + 1, L, L, "r", "r", "e", None)
        step(INST - 2, 0, NG - 2, NG - 4, L, L, "r", "r", "r", "w")
        step(INST - 1, 1, NG - 1, NG - 3, L, L, "r", "r", "r", "w")
        step(INST, 0, 0, NG - 2, L, L, None, "r", "r", "x")
        step(INST + 1, 1, 0, NG - 1, L, L, None, None, "r", None)

    def uses(table, slot):
        return [(k, kind, j) for k, (kind, j, at) in enumerate(table) if at == slot]

    def v_uses(B, slot):
        return [u for u in uses({"t": A_TOWER, "r": A_ROTARY, None: []}[B], slot) if u[1] == "v"]

    def a_uses(A, slot):
        return [u for u in uses({"t": A_TOWER, "r": A_ROTARY, None: []}[A], slot) if u[1] != "v"]

    def c_uses(C, slot):
        return uses({"t": C_TOWER, "r": C_ROTARY, "e": C_ROTARY, None: []}[C], slot)

    def first_units(A, slot):
        if A == "r":
            return range(AHEAD) if slot == SLOTS - 1 else ()
        return (slot - (SLOTS - AHEAD),) if A else ()

    def group(g):
        return x[:, bass.ds(g * GB, GB), :]

    def hi_view(ap):
        return ap.bitcast(BF16).rearrange("p (n two) -> p n two", two=2)[:, :, 1]

    PASSES = ((0, 0), (1, 0), (0, 1))

    U_E, H_E = uc(INST, True), hc(INST, True)
    U_END = U_E + E * (KF + 4)

    def ue(e):
        return e * (KF + 4) + (U_E + 2)

    def he(e):
        return e * (KF + 2) + (H_E + 2)

    def fe(e):
        return e * 4 + (U_E + 2)

    def experts(eng, expert):
        with eng.Fori(0, E // 2 - 1) as k:
            expert(k * 2, 0, k, False)
            expert(k * 2 + 1, 1, k, False)
        expert(E - 2, 0, E // 2 - 1, False)
        expert(E - 1, 1, E // 2 - 1, True)

    def hot(i, ch):
        if i % 2:
            return qs[:, :, :, :].rearrange("p a b n -> p (a b n)").rearrange("p (c n) -> p c n", c=NCH)[:, ch, :]
        w = (w1s, w2s)[ch // (NCH // 2)]
        return w[:, :, :, :].rearrange("p a k n -> p (a k n)").rearrange("p (c n) -> p c n", c=NCH // 2)[:, ch % (NCH // 2), :]

    block = ctx.enter_context(nc.Block())

    @block.sync
    def _(sp):
        def load_layer(l):
            one = bass.ds(l, 1)
            for i, v in enumerate((ln1_w, ln1_b, ln2_w, ln2_b)):
                sp.dma_start(raw_v[:, i, :], v[one, :].rearrange("l (k p) -> p (l k)", p=P),
                             allow_slow_non_contiguous=True).then_inc(s_lda, 16)
            for m, w in enumerate((wq, wk, wv)):
                sp.dma_start(raw_a[:, m, :, :], w[one, :, :].rearrange("l (k p) n -> p (l k) n", p=P)).then_inc(s_lda, 16)
            sp.dma_start(raw_p[:], w_proj[one, :, :].rearrange("l (k p) n -> p (l k) n", p=P)).then_inc(s_ldc, 16)
            sp.dma_start(raw_1, w1[one, :, :].rearrange("l (k p) n -> p (l k) n", p=P)).then_inc(s_ldc, 16)
            sp.dma_start(raw_b1[:], b1[one, :].rearrange("l (k p) -> p (l k)", p=P),
                         allow_slow_non_contiguous=True).then_inc(s_ldc, 16)
            sp.dma_start(raw_rows[:, 0, :], b_proj[one, :].broadcast_to([P, D])).then_inc(s_ldc, 16)
            sp.dma_start(raw_rows[:, 1, :], b2[one, :].broadcast_to([P, D])).then_inc(s_ldc, 16)

        sp.dma_start(idx[:], ids.rearrange("b t -> t b"), allow_slow_non_contiguous=True).then_inc(s_ids, 16)
        sp.dma_start(cst[:], consts.rearrange("c p n -> p c n")).then_inc(s_cst, 16)
        sp.dma_start(pos[:], pos_emb[0:T, :]).then_inc(s_cst, 16)
        load_layer(0)

        def step(n, par, ga, gc, la, lc, A, B, C, prep):
            for which in range(2):
                if A is None:
                    continue
                if A == "t":
                    sp.wait_ge(a_free, ua(n, False) + 4 + 2 * which)
                    sp.nop(nofuse=True)
                else:
                    sp.wait_ge(r_lo, (n - TOWER) * 4 + 2 + 2 * which)
                    sp.nop(nofuse=True)
                wait(sp, st_q, n * STACK_Q)
                sp.nop(nofuse=True)
                wait(sp, st_k, n * STACK_K)
                sp.nop(nofuse=True)
                sp.dma_start(stack_d[par, which].rearrange("j p h n -> p j h n"), qk_hl[:, which]).then_inc(st_out, 16)
                sp.wait_ge(st_out, n * 32 + 16 * (which + 1))
                sp.nop(nofuse=True)
                wait(sp, st_ready, (n - 1) * UNITS)
                sp.nop(nofuse=True)
                for c in range(4):
                    if which == 0:
                        rows = stack_d[par, 0, :, :, c // 2, :].rearrange("j (i p) n -> p (j i) n", p=32)
                        sp.dma_start(qs[32 * c:32 * c + 32, par, :, :], rows).then_inc(st_q, 16)
                    else:
                        for e in range(2):
                            r = 32 * c + HD * e
                            rows = stack_d[par, 1, :, :, c % 2, :].rearrange("j (i e p) n -> e p (j i) n", e=2, p=HD)[e]
                            sp.dma_start(ks[r:r + HD, par, :, e, :], rows).then_inc(st_k, 16)
                if which == 0 and C == "e":
                    sp.wait_ge(c_xn, (n - 2) * GB + GB)
                    sp.nop(nofuse=True)
                    sp.dma_start(tokens_d.rearrange("(b t) d -> t b d", t=T)[:, bass.ds(gc * GB, GB), :], c_x[:]).then_inc(m_out, 16)
            if prep == "c":
                sp.wait_ge(s_w1, la + 1)
                sp.nop(nofuse=True)
                sp.wait_ge(s_bias_pe, la * 2 + 2)
                sp.nop(nofuse=True)
                sp.dma_start(raw_2, w2[bass.ds(la, 1), :, :].rearrange("l (k p) n -> p (l k) n", p=P)).then_inc(s_ld2, 16)
            if prep == "x":
                sp.wait_ge(r_lo, NG * 4)
                sp.nop(nofuse=True)
                sp.dma_start(raw_1, e_w1[0].rearrange("(k p) n -> p k n", p=P)).then_inc(m_ld1, 16)
                sp.dma_start(e_raw2_0, e_w2[0].rearrange("(k p) n -> p k n", p=P)).then_inc(m_ld2, 16)
                for e in range(2):
                    sp.dma_start(e_row[e][:], e_b2[e:e + 1, :].broadcast_to([P, D])).then_inc(m_row[e], 16)

        def layer_done(l):
            sp.wait_ge(s_w2, l + 1)
            sp.nop(nofuse=True)
            sp.wait_ge(s_bias_c, l * 3 + 3)
            sp.nop(nofuse=True)

        def next_layer(l):
            layer_done(l)
            load_layer(l + 1)

        def rotary_weights():
            layer_done(L - 1)
            for m, w in enumerate((qw, kw, vw, ow)):
                sp.dma_start(fw[:, m, :, :], w.rearrange("(k p) n -> p k n", p=P)).then_inc(s_fw, 16)
            sp.dma_start(e_idx[:], top_idx.rearrange("(c p) e -> p e c", p=P), allow_slow_non_contiguous=True).then_inc(m_idx, 16)
            sp.dma_start(e_b1c[:], e_b1.rearrange("e (k p) -> p e k", p=P), allow_slow_non_contiguous=True).then_inc(m_b1, 16)

        walk(sp, step, next_layer, rotary_weights)

        sp.wait_ge(m_l1, 1)
        sp.nop(nofuse=True)
        sp.dma_start(raw_1, e_w1[1].rearrange("(k p) n -> p k n", p=P)).then_inc(m_ld1, 16)
        sp.wait_ge(pv, INST * UNITS)
        sp.nop(nofuse=True)
        sp.wait_ge(m_l2, 1)
        sp.nop(nofuse=True)
        sp.dma_start(e_raw2, e_w2[1].rearrange("(k p) n -> p k n", p=P)).then_inc(m_ld2, 16)
        sp.wait_ge(c_free, U_E)
        sp.nop(nofuse=True)
        for g in range(MB // GB, NG):
            sp.dma_start(out[g * GB:(g + 1) * GB].rearrange("b t d -> t b d"), group(g)).then_inc(s_out, 16)

        def expert(e, par, k):
            one = bass.ds(e, 1)
            sp.wait_ge(m_l1, e)
            sp.nop(nofuse=True)
            sp.dma_start(raw_1, e_w1[one, :, :].rearrange("l (k p) n -> p (l k) n", p=P)).then_inc(m_ld1, 16)
            sp.wait_ge(m_l2, e)
            sp.nop(nofuse=True)
            sp.dma_start(e_raw2, e_w2[one, :, :].rearrange("l (k p) n -> p (l k) n", p=P)).then_inc(m_ld2, 16)
            sp.wait_ge(m_w, e * 4 - 4)
            sp.nop(nofuse=True)
            sp.dma_start(e_row[par][:], e_b2[one, :].broadcast_to([P, D])).then_inc(m_row[par], 16)

        with sp.Fori(1, E // 2) as k:
            expert(k * 2, 0, k)
            expert(k * 2 + 1, 1, k)
        for g in range(MB // GB):
            sp.wait_ge(m_fin, (g + 1) * GB)
            sp.nop(nofuse=True)
            sp.dma_start(out[g * GB:(g + 1) * GB].rearrange("b t d -> t b d"), group(g)).then_inc(s_out, 16)
        sp.wait_ge(s_out, NG * 16)
        sp.nop(nofuse=True)

    @block.gpsimd
    def _(pool):
        pool.wait_ge(s_ids, 16)
        def embed(b):
            pool.indirect_dma_start(x[:, b, :], None, tok_emb, bass.IndirectOffsetOnAxis(ap=idx[:, b:b + 1].bitcast(U32), axis=0),
                                    ).then_inc(s_emb[b // GB], 16)

        for b in range(2 * GB):
            embed(b)
        nc.gpsimd.memset(half[:], -0.5).then_inc(s_half, 1)
        pool.wait_ge(s_half, 1)

        def inv_std(mv, ve, rs, s_mv, s_ve, s_rs, n):
            pool.wait_ge(s_mv, n * GB + GB)
            pool.nop(nofuse=True)
            nc.gpsimd.tensor_scalar(ve[:], mv[:, :, 1], EPS, 1.0, ALU.add, ALU.mult).then_inc(s_ve, 1)
            pool.wait_ge(s_ve, n + 1)
            nc.gpsimd.tensor_tensor(rs[:], ve[:], half[:], ALU.pow).then_inc(s_rs, 1)

        def add_contexts(b, q):
            pool.wait_ge(o_free, b * 8 + q + 1)
            dst = cx[:, q // 2, P * (q % 2):P * (q % 2) + P].rearrange("p (h d) -> p h d", d=HD)
            nc.gpsimd.tensor_tensor(dst, o_hl[:, :, 0, :], o_hl[:, :, 1, :], ALU.add).then_inc(o_ctx, 1)

        def add_row(row, g, i, done):
            seq = x[:, bass.ds(g * GB + i, 1), :].rearrange("p a d -> p (a d)")
            nc.gpsimd.tensor_tensor(seq, seq, row[:, :], ALU.add).then_inc(done, 1)

        def expert_rows(e, ch):
            pool.indirect_dma_start(e_x[e % 2][:, ch, :], None, tokens_d,
                                    bass.IndirectOffsetOnAxis(ap=e_idx[:, e, ch:ch + 1].bitcast(U32), axis=0)
                                    ).then_inc(m_x[e % 2], 16)

        def step(n, par, ga, gc, la, lc, A, B, C, prep):
            b, c = n - 1, n - 2
            for s in range(SLOTS):
                if B:
                    pool.wait_ge(p_exp, b * UNITS + s + 1)
                    wait(pool, pv, b * UNITS + s - 3)
                    flat = pr[:, s % 4].rearrange("p h t -> p (h t)")
                    nc.gpsimd.tensor_tensor(pr_lo[:, s % 4].rearrange("p h t -> p (h t)"), flat, hi_view(flat),
                                            ALU.subtract).then_inc(p_lo, 1)
                if s == LAST_CONTEXTS and C:
                    add_contexts(c, 7)
                if s == 0 and A:
                    inv_std(a_mv, a_ve, a_rs, a_mvs, a_ves, a_rstd, n)
                if isinstance(n, int) and n == 0 and 2 * (s + 1) <= NB - 2 * GB:
                    embed(2 * GB + 2 * s)
                    embed(2 * GB + 2 * s + 1)
                if B and s > LAG and (s - LAG) % 2:
                    if C and s == LAG + 1:
                        pool.wait_ge(c_ready, uc(c, C != "t") + 2)
                    add_contexts(b, (s - LAG) // 2)
                if C == "t" and s in ROW1_SLOTS:
                    if s == ROW1_SLOTS[0]:
                        pool.wait_ge(s_bias_c, lc * 3 + 3)
                        pool.nop(nofuse=True)
                    for i in range(GB):
                        if ROW1_SLOTS[i] == s:
                            add_row(row1, gc, i, s_row1)
                if C in ("t", "e") and s == LN_C_SLOT:
                    inv_std(c_mv, c_ve, c_rs, c_mvs, c_ves, c_rstd, c)
                if C == "t" and s in ROW2_SLOTS:
                    i = ROW2_SLOTS.index(s)
                    pool.wait_ge(c_xn, c * GB + i + 1)
                    pool.nop(nofuse=True)
                    add_row(row2, gc, i, s_row2)

                if prep == "w":
                    if s == 0:
                        pool.wait_ge(m_idx, 16)
                    ch = (n - (INST - 2)) * SLOTS + s
                    pool.indirect_dma_start(e_cw[:, ch, :], None, combine,
                                            bass.IndirectOffsetOnAxis(ap=e_idx[:, ch // 4, ch % 4:ch % 4 + 1].bitcast(U32), axis=0)
                                            ).then_inc(m_cw, 16)
                if prep == "x" and s < 2 * (CAP // P):
                    if s == 0:
                        pool.wait_ge(m_out, 16 * (MB // GB))
                        pool.wait_ge(a_ready, ua(INST - 1, True) + 2)
                    expert_rows(s // (CAP // P), s % (CAP // P))

        walk(pool, step)

        for e in range(2, E):
            pool.wait_ge(c_ready, max(ue(e - 2) - 2, U_E + 2))
            for ch in range(CAP // P):
                expert_rows(e, ch)

    @block.scalar
    def _(act):
        def split_hi(e, par, raw2=None):
            act.wait_ge(m_ld1, e * 16 + 16)
            nc.scalar.activation(e_w1s[par][:, 0], raw_1, ACT.Copy, scale=WS).then_inc(m_h1, 1)
            act.wait_ge(m_ld2, e * 16 + 16)
            nc.scalar.activation(e_w2s[par][:, 0], e_raw2 if raw2 is None else raw2, ACT.Copy, scale=WS).then_inc(m_h2, 1)

        def step(n, par, ga, gc, la, lc, A, B, C, prep):
            b, c = n - 1, n - 2

            def shifts(i, u):
                act.wait_ge(mx, i * UNITS + u + 1)
                wait(act, st_ready, i * UNITS + u - 1)
                for h in range(4):
                    last = nc.scalar.activation(shift[:, u % 2, h, :], mask_ts[:, :], ACT.Identity, bias=negm[:, u % 4, h:h + 1])
                last.then_inc(shifted, 1)

            for s in range(SLOTS):
                for k, kind, j in v_uses(B, s):
                    act.wait_ge(a_ready, ua(b, B == "r") + k + 1)
                    src = ps_a[:, :].rearrange("p (b h d) -> p b h d", b=2, h=H)
                    nc.scalar.activation(vs[:, 1 - par, 2 * j:2 * j + 2, :, 0:HD], src, ACT.Copy,
                                         scale=1.0 if B == "t" else WS).then_inc(a_hi, 1)
                for k, kind, j in a_uses(A, s):
                    if kind == "t" or A == "t":
                        act.wait_ge(a_ready, ua(n, A == "r") + k + 1)
                    if kind == "t":
                        nc.scalar.activation(a_xt[:, j, 0, :], ps_a[:, :], ACT.Copy).then_inc(a_hi, 1)
                    elif A == "t":
                        w = int(kind == "k")
                        wait(act, st_out, n * 32)
                        if kind == "q" and j == 0:
                            act.wait_ge(s_bias_a, la * 2 + 2)
                        nc.scalar.activation(qk_hl[:, w, j, 0, :], ps_a[:, :], ACT.Identity,
                                             bias=bqk[:, 2 * w + j:2 * w + j + 1]).then_inc(a_hi, 1)
                if s < SLOTS - 1:
                    if B:
                        shifts(b, s + 1)
                elif A:
                    shifts(n, 0)
                if B:
                    act.wait_ge(st_ready, b * UNITS + s + 1)
                    wait(act, pv, b * UNITS + s - 3)
                    nc.scalar.activation(pr[:, s % 4], ps_st[s % 2][:], ACT.Exp, scale=SCORE).then_inc(p_exp, 1)
                for k, kind, j in a_uses(A, s):
                    if kind in ("qs", "ks"):
                        w = int(kind == "ks")
                        r = (n - TOWER) * 4 + 2 * w + j
                        act.wait_ge(r_sum, r + 1)
                        act.wait_ge(st_out, n * 32)
                        nc.scalar.activation(qk_hl[:, w, j, 0, :], rot, ACT.Copy).then_inc(r_hi, 1)
                for k, kind, j in c_uses(C, s):
                    if kind in ("pj", "f2"):
                        continue
                    act.wait_ge(c_ready, uc(c, C != "t") + k + 1)
                    bank = ps_c[k % 2]
                    if kind == "ct":
                        nc.scalar.activation(cxt[:, j, 0, :], bank[:, :], ACT.Copy).then_inc(c_hi, 1)
                    elif kind == "t":
                        nc.scalar.activation(c_xt[:, j, 0, :], bank[:, :], ACT.Copy).then_inc(c_hi, 1)
                    else:
                        if j == 0:
                            act.wait_ge(s_bias_c, lc * 3 + 3)
                        nc.scalar.activation(hid[:, 0, j, :], bank[:, :], ACT.Relu, bias=b1c[:, j:j + 1]).then_inc(c_hi, 1)

                if prep == "x" and s == X_SLOT:
                    split_hi(0, 0, e_raw2_0)
            if prep == "c":
                wait(act, c_ready, uc(c, False) + 16)
                act.wait_ge(s_ld2, la * 16 + 16)
                nc.scalar.activation(w2s[:, 0], raw_2, ACT.Copy, scale=WS).then_inc(s_w2h, 1)

        act.wait_ge(s_init, 2)
        walk(act, step)

        act.wait_ge(m_b1, 16)

        def token_hi(count, j):
            act.wait_ge(c_ready, count)
            nc.scalar.activation(c_xt[:, j, 0, :], rows_ps[j], ACT.Copy).then_inc(c_hi, 1)

        for j in range(KD):
            token_hi(U_E + j + 1, j)
        act.wait_ge(m_l2, 1)

        def expert(e, par, k_, last):
            for j in range(KF):
                act.wait_ge(c_ready, ue(e) + j + 1)
                act.wait_ge(m_lo, e * KF + max(j - 1, 0))
                nc.scalar.activation(act32[:, j % 2, :], ps_c[j % 2][:, :], ACT.Gelu_apprx_tanh,
                                     scale=1.0 / WS, bias=e_b1c[:, bass.ds(e, 1), j:j + 1].rearrange("p a b -> p (a b)")).then_inc(m_g, 1)
                act.wait_ge(m_g, e * KF + j + 1)
                nc.scalar.activation(hid[:, 0, j, :], act32[:, j % 2, :], ACT.Copy).then_inc(c_hi, 1)
            if not last:
                for j in range(KD):
                    token_hi(ue(e) + KF + j + 1, j)
                split_hi(e + 1, 1 - par)

        experts(act, expert)

    @block.tensor
    def _(pe):
        mm = nc.tensor.matmul

        def step(n, par, ga, gc, la, lc, A, B, C, prep):
            b, c, pb = n - 1, n - 2, 1 - par
            UA, UC = ua(n, A == "r"), uc(c, C != "t")

            def tok(bb):
                return slice(T * bb, T * bb + T)

            def scores(i, pi, u):
                bb, quad = u // 4, u % 4
                dst = ps_s[u % 2]
                if u == 0:
                    pe.wait_ge(st_q, i * STACK_Q + STACK_Q)
                    pe.wait_ge(st_k, i * STACK_K + STACK_K)
                wait(pe, mx, i * UNITS + u - 1)
                mm(dst[:], ident16[:], mask_ts[:, :].unsqueeze(1).broadcast_to([P, 4, T]), start=True, stop=False)
                for z in range(2):
                    p = 2 * quad + z
                    last = mm(dst[:, 2 * z:2 * z + 2, :], qs[:, pi, p, tok(bb)], ks[:, pi, p, :, tok(bb)], start=False, stop=z == 1)
                last.then_inc(s_ready, 1)

            def scores_t(u):
                bb, quad = u // 4, u % 4
                dst = ps_st[u % 2]
                pe.wait_ge(shifted, b * UNITS + u + 1)
                wait(pe, p_exp, b * UNITS + u - 1)
                for h in range(4):
                    p = 2 * quad + h // 2
                    mm(dst[:, h, :], shift[:, u % 2, h, :], ident16[:], start=True, stop=False)
                    last = mm(dst[:, h, :], ks[:, pb, p, h % 2, tok(bb)], qs[:, pb, p, tok(bb)], start=False, stop=True)
                last.then_inc(st_ready, 1)

            def times_v(i, pi, u):
                bb, quad = u // 4, u % 4
                pe.wait_ge(p_lo, i * UNITS + u + 1)
                if u in (0, UNITS // 2):
                    pe.wait_ge(a_free, ua(i, B == "r") + (len(A_ROTARY) if B == "r" else len(A_TOWER)) - int(u == 0))
                if u % 2 == 0:
                    wait(pe, o_free, i * 8 + u // 2)
                for h in range(4):
                    dst = o_ps[:, 4 * (u % 2) + h, :]
                    v = vs[:, pi, bb, 4 * quad + h, :]
                    mm(dst, hi_view(pr[:, u % 4, h, :]), v, start=True, stop=False)
                    last = mm(dst, pr_lo[:, u % 4, h, :], v, start=False, stop=True)
                last.then_inc(pv, 1)

            def values(k, kind, j):
                wait(pe, a_free, ua(b, B == "r") + k)
                if j == 0 and C == "t":
                    pe.wait_ge(s_bias_c, lc * 3 + 3)
                for i in range(2):
                    t = tok(2 * j + i)
                    terms = [(kt, hw, hx) for kt in range(KD) for hw, hx in (PASSES if B == "t" else ((0, 0), (0, 1)))]
                    for z, (kt, hw, hx) in enumerate(terms):
                        w = wa[:, 2, hw, kt, :] if B == "t" else fw[:, 2, kt, :]
                        last = mm(ps_a[:, D * i:D * i + D], a_xt[:, kt, hx, t], w, start=z == 0, stop=z == len(terms) - 1)
                last.then_inc(a_ready, 1)

            def a_use(k, kind, j):
                wait(pe, a_free, UA + k)
                if kind == "t":
                    if j == 0:
                        pe.wait_ge(a_xn, n * GB + GB)
                        if prep == "a":
                            pe.wait_ge(s_bias_a, la * 2 + 2)
                    for bb in range(GB):
                        last = nc.tensor.transpose(ps_a[:, tok(bb)], a_x[:, bb, P * j:P * j + P], ident)
                else:
                    if kind == "q" and j == 0:
                        pe.wait_ge(s_wa, la + 1) if A == "t" else pe.wait_ge(s_fws, 4)
                    terms = [(kt, hw, hx) for kt in range(KD) for hw, hx in (PASSES if A == "t" else ((0, 0), (0, 1)))]
                    m = {"q": 0, "k": 1, "qs": 4, "ks": 5}[kind]
                    for z, (kt, hw, hx) in enumerate(terms):
                        w = (wa[:, m, hw, kt, :] if A == "t" else fw[:, m, kt, :])[:, P * j:P * j + P]
                        last = mm(ps_a[:, :], w, a_xt[:, kt, hx, :], start=z == 0, stop=z == len(terms) - 1)
                last.then_inc(a_ready, 1)

            def c_use(k, kind, j):
                bank = ps_c[k % 2]
                if kind != "f2":
                    wait(pe, c_free, UC + max(k - 1, 0))
                if kind == "ct":
                    if j == 0:
                        pe.wait_ge(o_ctx, c * 8 + 8)
                    for bb in range(GB):
                        last = nc.tensor.transpose(bank[:, tok(bb)], cx[:, bb, P * j:P * j + P], ident)
                elif kind == "pj":
                    if j == 0:
                        pe.wait_ge(c_free, UC + 2)
                        if C == "t":
                            pe.wait_ge(s_wp, lc + 1)
                    for i in range(2):
                        t = tok(2 * j + i)
                        terms = [(kt, hw, hx) for kt in range(KD) for hw, hx in (PASSES if C == "t" else ((0, 0), (0, 1)))]
                        for z, (kt, hw, hx) in enumerate(terms):
                            w = wp[:, hw, kt, :] if C == "t" else fw[:, 3, kt, :]
                            last = mm(bank[:, D * i:D * i + D], cxt[:, kt, hx, t], w, start=z == 0, stop=z == len(terms) - 1)
                elif kind == "t":
                    if j == 0:
                        pe.wait_ge(c_xn, c * GB + GB)
                    for bb in range(GB):
                        last = nc.tensor.transpose(bank[:, tok(bb)], c_x[:, bb, P * j:P * j + P], ident)
                elif kind == "f1":
                    if j == 0:
                        pe.wait_ge(c_free, UC + 6)
                        pe.wait_ge(s_w1, lc + 1)
                    last = feed_1(bank, w1s, j)
                last.then_inc(c_ready, 1)

            for s in range(SLOTS):
                if prep == "a" and s == PREP_A_SLOT:
                    bias_products_a(n, la)
                if prep == "c" and s == PREP_C_SLOT:
                    bias_products_c(n, la)
                for use in v_uses(B, s):
                    values(*use)
                for use in a_uses(A, s):
                    a_use(*use)
                if B:
                    scores_t(s)
                if s < SLOTS - AHEAD:
                    if B:
                        scores(b, pb, s + AHEAD)
                else:
                    for u in first_units(A, s):
                        scores(n, par, u)
                if s < LAG:
                    if C:
                        times_v(c, par, UNITS - LAG + s)
                elif B:
                    times_v(b, pb, s - LAG)
                for use in c_uses(C, s):
                    if use[1] != "f2":
                        c_use(*use)
                if C == "t" and s >= 12:
                    j, i = (s - 12) // 2, s % 2
                    k = 14 + j
                    if s == 12:
                        pe.wait_ge(s_w2, lc + 1)
                    if i == 0:
                        pe.wait_ge(c_free, UC + k - 1)
                    last = feed_2(ps_c[k % 2], w2s, 2 * j + i, i, (c_lo, c * KF) if s == 12 else None)
                    if i == 1:
                        last.then_inc(c_ready, 1)

        def feed_1(bank, w, j):
            terms = [(kt, hw, hx) for kt in range(KD) for hw, hx in PASSES]
            for z, (kt, hw, hx) in enumerate(terms):
                last = mm(bank[:, :], w[:, hw, kt, P * j:P * j + P], c_xt[:, kt, hx, :], start=z == 0, stop=z == len(terms) - 1)
            return last

        def feed_2(bank, w, bb, i, split=None):
            terms = [(kt, hw, hx) for kt in range(KF) for hw, hx in PASSES]
            for z, (kt, hw, hx) in enumerate(terms):
                if split and z % len(PASSES) == 0:
                    pe.wait_ge(split[0], split[1] + (kt + 1))
                last = mm(bank[:, D * i:D * i + D], hid[:, hx, kt, T * bb:T * bb + T], w[:, hw, kt, :],
                          start=z == 0, stop=z == len(terms) - 1)
            return last

        def bias_products_a(n, l):
            pe.wait_ge(s_lda, l * LOADS_A + LOADS_A)
            wait(pe, a_free, ua(n, False))
            for m in range(3):
                for j in range(KD):
                    for kt in range(KD):
                        col = 2 * m + j
                        last = mm(ps_a[:, col:col + 1], raw_a[:, m, kt, P * j:P * j + P], raw_v[:, 1, kt:kt + 1],
                                  start=kt == 0, stop=kt == KD - 1)
            last.then_inc(s_bias_pe, 1)

        def bias_products_c(n, l):
            pe.wait_ge(s_ldc, l * LOADS_C + LOADS_C)
            pe.wait_ge(a_free, ua(n, False) + len(A_TOWER) - 2)
            for kt in range(KD):
                mm(ps_a[:, 0:D], bv[:, kt:kt + 1].broadcast_to([P, P]), raw_p[:, kt, :], start=kt == 0, stop=kt == KD - 1)
            for j in range(KF):
                for kt in range(KD):
                    last = mm(ps_a[:, D + j:D + j + 1], raw_1[:, kt, P * j:P * j + P], raw_v[:, 3, kt:kt + 1],
                              start=kt == 0, stop=kt == KD - 1)
            last.then_inc(s_bias_pe, 1)

        pe.wait_ge(s_cst, 32)
        pe.wait_ge(s_init, 2)
        pe.wait_ge(s_zero, 2)
        walk(pe, step)

        def transpose_rows(j, par):
            for ch in range(CAP // P):
                last = nc.tensor.transpose(rows_ps[j][:, T * ch:T * ch + T], e_x[par][:, ch, P * j:P * j + P], ident)
            last.then_inc(c_ready, 1)

        pe.wait_ge(m_x[0], CAP // P * 16)
        pe.wait_ge(mx, INST * UNITS)
        for j in range(KD):
            transpose_rows(j, 0)
        pe.wait_ge(c_free, U_E + 2)
        pe.wait_ge(p_exp, INST * UNITS)

        def expert(e, par, k_, last):
            for j in range(KF):
                if j == 0:
                    pe.wait_ge(c_free, fe(e) - 2)
                    pe.wait_ge(m_l1, e + 1)
                pe.wait_ge(m_g, e * KF + max(j - 1, 0))
                feed_1(ps_c[j % 2], e_w1s[par], j).then_inc(c_ready, 1)
            if not last:
                pe.wait_ge(m_x[1 - par], (k_ + par) * 64 + 64)
                for j in range(KD):
                    transpose_rows(j, 1 - par)
            for j in range(2):
                pe.wait_ge(c_free, fe(e) - 1 + j)
                if j == 0:
                    pe.wait_ge(m_l2, e + 1)
                for i in range(2):
                    done = feed_2(out_ps[j], e_w2s[par], 2 * j + i, i, (m_lo, e * KF) if i == j == 0 else None)
                done.then_inc(c_ready, 1)

        experts(pe, expert)

        for b in range(MB):
            i, n0 = b * T // HOT, b * T % HOT
            if b >= 2:
                pe.wait_ge(m_fin, b - 1)
            elif b == 0:
                pe.wait_ge(m_g, E * KF)
            for ch in range(NCH):
                if n0 == 0:
                    pe.wait_ge(m_hot, i * NCH + ch + 1)
                if b == 0 and ch % (CAP // P) == 0:
                    pe.wait_ge(m_w, ch + CAP // P)
                for hl in range(2):
                    last = mm(ps_c[b % 2][:, 0:D], hot(i, ch)[:, n0:n0 + T], wout[:, ch, hl, :],
                              start=ch + hl == 0, stop=ch + hl == NCH)
            last.then_inc(c_ready, 1)

    @block.vector
    def _(dve):
        V = nc.vector
        ln_a = (a_st, a_mv, a_rs, a_x, a_stat, a_mvs, a_rstd, a_xn)
        ln_c = (c_st, c_mv, c_rs, c_x, c_stat, c_mvs, c_rstd, c_xn)

        def stats(ln, n, g, seqs=range(GB)):
            st, mv, rs, xn, s_st, s_mv, s_rs, s_xn = ln
            dve.nop(nofuse=True)
            for i in seqs:
                V.bn_stats(st[:, i, :], x[:, bass.ds(g * GB + i, 1), :].rearrange("p a d -> p (a d)")).then_inc(s_st, 1)
            for i in seqs:
                dve.wait_ge(s_st, n * GB + i + 1)
                dve.nop(nofuse=True)
                V.bn_aggr(mv[:, i, :], st[:, i, :]).then_inc(s_mv, 1)

        def normalise(ln, n, g, dst=None):
            st, mv, rs, xn, s_st, s_mv, s_rs, s_xn = ln
            dve.wait_ge(s_rs, n + 1)
            for i in range(GB):
                V.tensor_scalar((dst or xn)[:, i, :], x[:, bass.ds(g * GB + i, 1), :].rearrange("p a d -> p (a d)"),
                                mv[:, i, 0:1], rs[:, i:i + 1], ALU.subtract, ALU.mult).then_inc(s_xn, 1)

        def split_lo(dst, raw, scale, hi):
            return V.scalar_tensor_tensor(out=dst, in0=raw, scalar=scale, in1=hi, op0=ALU.mult, op1=ALU.subtract)

        def prep_a(n, l):
            dve.wait_ge(s_lda, l * LOADS_A + LOADS_A)
            wait(dve, a_ready, ua(n, False))
            V.tensor_scalar(lnw16[:], raw_v[:, 0:4:2, :], WS, None, ALU.mult).then_inc(s_ln16, 1)
            dve.wait_ge(s_ln16, l + 1)
            for kt in range(KD):
                V.tensor_scalar(wa[:, :, 0, kt, :], raw_a[:, :, kt, :], lnw16[:, 0, kt:kt + 1], None, ALU.mult).then_inc(s_wh, 1)
            dve.wait_ge(s_bias_pe, l * 2 + 1)
            V.tensor_scalar(bqk[:], ps_a[:, 0:4], WS, None, ALU.mult).then_inc(s_bias_a, 1)
            V.tensor_copy(bv[:], ps_a[:, 4:6]).then_inc(s_bias_a, 1)
            for kt in range(KD):
                dve.wait_ge(s_wh, l * SPLITS + kt + 1)
                last = split_lo(wa[:, :, 1, kt, :], raw_a[:, :, kt, :], lnw16[:, 0, kt:kt + 1], wa[:, :, 0, kt, :])
            last.then_inc(s_wa, 1)

        def prep_p(c, l):
            dve.wait_ge(s_ldc, l * LOADS_C + LOADS_C)
            wait(dve, c_ready, uc(c, False) + 4)
            V.tensor_scalar(wp[:, 0], raw_p[:], WS, None, ALU.mult).then_inc(s_wh, 1)
            dve.wait_ge(s_wh, l * SPLITS + 3)
            split_lo(wp[:, 1], raw_p[:], WS, wp[:, 0]).then_inc(s_wp, 1)

        def prep_1(c, l):
            wait(dve, c_ready, uc(c, False) + 14)
            for kt in range(KD):
                V.tensor_scalar(w1s[:, 0, kt, :], raw_1[:, kt, :], lnw16[:, 1, kt:kt + 1], None, ALU.mult).then_inc(s_wh, 1)
            for kt in range(KD):
                dve.wait_ge(s_wh, l * SPLITS + 4 + kt)
                last = split_lo(w1s[:, 1, kt, :], raw_1[:, kt, :], lnw16[:, 1, kt:kt + 1], w1s[:, 0, kt, :])
            last.then_inc(s_w1, 1)

        def prep_b(c, l):
            dve.wait_ge(s_bias_pe, l * 2 + 2)
            wait(dve, s_row1, c * GB + GB)
            wait(dve, s_row2, c * GB + GB)
            wait(dve, c_hi, hc(c, False) + 12)
            wait(dve, c_free, uc(c, False) + 14)
            V.tensor_tensor(row1[:], ps_a[:, 0:D], raw_rows[:, 0, :], ALU.add).then_inc(s_bias_c, 1)
            V.tensor_copy(row2[:], raw_rows[:, 1, :]).then_inc(s_bias_c, 1)
            V.tensor_tensor(b1c[:], ps_a[:, D:D + KF], raw_b1[:], ALU.add).then_inc(s_b1, 1)
            dve.wait_ge(s_b1, l + 1)
            V.tensor_scalar(b1c[:], b1c[:], WS, None, ALU.mult).then_inc(s_bias_c, 1)

        def prep_2(c, l):
            dve.wait_ge(s_w2h, l + 1)
            split_lo(w2s[:, 1], raw_2, WS, w2s[:, 0]).then_inc(s_w2, 1)

        def split_lows(e, par, raw2=None):
            dve.wait_ge(m_h1, e + 1)
            split_lo(e_w1s[par][:, 1], raw_1, WS, e_w1s[par][:, 0]).then_inc(m_l1, 1)
            dve.wait_ge(m_h2, e + 1)
            split_lo(e_w2s[par][:, 1], e_raw2 if raw2 is None else raw2, WS, e_w2s[par][:, 0]).then_inc(m_l2, 1)

        def prep_r():
            dve.wait_ge(s_fw, 64)
            for m in range(2):
                src = fw[:, m].rearrange("p k (n two) -> p k n two", two=2)
                dst = fw[:, 4 + m].rearrange("p k (n two) -> p k n two", two=2)
                V.tensor_scalar(dst[:, :, :, 0], src[:, :, :, 1], -1.0, None, ALU.mult).then_inc(s_fws, 1)
                V.tensor_copy(dst[:, :, :, 1], src[:, :, :, 0]).then_inc(s_fws, 1)

        def step(n, par, ga, gc, la, lc, A, B, C, prep):
            b, c = n - 1, n - 2
            UA, UC = ua(n, A == "r"), uc(c, C != "t")

            def maxima(i, u):
                dve.wait_ge(s_ready, i * UNITS + u + 1)
                V.tensor_reduce(negm[:, u % 4, :], ps_s[u % 2][:], AX_X, ALU.max, negate=True).then_inc(mx, 1)

            def contexts(i, q):
                dve.wait_ge(pv, i * UNITS + 2 * q + 2)
                V.reciprocal(rec[:], o_ps[:, :, 2 * HD]).then_inc(o_rec, 1)
                dve.wait_ge(o_rec, i * 8 + q + 1)
                wait(dve, o_ctx, i * 8 + q)
                V.tensor_tensor(o_hl[:].rearrange("p h a d -> p h (a d)"), o_ps[:, :, 0:2 * HD],
                                rec[:, :].unsqueeze(2).broadcast_to([P, 8, 2 * HD]), ALU.mult).then_inc(o_free, 1)

            def rotary_lo(kind, j):
                w = int(kind == "ks")
                r = (n - TOWER) * 4 + 2 * w + j
                dve.wait_ge(r_hi, r + 1)
                V.tensor_tensor(qk_hl[:, w, j, 1, :], rot, qk_hl[:, w, j, 0, :], ALU.subtract).then_inc(r_lo, 1)

            for s in range(SLOTS):
                for k, kind, j in a_uses(A, s - 1) if s else ():
                    if kind in ("qs", "ks"):
                        rotary_lo(kind, j)
                for k, kind, j in v_uses(B, s):
                    dve.wait_ge(a_hi, ha(b, B == "r") + (k + 1 if B == "t" else k - 7))
                    src = ps_a[:, :].rearrange("p (h d) -> p h d", d=HD)
                    v = vs[:, 1 - par, 2 * j:2 * j + 2, :, :].rearrange("p b h v -> p (b h) v")
                    V.scalar_tensor_tensor(out=v[:, :, HD:2 * HD], in0=src, scalar=1.0 if B == "t" else WS,
                                           in1=v[:, :, 0:HD], op0=ALU.mult, op1=ALU.subtract).then_inc(a_free, 1)
                for k, kind, j in a_uses(A, s):
                    if kind == "t" or A == "t":
                        dve.wait_ge(a_hi, ha(n, A == "r") + k + 1)
                    if kind == "t":
                        V.tensor_tensor(a_xt[:, j, 1, :], ps_a[:, :], a_xt[:, j, 0, :], ALU.subtract).then_inc(a_free, 1)
                    elif A == "t":
                        w = int(kind == "k")
                        V.scalar_tensor_tensor(out=qk_hl[:, w, j, 1, :], in0=ps_a[:, :], scalar=bqk[:, 2 * w + j:2 * w + j + 1],
                                               in1=qk_hl[:, w, j, 0, :], op0=ALU.add, op1=ALU.subtract).then_inc(a_free, 1)
                    else:
                        r = (n - TOWER) * 4 + 2 * (kind[0] == "k") + j
                        dve.wait_ge(a_ready, UA + k + 1)
                        wait(dve, r_sum, r)
                        table = sin16 if kind[1:] else cos16
                        V.tensor_tensor((rot_b if kind[1:] else rot_a).rearrange("p (b t) -> p b t", t=T),
                                        ps_a[:, :].rearrange("p (b t) -> p b t", t=T),
                                        table.unsqueeze(1).broadcast_to([P, GB, T]), ALU.mult).then_inc(a_free, 1)
                        if kind[1:]:
                            dve.wait_ge(a_free, UA + k + 1)
                            wait(dve, r_lo, r)
                            V.tensor_tensor(rot, rot_a, rot_b, ALU.add).then_inc(r_sum, 1)
                if s < SLOTS - AHEAD:
                    if B:
                        maxima(b, s + AHEAD)
                else:
                    for u in first_units(A, s):
                        maxima(n, u)
                if s == LAST_CONTEXTS and C:
                    contexts(c, 7)
                if s == 0 and A:
                    if isinstance(n, int) and n < 2:
                        position(n)
                    stats(ln_a, n, ga)
                if s > LAG and (s - LAG) % 2 and B:
                    contexts(b, (s - LAG) // 2)
                if s == 1 and A:
                    wait(dve, a_ready, UA - 2)
                    normalise(ln_a, n, ga)
                if s == PREP_A_SLOT and prep == "a":
                    prep_a(n, la)
                if s == 1 and prep == "r":
                    prep_r()
                if isinstance(n, int) and n == 1 and 3 <= s < 1 + NG:
                    position(s - 1)
                for k, kind, j in c_uses(C, s):
                    if kind == "f2":
                        continue
                    bank = ps_c[k % 2]
                    if kind == "pj":
                        dve.wait_ge(c_ready, UC + k + 1)
                        if C == "t":
                            dve.wait_ge(s_row1, c * GB + 2 * j + 2)
                        residual(bank, gc, j, WS * WS if C == "t" else WS)
                        continue
                    order = k + 1 if k < 2 else k - 1
                    dve.wait_ge(c_hi, hc(c, C != "t") + order)
                    if kind == "ct":
                        V.tensor_tensor(cxt[:, j, 1, :], bank[:, :], cxt[:, j, 0, :], ALU.subtract).then_inc(c_free, 1)
                    elif kind == "t":
                        V.tensor_tensor(c_xt[:, j, 1, :], bank[:, :], c_xt[:, j, 0, :], ALU.subtract).then_inc(c_free, 1)
                    else:
                        wait(dve, c_lo, c * KF + max(j - 1, 0))
                        V.tensor_scalar(act32[:, j % 2, :], bank[:, :], b1c[:, j:j + 1], 0.0, ALU.add, ALU.max).then_inc(c_free, 1)
                for k, kind, j in c_uses(C, s):
                    if kind == "f1":
                        dve.wait_ge(c_free, UC + k + 1)
                        V.tensor_tensor(hid[:, 1, j, :], act32[:, j % 2, :], hid[:, 0, j, :], ALU.subtract).then_inc(c_lo, 1)
                if C in ("t", "e") and s in (LN_C_SLOT - 1, LN_C_SLOT):
                    j = s - (LN_C_SLOT - 1)
                    dve.wait_ge(c_free, UC + 3 + j)
                    stats(ln_c, c, gc, range(2 * j, 2 * j + 2))
                if C in ("t", "e") and s == LN_C_SLOT + 1:
                    if C == "e":
                        dve.wait_ge(m_out, (c - TOWER) * 16)
                    normalise(ln_c, c, gc)
                if prep == "x" and s == X_SLOT + 1:
                    split_lows(0, 0, e_raw2_0)
                if C == "t" and s in (13, 15):
                    j = (s - 13) // 2
                    dve.wait_ge(c_ready, UC + 14 + j + 1)
                    dve.wait_ge(s_row2, c * GB + 2 * j + 2)
                    residual(ps_c[j], gc, j, WS * WS)
                if prep == "c" and s == 8:
                    prep_p(c, la)
                if prep == "c" and s == PREP_C_SLOT + 1:
                    prep_1(c, la)
                if prep == "c" and s == PREP_C_SLOT + 2:
                    prep_b(c, la)
            if prep == "c":
                prep_2(c, la)

        def residual(bank, g, j, scale):
            dst = x[:, bass.ds(g * GB + 2 * j, 2), :]
            V.scalar_tensor_tensor(out=dst, in0=bank[:, :].rearrange("p (b d) -> p b d", b=2), scalar=1.0 / scale, in1=dst,
                                   op0=ALU.mult, op1=ALU.add).then_inc(c_free, 1)

        def position(g):
            dve.wait_ge(s_emb[g], GB * 16)
            V.tensor_tensor(group(g), group(g), pos[:, :].unsqueeze(1).broadcast_to([P, GB, D]), ALU.add).then_inc(s_pos, 1)
            dve.wait_ge(s_pos, g + 1)

        V.memset(ks[:], 0.0).then_inc(s_zero, 1)
        V.memset(vs[:], 1.0).then_inc(s_zero, 1)
        dve.wait_ge(s_zero, 2)
        dve.wait_ge(s_cst, 32)
        V.tensor_copy(ident16[:], cst[:, 0, :]).then_inc(s_init, 1)
        V.tensor_copy(mask_ts[:], cst[:, 1, :]).then_inc(s_init, 1)

        walk(dve, step)

        def token_lo(count, j):
            dve.wait_ge(c_hi, count)
            V.tensor_tensor(c_xt[:, j, 1, :], rows_ps[j], c_xt[:, j, 0, :], ALU.subtract).then_inc(c_free, 1)

        for j in range(KD):
            token_lo(H_E + j + 1, j)
        dve.wait_ge(m_idx, 16)
        V.tensor_copy(e_idxf[:], e_idx[:].rearrange("p e c -> p (e c)")).then_inc(m_idxf, 1)
        for i in range(MB * T // HOT):
            V.tensor_scalar(num16[:, i, :], cst[:, 4:6, :].rearrange("p a n -> p (a n)"), float(i * HOT), None, ALU.add).then_inc(s_num, 1)
        dve.wait_ge(m_cw, NCH * 16)
        dve.wait_ge(m_l2, 1)

        def one_hot(i):
            for ch in range(NCH):
                V.tensor_scalar(hot(i, ch), num16[:, i, :], e_idxf[:, ch:ch + 1], None, ALU.is_equal).then_inc(m_hot, 1)

        def expert(e, par, k_, last):
            for j in range(KF):
                dve.wait_ge(c_hi, he(e) + j + 1)
                V.tensor_tensor(hid[:, 1, j, :], act32[:, j % 2, :], hid[:, 0, j, :], ALU.subtract).then_inc(m_lo, 1)
            if not last:
                for j in range(KD):
                    token_lo(he(e) + KF + j + 1, j)
                split_lows(e + 1, 1 - par)
            else:
                dve.wait_ge(m_idxf, 1)
                dve.wait_ge(s_num, MB * T // HOT)
                one_hot(0)
            dve.wait_ge(m_w, e * 4)
            for j in range(2):
                use = ue(e) + KF + j + (1 if last else 3)
                free = fe(e) + j + (1 if last else 3)
                dve.wait_ge(c_ready, use)
                if j == 0:
                    dve.wait_ge(m_row[par], k_ * 16 + 16)
                for i in range(2):
                    done = V.scalar_tensor_tensor(out=e_tmp[:, 2 * j + i, :], in0=out_ps[j][:, D * i:D * i + D], scalar=1.0 / WS,
                                                  in1=e_row[par][:], op0=ALU.mult, op1=ALU.add)
                    done.then_inc(m_o if i == 0 else c_free, 1)
                for i in range(2):
                    if i == 0:
                        dve.wait_ge(m_o, e * 2 + j + 1)
                    else:
                        dve.wait_ge(c_free, free)
                    ch = e * 4 + (2 * j + i)
                    w = e_cw[:, bass.ds(ch, 1), bass.ds(e, 1)].rearrange("p a b -> p (a b)")
                    dst = wout[:, bass.ds(ch, 1), :, :].rearrange("p c h n -> p (c h) n")
                    V.tensor_scalar(dst[:, 0, :], e_tmp[:, 2 * j + i, :], w, None, ALU.mult).then_inc(m_wh, 1)
                    dve.wait_ge(m_wh, e * 4 + 2 * j + i + 1)
                    split_lo(dst[:, 1, :], e_tmp[:, 2 * j + i, :], w, dst[:, 0, :]).then_inc(m_w, 1)

        experts(dve, expert)

        for i in range(MB * T // HOT):
            if i + 1 < MB * T // HOT:
                if i == 0:
                    dve.wait_ge(c_ready, U_END)
                else:
                    dve.wait_ge(c_ready, U_END + i * (HOT // T))
                one_hot(i + 1)
            for b in range(i * (HOT // T), (i + 1) * (HOT // T)):
                dve.wait_ge(c_ready, U_END + b + 1)
                V.tensor_tensor(x[:, b, :], ps_c[b % 2][:, 0:D], x[:, b, :], ALU.add).then_inc(m_fin, 1)

    ctx.close()


_INS = ['x', 'L0_tok_tok_emb', 'L0_tok_pos_emb', 'L0_tok_wq', 'L0_tok_wk', 'L0_tok_wv', 'L0_tok_w_proj', 'L0_tok_b_proj',
        'L0_tok_ln1_w', 'L0_tok_ln1_b', 'L0_tok_ln2_w', 'L0_tok_ln2_b', 'L0_tok_w1', 'L0_tok_b1', 'L0_tok_w2', 'L0_tok_b2',
        'L0_attn_qw', 'L0_attn_kw', 'L0_attn_vw', 'L0_attn_ow', 'L0_ffn_combine_weights', 'L0_ffn_top_idx',
        'L0_ffn_W1', 'L0_ffn_b1', 'L0_ffn_W2', 'L0_ffn_b2']


def _constants():
    import numpy as np

    c = np.zeros((6, P, P), np.float32)
    i = np.arange(P)
    c[0] = np.eye(P)
    c[1] = np.where(i[None, :] > i[:, None], np.float32(-2.0 ** 80), 0)
    inv = (np.float32(1.0) / np.float32(10000.0) ** (np.arange(0, HD, 2, dtype=np.float32) / np.float32(HD))).astype(np.float32)
    freq = (i.astype(np.float32)[:, None] * inv[None, :]).astype(np.float32)
    by_row = freq[:, (i % HD) // 2].T
    c[2] = np.cos(by_row) * np.float32(WS)
    c[3] = np.sin(by_row) * np.float32(WS)
    c[4], c[5] = i[None, :], i[None, :] + P
    return c


def kernel(**inputs):
    import numpy as _np
    import concourse.bacc as _bacc
    from concourse import mybir as _mybir
    from concourse.bass_utils import run_bass_kernel_spmd as _run

    nc = _bacc.Bacc("TRN2", target_bir_lowering=False, num_devices=1)
    arrays, args = {}, []
    for name in _INS + ["consts"]:
        a = _constants() if name == "consts" else _np.ascontiguousarray(inputs[name])
        arrays[f"in_{name}_dram"] = a
        args.append(nc.dram_tensor(f"in_{name}_dram", a.shape, _mybir.dt.from_np(a.dtype), kind="ExternalInput").ap())
    args.append(nc.dram_tensor("out_0_dram", (NB, T, D), _mybir.dt.from_np(_np.dtype("float32")), kind="ExternalOutput").ap())
    tower_model_kernel(nc, *args)
    r = _run(nc, [arrays], core_ids=[0])
    return r.results[0]["out_0_dram"]
```
